# Optimizing a Trainium2 kernel written in Bass

```python
import numpy as np
import jax
import jax.numpy as jnp

def _softmax(x, axis=-1):
    return jax.nn.softmax(x, axis=axis)

def _gelu(x):
    return jax.nn.gelu(x, approximate=True)

def _silu(x):
    return jax.nn.silu(x)

def _sigmoid(x):
    return jax.nn.sigmoid(x)

def _layernorm(x, axis=-1, eps=1e-05):
    m = jnp.mean(x, axis=axis, keepdims=True)
    v = jnp.var(x, axis=axis, keepdims=True)
    return (x - m) / jnp.sqrt(v + eps)

def _scatter_add(tgt, idx, src, axis=0):
    return tgt.at[idx].add(src)

def _segment_sum(src, seg, n):
    return jax.ops.segment_sum(src, seg, n)
kernel_name = 'mk_macaron_d2_jaxref_r8_c1254a'

def setup_inputs(seed: int=0):
    np.random.seed(seed)
    _w = jnp.asarray

    def _L0_attn_setup():
        import jax, jax.numpy as jnp
        import numpy as np
        B, T, C = (8, 512, 128)

        def _wkv(w_decay, u_first, k, v):
            w = -jnp.exp(w_decay)
            u = u_first
            kt = jnp.transpose(k, (1, 0, 2))
            vt = jnp.transpose(v, (1, 0, 2))
            a0 = jnp.zeros((k.shape[0], k.shape[2]), dtype=k.dtype)
            b0 = jnp.zeros_like(a0)
            p0 = jnp.full_like(a0, -1e+38)

            def step(carry, kv):
                a, b, p = carry
                k_t, v_t = kv
                q = jnp.maximum(p, u + k_t)
                e1 = jnp.exp(p - q)
                e2 = jnp.exp(u + k_t - q)
                y = (e1 * a + e2 * v_t) / (e1 * b + e2)
                q2 = jnp.maximum(p + w, k_t)
                f1 = jnp.exp(p + w - q2)
                f2 = jnp.exp(k_t - q2)
                return ((f1 * a + f2 * v_t, f1 * b + f2, q2), y)
            _, y = jax.lax.scan(step, (a0, b0, p0), (kt, vt))
            return jnp.transpose(y, (1, 0, 2))
        key = jax.random.key(seed)
        ks = jax.random.split(key, 5)
        scales = (jnp.arange(C, dtype=jnp.float32) / C).reshape(1, 1, C)
        return {'x': jax.random.normal(ks[0], (B, T, C), dtype=jnp.float32), 'time_decay': scales, 'time_first': scales, 'time_mix_k': scales, 'time_mix_v': scales, 'time_mix_r': scales, 'Wk': jax.random.normal(ks[1], (C, C), dtype=jnp.float32) / np.sqrt(C), 'Wv': jax.random.normal(ks[2], (C, C), dtype=jnp.float32) / np.sqrt(C), 'Wr': jax.random.normal(ks[3], (C, C), dtype=jnp.float32) / np.sqrt(C), 'Wo': jax.random.normal(ks[4], (C, C), dtype=jnp.float32) / np.sqrt(C)}
    _L0_attn_in = _L0_attn_setup()

    def _L0_ffn_setup():
        import jax, jax.numpy as jnp
        import numpy as np
        DIM = 128
        HIDDEN = 384
        SCALE = 1.0 / 127.0

        def _dequant(w_int, dtype):
            return w_int.astype(dtype) * jnp.asarray(SCALE, dtype)
        key = jax.random.key(seed)
        k_x, k_g, k_u, k_d = jax.random.split(key, 4)
        x = jax.random.normal(k_x, (4, 256, DIM), dtype=jnp.float32)
        w_gate = jax.random.randint(k_g, (HIDDEN, DIM), -127, 128, dtype=jnp.int32)
        w_up = jax.random.randint(k_u, (HIDDEN, DIM), -127, 128, dtype=jnp.int32)
        w_down = jax.random.randint(k_d, (DIM, HIDDEN), -127, 128, dtype=jnp.int32)
        return {'x': x, 'w_gate': w_gate, 'w_up': w_up, 'w_down': w_down}
    _L0_ffn_in = _L0_ffn_setup()

    def _L1_attn_setup():
        import jax, jax.numpy as jnp
        import numpy as np
        from jax import lax
        N_HEADS = 16
        EPS = 1e-06
        CHUNK = 128

        def causal_dot_product(q, k, v):
            B, H, L, D = q.shape
            M = v.shape[-1]
            nc = L // CHUNK
            qc = q.reshape(B, H, nc, CHUNK, D).transpose(2, 0, 1, 3, 4)
            kc = k.reshape(B, H, nc, CHUNK, D).transpose(2, 0, 1, 3, 4)
            vc = v.reshape(B, H, nc, CHUNK, M).transpose(2, 0, 1, 3, 4)

            def step(kv_carry, inp):
                qb, kb, vb = inp
                kv = jnp.einsum('bhcd,bhcm->bhcdm', kb, vb)
                kv_cum = jnp.cumsum(kv, axis=2) + kv_carry[:, :, None]
                out = jnp.einsum('bhcd,bhcdm->bhcm', qb, kv_cum)
                return (kv_cum[:, :, -1], out)
            init = jnp.zeros((B, H, D, M), q.dtype)
            _, outs = lax.scan(step, init, (qc, kc, vc))
            return outs.transpose(1, 2, 0, 3, 4).reshape(B, H, L, M)

        def flow_attention_causal(x, Wq, bq, Wk, bk, Wv, bv, Wo, bo):
            B, L, _ = x.shape
            d_model = Wq.shape[1]
            H = N_HEADS
            q = (x @ Wq + bq).reshape(B, L, H, -1).transpose(0, 2, 1, 3)
            k = (x @ Wk + bk).reshape(B, L, H, -1).transpose(0, 2, 1, 3)
            v = (x @ Wv + bv).reshape(B, L, H, -1).transpose(0, 2, 1, 3)
            q = jax.nn.sigmoid(q)
            k = jax.nn.sigmoid(k)
            sink_incoming = 1.0 / jnp.einsum('bhld,bhld->bhl', q + EPS, jnp.cumsum(k, axis=2) + EPS)
            source_outgoing = 1.0 / jnp.einsum('bhld,bhld->bhl', k + EPS, jnp.cumsum(q, axis=2) + EPS)
            normal = (jnp.arange(L, dtype=x.dtype) + 1.0)[None, None, :]
            sink_incoming = sink_incoming * normal
            source_outgoing = source_outgoing * normal
            conserved_sink = jnp.einsum('bhld,bhld->bhl', q + EPS, jnp.cumsum(k * source_outgoing[..., None], axis=2) + EPS) / normal
            conserved_source = jnp.einsum('bhld,bhld->bhl', k + EPS, jnp.cumsum(q * sink_incoming[..., None], axis=2) + EPS) / normal
            sink_allocation = jax.nn.sigmoid(conserved_sink)
            cs = jnp.exp(conserved_source)
            source_competition = cs / jnp.cumsum(cs, axis=-1) * normal
            out = causal_dot_product(q * (sink_incoming / normal)[..., None], k, v * source_competition[..., None]) * sink_allocation[..., None]
            out = out.transpose(0, 2, 1, 3).reshape(B, L, d_model)
            return out @ Wo + bo
        key = jax.random.key(seed)
        ks = jax.random.split(key, 9)
        B, L, d_model = (4, 512, 128)
        s = 0.02
        return {'x': jax.random.normal(ks[0], (B, L, d_model), dtype=jnp.float32), 'Wq': jax.random.normal(ks[1], (d_model, d_model), dtype=jnp.float32) * s, 'bq': jnp.zeros((d_model,), dtype=jnp.float32), 'Wk': jax.random.normal(ks[2], (d_model, d_model), dtype=jnp.float32) * s, 'bk': jnp.zeros((d_model,), dtype=jnp.float32), 'Wv': jax.random.normal(ks[3], (d_model, d_model), dtype=jnp.float32) * s, 'bv': jnp.zeros((d_model,), dtype=jnp.float32), 'Wo': jax.random.normal(ks[4], (d_model, d_model), dtype=jnp.float32) * s, 'bo': jnp.zeros((d_model,), dtype=jnp.float32)}
    _L1_attn_in = _L1_attn_setup()

    def _L1_ffn_setup():
        import jax, jax.numpy as jnp
        import numpy as np
        from jax.scipy.linalg import expm
        B, S, D, E, K, NROT = (2, 256, 128, 8, 2, 3)
        EPS = 1e-05

        def _gelu(x):
            return jax.nn.gelu(x, approximate=False)

        def _forward(x, ln_gamma, ln_beta, abel_w, abel_b, moe_gate_w, moe_gate_b, ew1, eb1, ew2, eb2, gens, gc_w, gc_b):
            residual = x
            mu = jnp.mean(x, axis=-1, keepdims=True)
            var = jnp.mean((x - mu) ** 2, axis=-1, keepdims=True)
            xn = (x - mu) * jax.lax.rsqrt(var + EPS) * ln_gamma + ln_beta
            abel_out = _gelu(xn @ abel_w + abel_b)
            logits = xn @ moe_gate_w + moe_gate_b
            topw, topi = jax.lax.top_k(logits, K)
            topw = jax.nn.softmax(topw, axis=-1)
            w_dense = jnp.sum(jax.nn.one_hot(topi, E, dtype=xn.dtype) * topw[..., None], axis=-2)
            h = _gelu(jnp.einsum('bsd,edh->ebsh', xn, ew1) + eb1[:, None, None, :])
            eo = jnp.einsum('ebsh,ehd->ebsd', h, ew2) + eb2[:, None, None, :]
            moe_out = jnp.einsum('ebsd,bse->bsd', eo, w_dense)
            for i in range(NROT):
                moe_out = moe_out @ expm(gens[i])
            combined = jnp.concatenate([abel_out, moe_out], axis=-1)
            gate = jax.nn.sigmoid(combined @ gc_w + gc_b)
            mixed = abel_out * (1.0 - gate) + moe_out * gate
            return residual + mixed
        key = jax.random.key(seed)
        ks = jax.random.split(key, 16)
        sc = 0.02
        x = jax.random.normal(ks[0], (B, S, D), jnp.float32)
        ln_gamma = 1.0 + sc * jax.random.normal(ks[1], (D,), jnp.float32)
        ln_beta = sc * jax.random.normal(ks[2], (D,), jnp.float32)
        abel_w = sc * jax.random.normal(ks[3], (D, D), jnp.float32)
        abel_b = sc * jax.random.normal(ks[4], (D,), jnp.float32)
        moe_gate_w = sc * jax.random.normal(ks[5], (D, E), jnp.float32)
        moe_gate_b = sc * jax.random.normal(ks[6], (E,), jnp.float32)
        ew1 = sc * jax.random.normal(ks[7], (E, D, 2 * D), jnp.float32)
        eb1 = sc * jax.random.normal(ks[8], (E, 2 * D), jnp.float32)
        ew2 = sc * jax.random.normal(ks[9], (E, 2 * D, D), jnp.float32)
        eb2 = sc * jax.random.normal(ks[10], (E, D), jnp.float32)
        g = sc * jax.random.normal(ks[11], (NROT, D, D), jnp.float32)
        gens = 0.5 * (g - jnp.swapaxes(g, -1, -2))
        gc_w = sc * jax.random.normal(ks[12], (2 * D, 1), jnp.float32)
        gc_b = sc * jax.random.normal(ks[13], (1,), jnp.float32)
        return dict(x=x, ln_gamma=ln_gamma, ln_beta=ln_beta, abel_w=abel_w, abel_b=abel_b, moe_gate_w=moe_gate_w, moe_gate_b=moe_gate_b, ew1=ew1, eb1=eb1, ew2=ew2, eb2=eb2, gens=gens, gc_w=gc_w, gc_b=gc_b)
    _L1_ffn_in = _L1_ffn_setup()
    _d = {'L0_attn_x': _L0_attn_in['x'], 'L0_attn_time_decay': _L0_attn_in['time_decay'], 'L0_attn_time_first': _L0_attn_in['time_first'], 'L0_attn_time_mix_k': _L0_attn_in['time_mix_k'], 'L0_attn_time_mix_v': _L0_attn_in['time_mix_v'], 'L0_attn_time_mix_r': _L0_attn_in['time_mix_r'], 'L0_attn_Wk': _L0_attn_in['Wk'], 'L0_attn_Wv': _L0_attn_in['Wv'], 'L0_attn_Wr': _L0_attn_in['Wr'], 'L0_attn_Wo': _L0_attn_in['Wo'], 'L0_ffn_w_gate': _L0_ffn_in['w_gate'], 'L0_ffn_w_up': _L0_ffn_in['w_up'], 'L0_ffn_w_down': _L0_ffn_in['w_down'], 'L1_attn_Wq': _L1_attn_in['Wq'], 'L1_attn_bq': _L1_attn_in['bq'], 'L1_attn_Wk': _L1_attn_in['Wk'], 'L1_attn_bk': _L1_attn_in['bk'], 'L1_attn_Wv': _L1_attn_in['Wv'], 'L1_attn_bv': _L1_attn_in['bv'], 'L1_attn_Wo': _L1_attn_in['Wo'], 'L1_attn_bo': _L1_attn_in['bo'], 'L1_ffn_ln_gamma': _L1_ffn_in['ln_gamma'], 'L1_ffn_ln_beta': _L1_ffn_in['ln_beta'], 'L1_ffn_abel_w': _L1_ffn_in['abel_w'], 'L1_ffn_abel_b': _L1_ffn_in['abel_b'], 'L1_ffn_moe_gate_w': _L1_ffn_in['moe_gate_w'], 'L1_ffn_moe_gate_b': _L1_ffn_in['moe_gate_b'], 'L1_ffn_ew1': _L1_ffn_in['ew1'], 'L1_ffn_eb1': _L1_ffn_in['eb1'], 'L1_ffn_ew2': _L1_ffn_in['ew2'], 'L1_ffn_eb2': _L1_ffn_in['eb2'], 'L1_ffn_gens': _L1_ffn_in['gens'], 'L1_ffn_gc_w': _L1_ffn_in['gc_w'], 'L1_ffn_gc_b': _L1_ffn_in['gc_b']}
    _x0 = _d['L0_attn_x']
    _d['L0_attn_x'] = jax.random.normal(jax.random.fold_in(jax.random.key(seed), 1), (4, 1024, 128), dtype=_x0.dtype)
    del _x0
    return _d

def reference(L0_attn_x, L0_attn_time_decay, L0_attn_time_first, L0_attn_time_mix_k, L0_attn_time_mix_v, L0_attn_time_mix_r, L0_attn_Wk, L0_attn_Wv, L0_attn_Wr, L0_attn_Wo, L0_ffn_w_gate, L0_ffn_w_up, L0_ffn_w_down, L1_attn_Wq, L1_attn_bq, L1_attn_Wk, L1_attn_bk, L1_attn_Wv, L1_attn_bv, L1_attn_Wo, L1_attn_bo, L1_ffn_ln_gamma, L1_ffn_ln_beta, L1_ffn_abel_w, L1_ffn_abel_b, L1_ffn_moe_gate_w, L1_ffn_moe_gate_b, L1_ffn_ew1, L1_ffn_eb1, L1_ffn_ew2, L1_ffn_eb2, L1_ffn_gens, L1_ffn_gc_w, L1_ffn_gc_b):

    def _L0_attn_ref(x, time_decay, time_first, time_mix_k, time_mix_v, time_mix_r, Wk, Wv, Wr, Wo):
        import jax, jax.numpy as jnp
        import numpy as np
        B, T, C = (8, 512, 128)

        def _wkv(w_decay, u_first, k, v):
            w = -jnp.exp(w_decay)
            u = u_first
            kt = jnp.transpose(k, (1, 0, 2))
            vt = jnp.transpose(v, (1, 0, 2))
            a0 = jnp.zeros((k.shape[0], k.shape[2]), dtype=k.dtype)
            b0 = jnp.zeros_like(a0)
            p0 = jnp.full_like(a0, -1e+38)

            def step(carry, kv):
                a, b, p = carry
                k_t, v_t = kv
                q = jnp.maximum(p, u + k_t)
                e1 = jnp.exp(p - q)
                e2 = jnp.exp(u + k_t - q)
                y = (e1 * a + e2 * v_t) / (e1 * b + e2)
                q2 = jnp.maximum(p + w, k_t)
                f1 = jnp.exp(p + w - q2)
                f2 = jnp.exp(k_t - q2)
                return ((f1 * a + f2 * v_t, f1 * b + f2, q2), y)
            _, y = jax.lax.scan(step, (a0, b0, p0), (kt, vt))
            return jnp.transpose(y, (1, 0, 2))
        x_prev = jnp.pad(x, ((0, 0), (1, 0), (0, 0)))[:, :-1]
        xk = x_prev + time_mix_k * (x - x_prev)
        xv = x_prev + time_mix_v * (x - x_prev)
        xr = x_prev + time_mix_r * (x - x_prev)
        k = jnp.einsum('btc,dc->btd', xk, Wk)
        v = jnp.einsum('btc,dc->btd', xv, Wv)
        sr = jax.nn.sigmoid(jnp.einsum('btc,dc->btd', xr, Wr))
        wkv = _wkv(time_decay.reshape(-1), time_first.reshape(-1), k, v)
        return jnp.einsum('btc,dc->btd', sr * wkv, Wo)

    def _L0_ffn_ref(x, w_gate, w_up, w_down):
        import jax, jax.numpy as jnp
        import numpy as np
        DIM = 128
        HIDDEN = 384
        SCALE = 1.0 / 127.0

        def _dequant(w_int, dtype):
            return w_int.astype(dtype) * jnp.asarray(SCALE, dtype)
        wg = _dequant(w_gate, x.dtype)
        wu = _dequant(w_up, x.dtype)
        wd = _dequant(w_down, x.dtype)
        gate = jnp.einsum('bsd,hd->bsh', x, wg)
        up = jnp.einsum('bsd,hd->bsh', x, wu)
        h = jax.nn.silu(gate) * up
        return jnp.einsum('bsh,dh->bsd', h, wd)

    def _L1_attn_ref(x, Wq, bq, Wk, bk, Wv, bv, Wo, bo):
        import jax, jax.numpy as jnp
        import numpy as np
        from jax import lax
        N_HEADS = 16
        EPS = 1e-06
        CHUNK = 128

        def causal_dot_product(q, k, v):
            B, H, L, D = q.shape
            M = v.shape[-1]
            nc = L // CHUNK
            qc = q.reshape(B, H, nc, CHUNK, D).transpose(2, 0, 1, 3, 4)
            kc = k.reshape(B, H, nc, CHUNK, D).transpose(2, 0, 1, 3, 4)
            vc = v.reshape(B, H, nc, CHUNK, M).transpose(2, 0, 1, 3, 4)

            def step(kv_carry, inp):
                qb, kb, vb = inp
                kv = jnp.einsum('bhcd,bhcm->bhcdm', kb, vb)
                kv_cum = jnp.cumsum(kv, axis=2) + kv_carry[:, :, None]
                out = jnp.einsum('bhcd,bhcdm->bhcm', qb, kv_cum)
                return (kv_cum[:, :, -1], out)
            init = jnp.zeros((B, H, D, M), q.dtype)
            _, outs = lax.scan(step, init, (qc, kc, vc))
            return outs.transpose(1, 2, 0, 3, 4).reshape(B, H, L, M)

        def flow_attention_causal(x, Wq, bq, Wk, bk, Wv, bv, Wo, bo):
            B, L, _ = x.shape
            d_model = Wq.shape[1]
            H = N_HEADS
            q = (x @ Wq + bq).reshape(B, L, H, -1).transpose(0, 2, 1, 3)
            k = (x @ Wk + bk).reshape(B, L, H, -1).transpose(0, 2, 1, 3)
            v = (x @ Wv + bv).reshape(B, L, H, -1).transpose(0, 2, 1, 3)
            q = jax.nn.sigmoid(q)
            k = jax.nn.sigmoid(k)
            sink_incoming = 1.0 / jnp.einsum('bhld,bhld->bhl', q + EPS, jnp.cumsum(k, axis=2) + EPS)
            source_outgoing = 1.0 / jnp.einsum('bhld,bhld->bhl', k + EPS, jnp.cumsum(q, axis=2) + EPS)
            normal = (jnp.arange(L, dtype=x.dtype) + 1.0)[None, None, :]
            sink_incoming = sink_incoming * normal
            source_outgoing = source_outgoing * normal
            conserved_sink = jnp.einsum('bhld,bhld->bhl', q + EPS, jnp.cumsum(k * source_outgoing[..., None], axis=2) + EPS) / normal
            conserved_source = jnp.einsum('bhld,bhld->bhl', k + EPS, jnp.cumsum(q * sink_incoming[..., None], axis=2) + EPS) / normal
            sink_allocation = jax.nn.sigmoid(conserved_sink)
            cs = jnp.exp(conserved_source)
            source_competition = cs / jnp.cumsum(cs, axis=-1) * normal
            out = causal_dot_product(q * (sink_incoming / normal)[..., None], k, v * source_competition[..., None]) * sink_allocation[..., None]
            out = out.transpose(0, 2, 1, 3).reshape(B, L, d_model)
            return out @ Wo + bo
        return flow_attention_causal(x, Wq, bq, Wk, bk, Wv, bv, Wo, bo)

    def _L1_ffn_ref(x, ln_gamma, ln_beta, abel_w, abel_b, moe_gate_w, moe_gate_b, ew1, eb1, ew2, eb2, gens, gc_w, gc_b):
        import jax, jax.numpy as jnp
        import numpy as np
        from jax.scipy.linalg import expm
        B, S, D, E, K, NROT = (2, 256, 128, 8, 2, 3)
        EPS = 1e-05

        def _gelu(x):
            return jax.nn.gelu(x, approximate=False)

        def _forward(x, ln_gamma, ln_beta, abel_w, abel_b, moe_gate_w, moe_gate_b, ew1, eb1, ew2, eb2, gens, gc_w, gc_b):
            residual = x
            mu = jnp.mean(x, axis=-1, keepdims=True)
            var = jnp.mean((x - mu) ** 2, axis=-1, keepdims=True)
            xn = (x - mu) * jax.lax.rsqrt(var + EPS) * ln_gamma + ln_beta
            abel_out = _gelu(xn @ abel_w + abel_b)
            logits = xn @ moe_gate_w + moe_gate_b
            topw, topi = jax.lax.top_k(logits, K)
            topw = jax.nn.softmax(topw, axis=-1)
            w_dense = jnp.sum(jax.nn.one_hot(topi, E, dtype=xn.dtype) * topw[..., None], axis=-2)
            h = _gelu(jnp.einsum('bsd,edh->ebsh', xn, ew1) + eb1[:, None, None, :])
            eo = jnp.einsum('ebsh,ehd->ebsd', h, ew2) + eb2[:, None, None, :]
            moe_out = jnp.einsum('ebsd,bse->bsd', eo, w_dense)
            for i in range(NROT):
                moe_out = moe_out @ expm(gens[i])
            combined = jnp.concatenate([abel_out, moe_out], axis=-1)
            gate = jax.nn.sigmoid(combined @ gc_w + gc_b)
            mixed = abel_out * (1.0 - gate) + moe_out * gate
            return residual + mixed
        return _forward(x, ln_gamma, ln_beta, abel_w, abel_b, moe_gate_w, moe_gate_b, ew1, eb1, ew2, eb2, gens, gc_w, gc_b)
    x = L0_attn_x
    x = x + 0.5 * _L0_ffn_ref(_layernorm(x, axis=-1), L0_ffn_w_gate, L0_ffn_w_up, L0_ffn_w_down)
    x = x + _L0_attn_ref(_layernorm(x, axis=-1), L0_attn_time_decay, L0_attn_time_first, L0_attn_time_mix_k, L0_attn_time_mix_v, L0_attn_time_mix_r, L0_attn_Wk, L0_attn_Wv, L0_attn_Wr, L0_attn_Wo)
    x = x + 0.5 * _L0_ffn_ref(_layernorm(x, axis=-1), L0_ffn_w_gate, L0_ffn_w_up, L0_ffn_w_down)
    x = x + 0.5 * _L1_ffn_ref(_layernorm(x, axis=-1), L1_ffn_ln_gamma, L1_ffn_ln_beta, L1_ffn_abel_w, L1_ffn_abel_b, L1_ffn_moe_gate_w, L1_ffn_moe_gate_b, L1_ffn_ew1, L1_ffn_eb1, L1_ffn_ew2, L1_ffn_eb2, L1_ffn_gens, L1_ffn_gc_w, L1_ffn_gc_b)
    x = x + _L1_attn_ref(_layernorm(x, axis=-1), L1_attn_Wq, L1_attn_bq, L1_attn_Wk, L1_attn_bk, L1_attn_Wv, L1_attn_bv, L1_attn_Wo, L1_attn_bo)
    x = x + 0.5 * _L1_ffn_ref(_layernorm(x, axis=-1), L1_ffn_ln_gamma, L1_ffn_ln_beta, L1_ffn_abel_w, L1_ffn_abel_b, L1_ffn_moe_gate_w, L1_ffn_moe_gate_b, L1_ffn_ew1, L1_ffn_eb1, L1_ffn_ew2, L1_ffn_eb2, L1_ffn_gens, L1_ffn_gc_w, L1_ffn_gc_b)
    return x

_drawn_inputs = setup_inputs


def setup_inputs(seed=0):
    import zlib

    import numpy as np

    out = dict(_drawn_inputs(seed))
    spreads = {'L1_attn_bq': (0.0, 2.0),
     'L1_attn_bk': (0.0, 2.0),
     'L1_attn_bv': (0.0, 2.0),
     'L1_attn_bo': (0.0, 2.0)}
    factors = {'L0_attn_time_decay': 8.0,
     'L0_attn_time_first': 8.0,
     'L0_attn_time_mix_k': 8.0,
     'L0_attn_time_mix_v': 8.0,
     'L0_attn_time_mix_r': 8.0,
     'L0_attn_Wk': 8.0,
     'L0_attn_Wv': 8.0,
     'L0_attn_Wr': 8.0,
     'L0_attn_Wo': 8.0,
     'L1_attn_Wq': 64.0,
     'L1_attn_Wk': 64.0,
     'L1_attn_Wv': 64.0,
     'L1_attn_Wo': 64.0,
     'L1_ffn_ln_gamma': 64.0,
     'L1_ffn_ln_beta': 64.0,
     'L1_ffn_abel_w': 8.0,
     'L1_ffn_abel_b': 200.0,
     'L1_ffn_moe_gate_w': 8.0,
     'L1_ffn_moe_gate_b': 64.0,
     'L1_ffn_ew1': 8.0,
     'L1_ffn_eb1': 64.0,
     'L1_ffn_ew2': 8.0,
     'L1_ffn_eb2': 200.0,
     'L1_ffn_gens': 8.0,
     'L1_ffn_gc_w': 8.0}
    for name, (base, spread) in spreads.items():
        noise = np.random.default_rng([zlib.crc32(name.encode()), seed]).standard_normal(out[name].shape)
        drawn = base * np.exp(spread * noise) if base else spread * noise
        out[name] = jnp.asarray(drawn.astype(out[name].dtype))
    for name, factor in factors.items():
        out[name] = (out[name] * factor).astype(out[name].dtype)
    return out
```

```python
from contextlib import ExitStack

import concourse.bass as bass
from concourse import mybir

ALU = mybir.AluOpType
ACT = mybir.ActivationFunctionType
F32 = mybir.dt.float32
F16 = mybir.dt.float16
I32 = mybir.dt.int32
U32 = mybir.dt.uint32
AX = mybir.AxisListType
RMAX = bass.bass_isa.ReduceOp.max

P = 128
TILES = 4
CH = P * TILES
LN_EPS = 1e-5
FLOW_EPS = 1e-6
QSCALE = 1.0 / 127.0
WS = 64.0
TAYLOR = 10
SQUARINGS = 16
HEADS = 16
HD = P // HEADS
SKEW = 5
FAR = -1e38


def after(eng, sem, count):
    if isinstance(count, int) and count <= 0:
        return
    eng.wait_ge(sem, count)


class Buffers:
    pass


class Semaphores:
    pass


class Chain:

    def __init__(self, eng, sem, per_chunk=0):
        self.eng, self.sem, self.per_chunk = eng, sem, per_chunk
        self.base = self.n = 0

    def at(self, chunk):
        self.base, self.n = self.per_chunk * chunk, 0

    def link(self, instruction, wait=None):
        instruction.then_inc(self.sem, 1)
        self.n += 1
        if wait:
            wait(self.eng, self.sem, self.base + self.n)
        else:
            self.eng.wait_ge(self.sem, self.base + self.n)

    def close(self):
        assert self.n == self.per_chunk, (self.n, self.per_chunk)


def pipeline(eng, first, chunks, step):
    step(first - 1, 1, True, False, False)
    step(first, 0, True, True, False)
    with eng.Fori(0, (chunks - 2) // 2) as m:
        step(2 * m + (first + 1), 1, True, True, True)
        step(2 * m + (first + 2), 0, True, True, True)
    step(first + chunks - 1, 1, False, True, True)
    step(first + chunks, 0, False, False, True)


class Arena:

    def __init__(self, whole):
        self.whole, self.used = whole, 0

    def take(self, dims, dt=F32, parts=P):
        n = 1
        for d in dims:
            n *= d
        words = n if dt != F16 else n // 2
        view = self.whole[0:parts, self.used:self.used + words]
        self.used += words
        assert self.used <= self.whole.shape[1], self.used
        if dt != F32:
            view = view.bitcast(dt)
        if len(dims) == 2:
            view = view.rearrange("p (a b) -> p a b", a=dims[0])
        if len(dims) == 3:
            view = view.rearrange("p (a b c) -> p a b c", a=dims[0], b=dims[1])
        return view


def macaron_kernel(nc, ins, out):
    B, T, C = ins["L0_attn_x"].shape
    TOK = B * T
    NCH = TOK // CH
    NT = TOK // P
    HB = ins["L0_ffn_w_gate"].shape[0] // P
    E, _, EH = ins["L1_ffn_ew1"].shape
    EB = EH // P
    NU = E * EB
    NROT = ins["L1_ffn_gens"].shape[0]
    assert C == P and T == 2 * CH and NCH % 2 == 0 and NU % 8 == 0 and HB == 3

    ctx = ExitStack()
    with ctx:
        ctx.enter_context(nc.allow_non_contiguous_dma(reason="small vectors and permuted rows of weights"))

        def sb(name, shape, dt=F32):
            return ctx.enter_context(nc.sbuf_tensor(name, shape, dt))

        def sem(name):
            return ctx.enter_context(nc.semaphore(name))

        bank = [ctx.enter_context(nc.psum_tensor(f"bank{i}", [P, CH], F32)) for i in range(8)]
        X = sb("X", [P, NT * P])
        ident = sb("ident", [P, P])
        ident16 = sb("ident16", [P, P], F16)
        neghalf = sb("neghalf", [P, TILES])
        negone = sb("negone", [P, TILES])
        eps = sb("eps", [P, TILES])
        nmean = sb("nmean", [P, 2, TILES])
        spare = sb("spare", [P, 4])
        stats = sb("stats", [P, 2, TILES, 6])
        meanvar = sb("meanvar", [P, 2, TILES, 2])
        veps = sb("veps", [P, 2, TILES])
        rstd = sb("rstd", [P, 2, TILES])
        nbias = sb("nbias", [P, 2, TILES])
        f0hi = sb("f0hi", [P, 3, HB * P], F16)
        f0lo = sb("f0lo", [P, 3, HB * P], F16)
        ew1hi = sb("ew1hi", [P, NU, P], F16)
        ew1lo = sb("ew1lo", [P, NU, P], F16)
        ew2hi = sb("ew2hi", [P, NU, P], F16)
        ew2lo = sb("ew2lo", [P, NU, P], F16)
        abhi = sb("abhi", [P, P], F16)
        ablo = sb("ablo", [P, P], F16)
        ebhi = sb("ebhi", [2 * E, P], F16)
        eblo = sb("eblo", [2 * E, P], F16)
        sel = sb("sel", [2 * E, E, P], F16)
        gamma = sb("gamma", [P, 1])
        beta = sb("beta", [P, 1])
        abel_b = sb("abel_b", [P, 1])
        eb1 = sb("eb1", [P, NU])
        gate_w = sb("gate_w", [P, E])
        gate_b = sb("gate_b", [1, E])
        gate_b4 = sb("gate_b4", [P, TILES, E])
        gcw = sb("gcw", [P, 2])
        gcb = sb("gcb", [1, 1])
        gcbh = sb("gcbh", [P, 1])
        gc12 = sb("gc12", [P, 1])
        ones = sb("ones", [1, P])
        iota8 = sb("iota8", [P, TILES, E])
        waT = sb("waT", [P, 4, P])
        tvec = sb("tvec", [P, 5])
        wneg = sb("wneg", [P, 1])
        fw = sb("fw", [P, 4, P])
        WoR = sb("WoR", [P, HD, P])
        WvR = sb("WvR", [P, HD, P])
        bvR = sb("bvR", [P, HD])
        fb = sb("fb", [P, 2])
        bo = sb("bo", [1, P])
        blockones = sb("blockones", [P, P])
        zcol = sb("zcol", [P, 1])
        onecol = sb("onecol", [P, 1])
        arena = sb("arena", [P, 27000])

        a = Arena(arena)
        sm = Buffers()
        sm.wi = a.take([3, HB * P], I32)
        sm.wf = a.take([3, HB * P])
        sm.wa = a.take([4, P])
        sm.ew1 = a.take([NU, P])
        sm.ew2 = a.take([NU, P])
        sm.ab = a.take([P])
        sm.eb2 = a.take([P], parts=E)
        sm.eb2T = a.take([2, E])
        sm.G = a.take([NROT, P])
        sm.Gabs = a.take([NROT, P])
        sm.GT = a.take([NROT, P])
        sm.rot = a.take([NROT, P])
        sm.rotT = a.take([NROT, P])
        sm.ident3 = a.take([NROT, P])
        sm.mask = a.take([NROT, P])
        sm.thr = a.take([NROT, SQUARINGS])
        sm.cneg = a.take([NROT, SQUARINGS])
        sm.active = a.take([NROT, SQUARINGS])
        sm.shrink = a.take([NROT, SQUARINGS])
        sm.rowsum = a.take([NROT])
        sm.norm = a.take([NROT])
        sm.factor = a.take([NROT])
        sm.MT = a.take([P])
        sm.R = a.take([P])
        sm.blkT = a.take([TILES, P])
        a = Arena(arena)
        f0 = Buffers()
        f0.z = a.take([2, CH])
        f0.xhi = a.take([2, CH], F16)
        f0.xlo = a.take([2, CH], F16)
        f0.sg = a.take([2, CH])
        f0.h = a.take([2, CH])
        f0.hhi = a.take([2 * HB, CH], F16)
        f0.hlo = a.take([2 * HB, CH], F16)
        a = Arena(arena)
        tm = Buffers()
        tm.z = a.take([2, CH])
        tm.XN = a.take([1 + 2 * CH])
        tm.D = a.take([CH])
        tm.xk = a.take([CH])
        tm.xv = a.take([CH])
        tm.xr = a.take([CH])
        tm.PM = a.take([1 + 2 * CH])
        tm.SA = a.take([1 + 2 * CH])
        tm.SB = a.take([1 + 2 * CH])
        tm.arg = a.take([4, CH])
        tm.ex = a.take([4, CH])
        tm.q = a.take([CH])
        tm.f2v = a.take([CH])
        tm.e2v = a.take([CH])
        tm.n1 = a.take([CH])
        tm.n2 = a.take([CH])
        tm.num = a.take([CH])
        tm.den = a.take([CH])
        tm.lnd = a.take([CH])
        tm.r0 = a.take([CH])
        tm.t = a.take([CH])
        tm.sr = a.take([CH])
        tm.y = a.take([2, CH])
        a = Arena(arena)
        mo = Buffers()
        mo.z1 = a.take([2, CH])
        mo.z2 = a.take([2, CH])
        mo.xn = a.take([CH])
        mo.xhi = a.take([2, CH], F16)
        mo.xlo = a.take([2, CH], F16)
        mo.hf = a.take([4, CH])
        mo.hw = a.take([4, CH])
        mo.hhi = a.take([8, CH], F16)
        mo.hlo = a.take([8, CH], F16)
        mo.ab = a.take([2, CH])
        mo.dm = a.take([2, CH])
        mo.m = a.take([CH])
        mo.lgs = a.take([TILES, E])
        mo.top = a.take([TILES, E])
        mo.topi = a.take([TILES, E], U32)
        mo.topf = a.take([TILES, E])
        mo.dtop = a.take([TILES])
        mo.th = a.take([TILES])
        mo.w12 = a.take([2, TILES])
        mo.eq = a.take([2, TILES, E])
        mo.wd = a.take([TILES, E])
        mo.wp = a.take([TILES, 2 * E], F16)
        mo.wT = a.take([2, CH], F16, parts=2 * E)
        mo.tg = a.take([TILES])
        mo.gq = a.take([TILES])
        a = Arena(arena)
        fl = Buffers()
        fl.NRM = a.take([2, CH])
        fl.INV = a.take([2, CH])
        fl.z = a.take([2, CH])
        fl.xn = a.take([2, CH])
        fl.q = a.take([CH])
        fl.k = a.take([CH])
        fl.NQ = a.take([CH])
        fl.NK = a.take([CH])
        fl.Ck = a.take([CH])
        fl.Cq = a.take([CH])
        fl.Cks = a.take([CH])
        fl.Cqs = a.take([CH])
        fl.Cc = a.take([CH])
        fl.pr = a.take([2, CH])
        fl.lnd = a.take([2, CH])
        fl.r = a.take([2, CH])
        fl.t = a.take([CH])
        fl.rd = a.take([2, CH])
        fl.ks = a.take([CH])
        fl.c = a.take([2, CH])
        fl.sa = a.take([CH])
        fl.cs = a.take([CH])
        fl.rc = a.take([CH])
        fl.m1 = a.take([CH])
        fl.kc = a.take([2, CH])
        fl.qr = a.take([CH])
        fl.qq = a.take([2, CH])
        fl.kv = a.take([2, CH])
        fl.S = a.take([HD, CH])
        fl.pd = a.take([4, CH])

        S0 = Semaphores()
        S0.x_first = sem("setup_x_first")
        S0.x_rest = sem("setup_x_rest")
        S0.w_ffn0 = sem("setup_w_ffn0")
        S0.w_attn0 = sem("setup_w_attn0")
        S0.w_moe = sem("setup_w_moe")
        S0.w_gens = sem("setup_w_gens")
        S0.w_flow = sem("setup_w_flow")
        S0.consts = sem("setup_consts")
        S0.dve = sem("setup_dve")
        S0.act = sem("setup_act")
        S0.pool = sem("setup_pool")
        S0.loop_pe = sem("setup_loop_pe")
        S0.pair = sem("setup_pair")
        S0.loop_mask = sem("setup_loop_mask")
        S0.norm = sem("setup_norm")
        S0.cast = sem("setup_cast")
        S0.gabs = sem("setup_gabs")
        S0.rowsum = sem("setup_rowsum")
        S0.trf = sem("setup_trf")
        S0.f0hi = sem("setup_f0hi")
        S0.f0lo = sem("setup_f0lo")
        S0.trw = sem("setup_trw")
        S0.decay = sem("setup_decay")
        S0.e1hi = sem("setup_e1hi")
        S0.small = sem("setup_small")
        S0.small2 = sem("setup_small2")
        S0.eb2T = sem("setup_eb2T")
        S0.g = sem("setup_g")
        S0.gtp = sem("setup_gtp")
        S0.gt = sem("setup_gt")
        S0.rot = sem("setup_rot")
        S0.hp = sem("setup_hp")
        S0.rtp = sem("setup_rtp")
        S0.mtp = sem("setup_mtp")
        S0.mt = sem("setup_mt")
        S0.rp = sem("setup_rp")
        S0.r = sem("setup_r")
        S0.ft = sem("setup_ft")
        S0.fT = sem("setup_fT")
        S0.fm = sem("setup_fm")
        S0.fhi = sem("setup_fhi")
        S0.flo = sem("setup_flo")
        S0.nrm = sem("setup_nrm")
        FF = Semaphores()
        FF.stats = sem("ffn_stats")
        FF.rstd = sem("ffn_rstd")
        FF.z = sem("ffn_z")
        FF.tr = sem("ffn_tr")
        FF.chain = sem("ffn_chain")
        FF.pchain = sem("ffn_pchain")
        FF.x = sem("ffn_x")
        FF.xhi = sem("ffn_xhi")
        FF.xlo = sem("ffn_xlo")
        FF.gu = sem("ffn_gu")
        FF.sg = sem("ffn_sg")
        FF.h = sem("ffn_h")
        FF.hhi = sem("ffn_hhi")
        FF.hlo = sem("ffn_hlo")
        FF.down = sem("ffn_down")
        TM = Semaphores()
        TM.stats = sem("mix_stats")
        TM.rstd = sem("mix_rstd")
        TM.z = sem("mix_z")
        TM.tr = sem("mix_tr")
        TM.chain = sem("mix_chain")
        TM.pchain = sem("mix_pchain")
        TM.x = sem("mix_x")
        TM.init = sem("mix_init")
        TM.own = sem("mix_own")
        TM.xn = sem("mix_xn")
        TM.d = sem("mix_d")
        TM.xkvr = sem("mix_xkvr")
        TM.kv = sem("mix_kv")
        TM.arg_q = sem("mix_arg_q")
        TM.arg3 = sem("mix_arg3")
        TM.args = sem("mix_args")
        TM.ex = sem("mix_ex")
        TM.dex = sem("mix_dex")
        TM.sr = sem("mix_sr")
        TM.den = sem("mix_den")
        TM.scans = sem("mix_scans")
        TM.n12 = sem("mix_n12")
        TM.y = sem("mix_y")
        TM.out = sem("mix_out")
        MO = Semaphores()
        MO.stats = sem("moe_stats")
        MO.rstd = sem("moe_rstd")
        MO.z = sem("moe_z")
        MO.tr = sem("moe_tr")
        MO.chain = sem("moe_chain")
        MO.pchain = sem("moe_pchain")
        MO.x = sem("moe_x")
        MO.own = sem("moe_own")
        MO.xhi = sem("moe_xhi")
        MO.xlo = sem("moe_xlo")
        MO.stats2 = sem("moe_stats2")
        MO.rstd2 = sem("moe_rstd2")
        MO.z2 = sem("moe_z2")
        MO.xn = sem("moe_xn")
        MO.logits = sem("moe_logits")
        MO.dtop = sem("moe_dtop")
        MO.th = sem("moe_th")
        MO.wpair = sem("moe_wpair")
        MO.wpT = sem("moe_wpT")
        MO.wT = sem("moe_wT")
        MO.abel_mm = sem("moe_abel_mm")
        MO.abel = sem("moe_abel")
        MO.mm1 = sem("moe_mm1")
        MO.gelu = sem("moe_gelu")
        MO.wb = sem("moe_wb")
        MO.hw = sem("moe_hw")
        MO.hhi = sem("moe_hhi")
        MO.hlo = sem("moe_hlo")
        MO.mm2 = sem("moe_mm2")
        MO.dm = sem("moe_dm")
        MO.gate = sem("moe_gate")
        MO.tg = sem("moe_tg")
        MO.gq = sem("moe_gq")
        MO.abT = sem("moe_abT")
        MO.r2 = sem("moe_r2")
        MO.dmT = sem("moe_dmT")
        MO.zadd = sem("moe_zadd")
        MO.m = sem("moe_m")
        FL = Semaphores()
        FL.stats = sem("flow_stats")
        FL.rstd = sem("flow_rstd")
        FL.z = sem("flow_z")
        FL.tr = sem("flow_tr")
        FL.chain = sem("flow_chain")
        FL.pchain = sem("flow_pchain")
        FL.x = sem("flow_x")
        FL.own = sem("flow_own")
        FL.inv = sem("flow_inv")
        FL.xn = sem("flow_xn")
        FL.qk = sem("flow_qk")
        FL.sig = sem("flow_sig")
        FL.nqk = sem("flow_nqk")
        FL.pr = sem("flow_pr")
        FL.den = sem("flow_den")
        FL.lnr = sem("flow_lnr")
        FL.sa_cs = sem("flow_sa_cs")
        FL.c12 = sem("flow_c12")
        FL.kcqq = sem("flow_kcqq")
        FL.v = sem("flow_v")
        FL.kv = sem("flow_kv")
        FL.s = sem("flow_s")
        FL.pd = sem("flow_pd")
        FL.out = sem("flow_out")
        N_CONST = 11
        N_MOE = 13
        N_FLOW = 4 + 2 + 1 + 2 * (2 * HD - 1)

        CREDIT = 1

        def wait_apart(eng, sem, count):
            eng.wait_ge(sem, count)
            eng.memset(spare[:, 0:1], 0.0)

        def stages(eng, ffn0, mixing, experts, flow):
            eng.wait_ge(S0.consts, N_CONST)
            eng.wait_ge(S0.flo, NU // TILES + 1)
            eng.wait_ge(S0.x_first, 16)
            eng.wait_ge(S0.x_rest, 16 * (NCH - 1))
            ffn0(FF, 0)
            eng.wait_ge(FF.x, NCH)
            mixing(TM, 0)
            eng.wait_ge(TM.x, NCH + CREDIT)
            ffn0(FF, NCH)
            eng.wait_ge(FF.x, 2 * NCH)
            experts(MO, 0)
            eng.wait_ge(MO.x, NCH)
            flow(FL, 0)
            eng.wait_ge(FL.x, NCH + CREDIT)
            experts(MO, NCH)
        stored = ctx.enter_context(nc.semaphore("stored"))

        x_tiles = ins["L0_attn_x"].rearrange("b (t p) c -> p (b t) c", p=P)
        out_tiles = out.rearrange("b (t p) c -> p (b t) c", p=P)
        X3 = X[:, :].rearrange("p (t c) -> p t c", c=P)

        block = ctx.enter_context(nc.Block())

        @block.sync
        def _(sp):
            sp.dma_start(X3[:, 0:TILES, :], x_tiles[:, 0:TILES, :]).then_inc(S0.x_first, 16)
            for k, name in enumerate(("gate", "up")):
                sp.dma_start(sm.wi[:, k, :].rearrange("p (j d) -> p j d", d=P),
                             ins[f"L0_ffn_w_{name}"].rearrange("(j p) d -> p j d", p=P)).then_inc(S0.w_ffn0, 16)
            sp.dma_start(sm.wi[:, 2, :], ins["L0_ffn_w_down"]).then_inc(S0.w_ffn0, 16)
            sp.dma_start(sm.G, ins["L1_ffn_gens"].rearrange("r p c -> p r c")).then_inc(S0.w_gens, 16)
            for k, name in enumerate(("Wk", "Wv", "Wr", "Wo")):
                sp.dma_start(sm.wa[:, k, :], ins[f"L0_attn_{name}"]).then_inc(S0.w_attn0, 16)
            for k, name in enumerate(("time_decay", "time_first", "time_mix_k", "time_mix_v", "time_mix_r")):
                sp.dma_start(tvec[:, k:k + 1], ins[f"L0_attn_{name}"].rearrange("a b c -> c (a b)"))\
                  .then_inc(S0.w_attn0, 16)
            for c in range(1, NCH):
                sp.dma_start(X3[:, c * TILES:(c + 1) * TILES, :], x_tiles[:, c * TILES:(c + 1) * TILES, :])\
                  .then_inc(S0.x_rest, 16)
            ew2_rows = ins["L1_ffn_ew2"].rearrange("e (j p) d -> p (e j) d", p=P)
            moe_loads = [
                (sm.ew1.rearrange("p (e j) n -> p e (j n)", j=EB), ins["L1_ffn_ew1"].rearrange("e c h -> c e h")),
                (sm.ew2[:, 0:NU // 2, :], ew2_rows[:, 0:NU // 2, :]),
                (sm.ew2[:, NU // 2:NU, :], ew2_rows[:, NU // 2:NU, :]),
                (sm.ab, ins["L1_ffn_abel_w"]),
                (sm.eb2, ins["L1_ffn_eb2"]),
                (gamma[:, :], ins["L1_ffn_ln_gamma"].rearrange("(c o) -> c o", o=1)),
                (beta[:, :], ins["L1_ffn_ln_beta"].rearrange("(c o) -> c o", o=1)),
                (abel_b[:, :], ins["L1_ffn_abel_b"].rearrange("(c o) -> c o", o=1)),
                (eb1[:, :], ins["L1_ffn_eb1"].rearrange("e (j p) -> p (e j)", p=P)),
                (gate_w[:, :], ins["L1_ffn_moe_gate_w"]),
                (gate_b[:, :], ins["L1_ffn_moe_gate_b"].rearrange("(o e) -> o e", o=1)),
                (gcw[:, :], ins["L1_ffn_gc_w"].rearrange("(a p) o -> p (a o)", p=P)),
                (gcb[:, :], ins["L1_ffn_gc_b"].rearrange("(o e) -> o e", o=1)),
            ]
            assert len(moe_loads) == N_MOE
            for dst, src in moe_loads:
                sp.dma_start(dst, src).then_inc(S0.w_moe, 16)
            for k, name in enumerate(("Wq", "Wk", "Wv", "Wo")):
                sp.dma_start(fw[:, k, :], ins[f"L1_attn_{name}"]).then_inc(S0.w_flow, 16)
            for k, name in enumerate(("bq", "bk")):
                sp.dma_start(fb[:, k:k + 1], ins[f"L1_attn_{name}"].rearrange("(c o) -> c o", o=1))\
                  .then_inc(S0.w_flow, 16)
            sp.dma_start(bo[:, :], ins["L1_attn_bo"].rearrange("(o c) -> o c", o=1)).then_inc(S0.w_flow, 16)
            wo_rows = ins["L1_attn_Wo"].rearrange("(h m) n -> h m n", m=HD)
            bv_rows = ins["L1_attn_bv"].rearrange("(h m) -> h m", m=HD)
            for d in range(HD):
                sp.dma_start(WoR[d:P:HD, 0:HD - d, :], wo_rows[:, d:HD, :]).then_inc(S0.w_flow, 16)
                sp.dma_start(bvR[d:P:HD, 0:HD - d], bv_rows[:, d:HD]).then_inc(S0.w_flow, 16)
                if d:
                    sp.dma_start(WoR[d:P:HD, HD - d:HD, :], wo_rows[:, 0:d, :]).then_inc(S0.w_flow, 16)
                    sp.dma_start(bvR[d:P:HD, HD - d:HD], bv_rows[:, 0:d]).then_inc(S0.w_flow, 16)
            with sp.Fori(0, NCH) as c:
                sp.wait_ge(MO.x, c + (NCH + 1))
                sp.dma_start(out_tiles[:, bass.ds(c * TILES, TILES), :],
                             X3[:, bass.ds(c * TILES, TILES), :]).then_inc(stored, 16)
            sp.wait_ge(stored, 16 * NCH)

        @block.gpsimd
        def _(pool):

            def setup():
                pool.memset(ident[:, :], 0.0).then_inc(S0.pool, 1)
                pool.memset(ident16[:, :], 0.0).then_inc(S0.pool, 1)
                pool.memset(sm.ident3, 0.0).then_inc(S0.pool, 1)
                pool.memset(sel[:, :, :], 0.0).then_inc(S0.pool, 1)
                pool.memset(blockones[:, :], 1.0).then_inc(S0.pool, 1)
                pool.memset(neghalf[:, :], -0.5).then_inc(S0.consts, 1)
                pool.memset(negone[:, :], -1.0).then_inc(S0.consts, 1)
                pool.memset(eps[:, :], LN_EPS).then_inc(S0.consts, 1)
                pool.memset(ones[:, :], 1.0).then_inc(S0.consts, 1)
                pool.memset(onecol[:, :], 1.0).then_inc(S0.consts, 1)
                pool.iota(iota8[:, :, :], [[0, TILES], [1, E]], base=0, channel_multiplier=0,
                          allow_small_or_imprecise_dtypes=True).then_inc(S0.consts, 1)
                pool.wait_ge(S0.pool, 5)
                pool.affine_select(out=sel[:, :, :], in_=sel[:, :, :], compare_op=ALU.not_equal, fill=1.0, base=0,
                                   pattern=[[-1, E], [0, P]], channel_multiplier=1).then_inc(S0.pool, 1)
                pool.affine_select(out=blockones[:, :], in_=blockones[:, :], compare_op=ALU.is_ge, fill=0.0,
                                   base=0, pattern=[[-HD, HEADS], [0, HD]], channel_multiplier=1)\
                    .then_inc(S0.pool, 1)
                for m in (ident[:, :], ident16[:, :]):
                    pool.affine_select(out=m, in_=m, compare_op=ALU.not_equal, fill=1.0, base=0,
                                       pattern=[[-1, P]], channel_multiplier=1).then_inc(S0.consts, 1)
                pool.affine_select(out=sm.ident3, in_=sm.ident3, compare_op=ALU.not_equal, fill=1.0, base=0,
                                   pattern=[[0, NROT], [-1, P]], channel_multiplier=1).then_inc(S0.consts, 1)
                pool.wait_ge(S0.pool, 7)
                pool.affine_select(out=sel[:, :, :], in_=sel[:, :, :], compare_op=ALU.not_equal, fill=1.0, base=-E,
                                   pattern=[[-1, E], [0, P]], channel_multiplier=1).then_inc(S0.consts, 1)
                pool.affine_select(out=blockones[:, :], in_=blockones[:, :], compare_op=ALU.is_ge, fill=0.0,
                                   base=HD - 1, pattern=[[HD, HEADS], [0, HD]], channel_multiplier=-1)\
                    .then_inc(S0.consts, 1)
                pool.wait_ge(S0.rowsum, 1)
                pool.partition_all_reduce(sm.norm, sm.rowsum, P, RMAX).then_inc(S0.norm, 1)

            def inv_std(S, stat_sem, out_sem, chain, c, p):
                pool.wait_ge(stat_sem, c + 1)
                chain.link(pool.tensor_tensor(veps[:, p, :], meanvar[:, p, :, 1], eps[:, :], ALU.add))
                pool.tensor_tensor(nmean[:, p, :], meanvar[:, p, :, 0], negone[:, :], ALU.mult)
                chain.link(pool.tensor_tensor(rstd[:, p, :], veps[:, p, :], neghalf[:, :], ALU.pow))
                pool.tensor_tensor(nbias[:, p, :], nmean[:, p, :], rstd[:, p, :], ALU.mult).then_inc(out_sem, 1)

            def ffn0(S, first):
                chain = Chain(pool, S.pchain, 2)

                def step(i, p, lead, mid, lag):
                    if lead:
                        chain.at(i + 1)
                        inv_std(S, S.stats, S.rstd, chain, i + 1, 1 - p)
                        chain.close()
                    if mid:
                        for j in range(HB):
                            u = HB * p + j
                            pool.wait_ge(S.hhi, HB * i + j + 1)
                            pool.tensor_tensor(f0.hlo[:, u, :], f0.h[:, u % 2, :], f0.hhi[:, u, :],
                                               ALU.subtract).then_inc(S.hlo, 1)
                pipeline(pool, first, NCH, step)

            def mixing(S, first):
                chain = Chain(pool, S.pchain, 2)

                def step(i, p, lead, mid, lag):
                    o = p * CH
                    if mid:
                        pool.wait_ge(S.arg_q, i + 1)
                        pool.tensor_tensor(tm.arg[:, 2, :], tm.PM[:, o:o + CH], tm.q, ALU.subtract)\
                            .then_inc(S.arg3, 1)
                    if lead:
                        chain.at(i + 1)
                        inv_std(S, S.stats, S.rstd, chain, i + 1, 1 - p)
                        chain.close()
                        n = (1 - p) * CH
                        pool.wait_ge(S.xn, i + 2)
                        pool.tensor_tensor(tm.D, tm.XN[:, 1 + n:1 + n + CH], tm.XN[:, n:n + CH],
                                           ALU.subtract).then_inc(S.d, 1)
                    if mid:
                        pool.wait_ge(S.ex, 4 * i + 4)
                        pool.wait_ge(S.scans, 2 * i + 2)
                        pool.tensor_tensor(tm.n1, tm.ex[:, 2, :], tm.SA[:, o:o + CH], ALU.mult)\
                            .then_inc(S.n12, 1)
                        pool.tensor_tensor(tm.n2, tm.ex[:, 2, :], tm.SB[:, o:o + CH], ALU.mult)\
                            .then_inc(S.n12, 1)
                pipeline(pool, first, NCH, step)

            def experts(S, first):
                chain = Chain(pool, S.pchain, 4)

                def step(i, p, lead, mid, lag):
                    def low(u):
                        pool.wait_ge(S.hhi, NU * i + u + 1)
                        pool.tensor_tensor(mo.hlo[:, u % 8, :], mo.hw[:, u % 4, :], mo.hhi[:, u % 8, :],
                                           ALU.subtract).then_inc(S.hlo, 1)
                    for u in range(NU):
                        if lead and u == 0:
                            chain.at(i + 1)
                            inv_std(S, S.stats, S.rstd, chain, i + 1, 1 - p)
                        if lead and u == 3:
                            inv_std(S, S.stats2, S.rstd2, chain, i + 1, 1 - p)
                            chain.close()
                        if mid:
                            low(u)
                pipeline(pool, first, NCH, step)

            def flow(S, first):
                chain = Chain(pool, S.pchain, 2)
                pool.iota(fl.NRM.rearrange("p a n -> p (a n)"), [[1, 2 * CH]], base=1, channel_multiplier=0,
                          allow_small_or_imprecise_dtypes=True).then_inc(S0.nrm, 1)
                pool.wait_ge(S0.nrm, 1)

                def step(i, p, lead, mid, lag):
                    if mid:
                        pool.wait_ge(S.sig, 2 * i + 2)
                        pool.tensor_tensor(fl.NK, fl.k, fl.NRM[:, p, :], ALU.mult).then_inc(S.nqk, 1)
                        pool.tensor_tensor(fl.NQ, fl.q, fl.NRM[:, p, :], ALU.mult).then_inc(S.nqk, 1)
                    for o in range(HD):
                        if lag:
                            pool.wait_ge(S.s, HD * (i - 1) + o + 1)
                            after(pool, S.out, HD * (i - 1) + max(o - 3, 0) + CREDIT)
                            pool.tensor_tensor(fl.pd[:, o % 4, :], fl.S[:, o, :], fl.qq[:, 1 - p, :],
                                               ALU.mult).then_inc(S.pd, 1)
                        if lead and o == 1:
                            chain.at(i + 1)
                            inv_std(S, S.stats, S.rstd, chain, i + 1, 1 - p)
                            chain.close()
                pipeline(pool, first, NCH, step)

            setup()
            stages(pool, ffn0, mixing, experts, flow)

        @block.scalar
        def _(act):
            A = act.activation

            def setup():
                act.wait_ge(S0.w_gens, 16)
                A(sm.Gabs, sm.G, ACT.Abs).then_inc(S0.gabs, 1)
                for k in range(3):
                    act.wait_ge(S0.trf, k + 1)
                    A(f0hi[:, k, :], bank[k][:, 0:HB * P], ACT.Copy).then_inc(S0.f0hi, 1)
                act.wait_ge(S0.trw, 1)
                A(waT[:, :, :].rearrange("p a b -> p (a b)"), bank[3][:, :], ACT.Copy).then_inc(S0.act, 1)
                A(wneg[:, :], tvec[:, 0:1], ACT.Exp).then_inc(S0.decay, 1)
                act.wait_ge(S0.gtp, 1)
                A(sm.GT.rearrange("p a b -> p (a b)"), bank[6][:, 0:NROT * P], ACT.Copy).then_inc(S0.gt, 1)
                act.wait_ge(S0.w_moe, 16 * N_MOE)
                A(ew1hi[:, :, :], sm.ew1, ACT.Copy, scale=WS).then_inc(S0.e1hi, 1)
                A(abhi[:, :], sm.ab, ACT.Copy, scale=WS).then_inc(S0.e1hi, 1)
                act.wait_ge(S0.rtp, 1)
                A(sm.rotT.rearrange("p a b -> p (a b)"), bank[7][:, 0:NROT * P], ACT.Copy).then_inc(S0.pair, 1)
                act.wait_ge(S0.mtp, 1)
                A(sm.MT, bank[6][:, 0:P], ACT.Copy).then_inc(S0.mt, 1)
                act.wait_ge(S0.rp, 1)
                A(sm.R, bank[7][:, 0:P], ACT.Copy).then_inc(S0.r, 1)
                act.wait_ge(S0.small, 1)
                for n in range(2):
                    A(sm.eb2T[:, n, :], bank[4][:, 0:E], ACT.Copy).then_inc(S0.eb2T, 1)
                for g in range(NU // TILES):
                    act.wait_ge(S0.ft, g + 1)
                    A(sm.blkT.rearrange("p a b -> p (a b)"), bank[0][:, :], ACT.Copy).then_inc(S0.fT, 1)
                    act.wait_ge(S0.fm, g + 1)
                    A(ew2hi[:, TILES * g:TILES * g + TILES, :].rearrange("p a b -> p (a b)"), bank[1][:, :],
                      ACT.Copy, scale=WS).then_inc(S0.fhi, 1)
                act.wait_ge(S0.fm, NU // TILES + 1)
                A(ebhi[:, :], bank[2][0:2 * E, 0:P], ACT.Copy, scale=WS).then_inc(S0.fhi, 1)

            def normalise(z, zp, c, p, sem, first):
                for t in range(TILES):
                    ins_ = A(z[:, zp, t * P:(t + 1) * P], X[:, bass.ds((c - first) * CH + t * P, P)], ACT.Identity,
                             bias=nbias[:, p, t:t + 1], scale=rstd[:, p, t:t + 1])
                ins_.then_inc(sem, 1)

            def ffn0(S, first):
                def step(i, p, lead, mid, lag):
                    def low(j):
                        act.wait_ge(S.h, HB * i + j + 1)
                        A(f0.hhi[:, HB * p + j, :], f0.h[:, (HB * p + j) % 2, :], ACT.Copy).then_inc(S.hhi, 1)
                    for j in range(HB):
                        if mid:
                            act.wait_ge(S.gu, HB * i + j + 1)
                            A(f0.sg[:, (HB * p + j) % 2, :], bank[1 + (HB * p + j) % 2][:, :], ACT.Silu,
                              scale=QSCALE).then_inc(S.sg, 1)
                        if lead and j == 0:
                            act.wait_ge(S.rstd, i + 2)
                            normalise(f0.z, 1 - p, i + 1, 1 - p, S.z, first)
                        if mid and j:
                            low(j - 1)
                        if lead and j == 1:
                            act.wait_ge(S.tr, i + 2)
                            A(f0.xhi[:, 1 - p, :], bank[0][:, :], ACT.Copy).then_inc(S.xhi, 1)
                    if mid:
                        low(HB - 1)
                pipeline(act, first, NCH, step)

            def mixing(S, first):
                def step(i, p, lead, mid, lag):
                    if mid:
                        o = p * CH
                        act.wait_ge(S.args, 3 * i + 1)
                        A(tm.ex[:, 0, :], tm.arg[:, 0, :], ACT.Exp).then_inc(S.ex, 1)
                        act.wait_ge(S.args, 3 * i + 2)
                        A(tm.ex[:, 1, :], tm.arg[:, 1, :], ACT.Exp).then_inc(S.ex, 1)
                        act.wait_ge(S.args, 3 * i + 3)
                        A(tm.ex[:, 3, :], tm.arg[:, 3, :], ACT.Exp).then_inc(S.ex, 1)
                        act.wait_ge(S.arg3, i + 1)
                        A(tm.ex[:, 2, :], tm.arg[:, 2, :], ACT.Exp).then_inc(S.ex, 1)
                    if lead:
                        act.wait_ge(S.rstd, i + 2)
                        normalise(tm.z, 1 - p, i + 1, 1 - p, S.z, first)
                        act.wait_ge(S.tr, i + 2)
                        n = 1 + (1 - p) * CH
                        A(tm.XN[:, n:n + CH], bank[0][:, :], ACT.Copy).then_inc(S.xn, 1)
                    if mid:
                        act.wait_ge(S.kv, 3 * i + 3)
                        A(tm.sr, bank[3 + 3 * p][:, :], ACT.Sigmoid).then_inc(S.sr, 1)
                        act.wait_ge(S.den, i + 1)
                        A(tm.lnd, tm.den, ACT.Ln).then_inc(S.dex, 1)
                        act.wait_ge(S.dex, 2 * i + 1)
                        A(tm.r0, tm.lnd, ACT.Exp, scale=-1.0).then_inc(S.dex, 1)
                pipeline(act, first, NCH, step)

            def experts(S, first):
                def step(i, p, lead, mid, lag):
                    def high(c, u):
                        act.wait_ge(S.hw, NU * c + u + 1)
                        after(act, S.mm2, NU * c + u - 7)
                        A(mo.hhi[:, u % 8, :], mo.hw[:, u % 4, :], ACT.Copy).then_inc(S.hhi, 1)
                    for u in range(NU):
                        if mid:
                            act.wait_ge(S.mm1, NU * i + u + 1)
                            after(act, S.hw, NU * i + u - 3)
                            A(mo.hf[:, u % 4, :], bank[1 + u % 2][:, :], ACT.Gelu, scale=1.0 / WS,
                              bias=eb1[:, u:u + 1]).then_inc(S.gelu, 1)
                            if u:
                                high(i, u - 1)
                        if lead and u == 1:
                            act.wait_ge(S.rstd, i + 2)
                            normalise(mo.z1, 1 - p, i + 1, 1 - p, S.z, first)
                        if lead and u == 4:
                            act.wait_ge(S.rstd2, i + 2)
                            for t in range(TILES):
                                last = A(mo.z2[:, 1 - p, t * P:(t + 1) * P], mo.z1[:, 1 - p, t * P:(t + 1) * P],
                                         ACT.Identity, bias=nbias[:, 1 - p, t:t + 1],
                                         scale=rstd[:, 1 - p, t:t + 1])
                            last.then_inc(S.z2, 1)
                        if lag and u == 7:
                            act.wait_ge(S.gate, i)
                            A(mo.tg, bank[7][:, 0:TILES], ACT.Tanh, scale=0.5, bias=gcbh[:, :]).then_inc(S.tg, 1)
                        if lead and u == 7:
                            act.wait_ge(S.tr, i + 2)
                            A(mo.xn, bank[0][:, :], ACT.Identity, scale=gamma[:, :], bias=beta[:, :])\
                                .then_inc(S.xn, 1)
                        if lead and u == 11:
                            act.wait_ge(S.dtop, i + 2)
                            A(mo.th, mo.dtop, ACT.Tanh, scale=0.5).then_inc(S.th, 1)
                        if lead and u == NU - 1:
                            act.wait_ge(S.abel_mm, i + 2)
                            A(mo.ab[:, 1 - p, :], bank[7][:, :], ACT.Gelu, scale=1.0 / WS, bias=abel_b[:, :])\
                                .then_inc(S.abel, 1)
                    if mid:
                        high(i, NU - 1)
                pipeline(act, first, NCH, step)

            def flow(S, first):
                def step(i, p, lead, mid, lag):
                    if mid:
                        for n, dst in enumerate((fl.q, fl.k)):
                            act.wait_ge(S.qk, 2 * i + n + 1)
                            after(act, S.kcqq, 2 * i)
                            A(dst, bank[1 + n][:, :], ACT.Sigmoid, bias=fb[:, n:n + 1]).then_inc(S.sig, 1)
                        for n in range(2):
                            act.wait_ge(S.den, 4 * i + n + 1)
                            A(fl.lnd[:, n, :], bank[3 + n][:, :], ACT.Ln).then_inc(S.lnr, 1)
                        for n in range(2):
                            act.wait_ge(S.lnr, 4 * i + n + 1)
                            A(fl.r[:, n, :], fl.lnd[:, n, :], ACT.Exp, scale=-1.0).then_inc(S.lnr, 1)
                    if lead:
                        act.wait_ge(S.rstd, i + 2)
                        normalise(fl.z, 1 - p, i + 1, 1 - p, S.z, first)
                        act.wait_ge(S.tr, i + 2)
                        after(act, S.v, HD * i)
                        A(fl.xn[:, 1 - p, :], bank[0][:, :], ACT.Copy).then_inc(S.xn, 1)
                    if mid:
                        act.wait_ge(S.c12, 2 * i + 1)
                        A(fl.sa, fl.c[:, 0, :], ACT.Sigmoid, scale=-1.0).then_inc(S.sa_cs, 1)
                        act.wait_ge(S.c12, 2 * i + 2)
                        A(fl.cs, fl.c[:, 1, :], ACT.Exp, scale=-1.0).then_inc(S.sa_cs, 1)
                pipeline(act, first, NCH, step)

            setup()
            stages(act, ffn0, mixing, experts, flow)

        @block.vector
        def _(dve):
            TS, TT, STT = dve.tensor_scalar, dve.tensor_tensor, dve.scalar_tensor_tensor
            flat = "p a b -> p (a b)"

            def setup():
                chain = Chain(dve, S0.dve)
                dve.wait_ge(S0.w_ffn0, 48)
                dve.tensor_copy(sm.wf, sm.wi).then_inc(S0.cast, 1)
                for i in range(SQUARINGS):
                    last = dve.memset(sm.thr[:, :, i:i + 1], float(2 ** i))
                chain.link(last)
                dve.wait_ge(S0.gabs, 1)
                dve.tensor_reduce(sm.rowsum, sm.Gabs, AX.X, ALU.add).then_inc(S0.rowsum, 1)
                chain.link(dve.reciprocal(sm.cneg.rearrange(flat), sm.thr.rearrange(flat)))
                chain.link(TS(sm.cneg.rearrange(flat), sm.cneg.rearrange(flat), 0.5, -1.0, ALU.mult, ALU.add))
                for k in range(3):
                    dve.wait_ge(S0.f0hi, k + 1)
                    TT(f0lo[:, k, :], bank[k][:, 0:HB * P], f0hi[:, k, :], ALU.subtract).then_inc(S0.f0lo, 1)
                dve.wait_ge(S0.norm, 1)
                for r in range(NROT):
                    last = TS(sm.active[:, r, :], sm.thr[:, r, :], sm.norm[:, r:r + 1], None, ALU.is_lt)
                chain.link(last)
                chain.link(TT(sm.shrink, sm.active, sm.cneg, ALU.mult))
                chain.link(TS(sm.shrink, sm.shrink, 1.0, None, ALU.add))
                chain.link(dve.tensor_reduce(sm.factor, sm.shrink, AX.X, ALU.min))
                for r in range(NROT):
                    last = TS(sm.G[:, r, :], sm.G[:, r, :], sm.factor[:, r:r + 1], None, ALU.mult)
                last.then_inc(S0.g, 1)
                dve.wait_ge(S0.g, 1)
                dve.wait_ge(S0.consts, N_CONST)
                STT(out=sm.rot, in0=sm.G, scalar=1.0 / TAYLOR, in1=sm.ident3, op0=ALU.mult, op1=ALU.add)\
                    .then_inc(S0.rot, 1)
                for n, k in enumerate(range(TAYLOR - 1, 0, -1)):
                    dve.wait_ge(S0.hp, n + 1)
                    STT(out=sm.rot.rearrange(flat), in0=bank[6][:, 0:NROT * P], scalar=1.0 / k,
                        in1=sm.ident3.rearrange(flat), op0=ALU.mult, op1=ALU.add).then_inc(S0.rot, 1)
                with dve.Fori(0, SQUARINGS) as i:
                    dve.wait_ge(S0.pair, i + 1)
                    for r in range(NROT):
                        last = dve.tensor_copy(sm.mask[:, r, :],
                                               sm.active[:, r, bass.ds(i, 1)].to_broadcast([P, P]))
                    last.then_inc(S0.loop_mask, 1)
                    dve.wait_ge(S0.loop_mask, i + 1)
                    wait_apart(dve, S0.loop_pe, i + 1)
                    bits = sm.mask.rearrange(flat).bitcast(I32)
                    dve.copy_predicated(sm.rot.rearrange(flat), bits, bank[6][:, 0:NROT * P])
                    dve.copy_predicated(sm.rotT.rearrange(flat), bits, bank[7][:, 0:NROT * P])\
                       .then_inc(S0.pair, 1)
                dve.wait_ge(S0.decay, 1)
                chain.link(TS(wneg[:, :], wneg[:, :], -1.0, None, ALU.mult))
                dve.wait_ge(S0.e1hi, 2)
                STT(out=ew1lo[:, :, :], in0=sm.ew1, scalar=WS, in1=ew1hi[:, :, :], op0=ALU.mult, op1=ALU.subtract)
                STT(out=ablo[:, :], in0=sm.ab, scalar=WS, in1=abhi[:, :], op0=ALU.mult, op1=ALU.subtract)
                TT(gc12[:, :], gcw[:, 0:1], gcw[:, 1:2], ALU.add)
                dve.wait_ge(S0.small2, 1)
                for t in range(TILES):
                    dve.tensor_copy(gate_b4[:, t, :], bank[5][:, 0:E])
                TS(gcbh[:, :], bank[5][:, E:E + 1], 0.5, None, ALU.mult)
                dve.wait_ge(S0.w_flow, 16 * N_FLOW)
                wv = fw[:, 2, :].rearrange("p (h m) -> p h m", m=HD)
                for o in range(HD):
                    turned = WvR[:, o, :].rearrange("p (h d) -> p h d", d=HD)
                    last = dve.tensor_copy(turned[:, :, 0:HD - o], wv[:, :, o:HD])
                    if o:
                        last = dve.tensor_copy(turned[:, :, HD - o:HD], wv[:, :, 0:o])
                for g in range(NU // TILES):
                    dve.wait_ge(S0.fhi, g + 1)
                    STT(out=ew2lo[:, TILES * g:TILES * g + TILES, :].rearrange(flat), in0=bank[1][:, :], scalar=WS,
                        in1=ew2hi[:, TILES * g:TILES * g + TILES, :].rearrange(flat), op0=ALU.mult,
                        op1=ALU.subtract).then_inc(S0.flo, 1)
                dve.wait_ge(S0.fhi, NU // TILES + 1)
                STT(out=eblo[:, :], in0=bank[2][0:2 * E, 0:P], scalar=WS, in1=ebhi[:, :], op0=ALU.mult,
                    op1=ALU.subtract).then_inc(S0.flo, 1)

            def moments(chain, c, first, p, sem, source=None):
                for t in range(TILES):
                    tile = X[:, bass.ds((c - first) * CH + t * P, P)] if source is None else source[:, t * P:(t + 1) * P]
                    last = dve.bn_stats(stats[:, p, t, :], tile)
                chain.link(last, wait_apart)
                for t in range(TILES):
                    last = dve.bn_aggr(meanvar[:, p, t, :], stats[:, p, t, :])
                last.then_inc(sem, 1)

            def add_to_x(c, first, in0, scalar, sem):
                xc = X[:, bass.ds((c - first) * CH, CH)]
                STT(out=xc, in0=in0, scalar=scalar, in1=xc, op0=ALU.mult, op1=ALU.add).then_inc(sem, 1)

            def ffn0(S, first):
                chain = Chain(dve, S.chain, 1)

                def step(i, p, lead, mid, lag):
                    if lead:
                        chain.at(i + 1)
                        moments(chain, i + 1, first, 1 - p, S.stats)
                        chain.close()
                    if mid:
                        for j in range(HB):
                            u = (HB * p + j) % 2
                            dve.wait_ge(S.sg, HB * i + j + 1)
                            after(dve, S.hlo, HB * i + j - 1)
                            STT(out=f0.h[:, u, :], in0=bank[3 + u][:, :], scalar=QSCALE, in1=f0.sg[:, u, :],
                                op0=ALU.mult, op1=ALU.mult).then_inc(S.h, 1)
                    if lead:
                        dve.wait_ge(S.xhi, i + 2)
                        TT(f0.xlo[:, 1 - p, :], bank[0][:, :], f0.xhi[:, 1 - p, :], ALU.subtract)\
                            .then_inc(S.xlo, 1)
                    if lag:
                        dve.wait_ge(S.down, i)
                        add_to_x(i - 1, first, bank[6 - p][:, :], 0.5 * QSCALE, S.x)
                pipeline(dve, first, NCH, step)

            def mixing(S, first):
                chain = Chain(dve, S.chain, 1)
                own = Chain(dve, S.own, 7)
                w, u, mix = wneg[:, 0:1], tvec[:, 1:2], lambda n: tvec[:, 2 + n:3 + n]
                dve.memset(tm.XN[:, 0:1], 0.0)
                dve.memset(tm.PM[:, 0:1], FAR)
                dve.memset(tm.SA[:, 0:1], 0.0)
                dve.memset(tm.SB[:, 0:1], 0.0).then_inc(S.init, 1)
                dve.wait_ge(S.init, 1)
                dve.memset(spare[:, 1:2], 0.0).then_inc(S.x, CREDIT)

                def step(i, p, lead, mid, lag):
                    o = p * CH
                    if mid:
                        own.at(i)
                    if lead:
                        chain.at(i + 1)
                        moments(chain, i + 1, first, 1 - p, S.stats)
                        chain.close()
                    if mid:
                        k, v = bank[2 + 3 * p - 1][:, :], bank[2 + 3 * p][:, :]
                        before, now = slice(o, o + CH), slice(o + 1, o + 1 + CH)
                        dve.wait_ge(S.kv, 3 * i + 1)
                        own.link(dve.tensor_tensor_scan(tm.PM[:, now], w.to_broadcast([P, CH]), k,
                                                        tm.PM[:, o:o + 1] if p else FAR, ALU.add, ALU.max))
                        STT(out=tm.q, in0=k, scalar=u, in1=tm.PM[:, before], op0=ALU.add, op1=ALU.max)\
                            .then_inc(S.arg_q, 1)
                        STT(out=tm.arg[:, 0, :], in0=tm.PM[:, before], scalar=w, in1=tm.PM[:, now], op0=ALU.add,
                            op1=ALU.subtract).then_inc(S.args, 1)
                        TT(tm.arg[:, 1, :], k, tm.PM[:, now], ALU.subtract).then_inc(S.args, 1)
                        dve.wait_ge(S.arg_q, i + 1)
                        STT(out=tm.arg[:, 3, :], in0=k, scalar=u, in1=tm.q, op0=ALU.add, op1=ALU.subtract)\
                            .then_inc(S.args, 1)
                    if lag:
                        dve.wait_ge(S.out, i)
                        add_to_x(i - 1, first, bank[7][:, :], -1.0, S.x)
                    if mid:
                        dve.wait_ge(S.kv, 3 * i + 2)
                        dve.wait_ge(S.ex, 4 * i + 2)
                        own.link(TT(tm.f2v, tm.ex[:, 1, :], v, ALU.mult))
                        dve.tensor_tensor_scan(tm.SB[:, now], tm.ex[:, 0, :], tm.ex[:, 1, :],
                                               tm.SB[:, o:o + 1] if p else 0.0, ALU.mult, ALU.add)\
                           .then_inc(S.scans, 1)
                        dve.tensor_tensor_scan(tm.SA[:, now], tm.ex[:, 0, :], tm.f2v,
                                               tm.SA[:, o:o + 1] if p else 0.0, ALU.mult, ALU.add)\
                           .then_inc(S.scans, 1)
                        dve.wait_ge(S.ex, 4 * i + 3)
                        own.link(TT(tm.e2v, tm.ex[:, 3, :], v, ALU.mult))
                    if lead:
                        n = (1 - p) * CH
                        dve.wait_ge(S.d, i + 2)
                        for m, dst in enumerate((tm.xk, tm.xv, tm.xr)):
                            after(dve, S.kv, 3 * i + m + 1)
                            STT(out=dst, in0=tm.D, scalar=mix(m), in1=tm.XN[:, n:n + CH], op0=ALU.mult,
                                op1=ALU.add).then_inc(S.xkvr, 1)
                    if mid:
                        dve.wait_ge(S.n12, 2 * i + 2)
                        TT(tm.den, tm.n2, tm.ex[:, 3, :], ALU.add).then_inc(S.den, 1)
                        own.link(TT(tm.num, tm.n1, tm.e2v, ALU.add))
                        dve.wait_ge(S.dex, 2 * i + 2)
                        dve.wait_ge(S.den, i + 1)
                        own.link(TT(tm.t, tm.den, tm.r0, ALU.mult))
                        own.link(STT(out=tm.t, in0=tm.t, scalar=2.0, in1=tm.r0, op0=ALU.subtract, op1=ALU.mult))
                        own.link(TT(tm.num, tm.num, tm.t, ALU.mult))
                        dve.wait_ge(S.sr, i + 1)
                        own.close()
                        TT(tm.y[:, p, :], tm.num, tm.sr, ALU.mult).then_inc(S.y, 1)
                pipeline(dve, first, NCH, step)

            def experts(S, first):
                chain = Chain(dve, S.chain, 2)
                own = Chain(dve, S.own, 12)

                def step(i, p, lead, mid, lag):
                    n = 1 - p
                    for u in range(NU):
                        if lead and u == 0:
                            chain.at(i + 1)
                            moments(chain, i + 1, first, n, S.stats)
                        if mid:
                            dve.wait_ge(S.gelu, NU * i + u + 1)
                            dve.wait_ge(S.wb, E * i + u // EB + 1)
                            after(dve, S.hlo, NU * i + u - 3)
                            TT(mo.hw[:, u % 4, :], mo.hf[:, u % 4, :], bank[3 + (u // EB) % 2][:, :], ALU.mult)\
                                .then_inc(S.hw, 1)
                        if lag and u == 4:
                            dve.wait_ge(S.mm2, NU * i)
                            STT(out=mo.dm[:, n, :], in0=bank[5][:, :], scalar=1.0 / WS, in1=mo.ab[:, n, :],
                                op0=ALU.mult, op1=ALU.subtract).then_inc(S.dm, 1)
                        if lead and u == 3:
                            dve.wait_ge(S.z, i + 2)
                            moments(chain, i + 1, first, n, S.stats2, mo.z1[:, n, :])
                            chain.close()
                            add_to_x(i + 1, first, mo.z1[:, n, :], 0.5, S.zadd)
                        if lag and u == 7:
                            dve.wait_ge(S.abT, i)
                            dve.wait_ge(S.zadd, i)
                            add_to_x(i - 1, first, bank[6][:, :], 0.5, S.r2)
                        if lead and u == 8:
                            dve.wait_ge(S.xn, i + 2)
                            dve.tensor_copy(mo.xhi[:, n, :], mo.xn).then_inc(S.xhi, 1)
                            dve.wait_ge(S.xhi, i + 2)
                            TT(mo.xlo[:, n, :], mo.xn, mo.xhi[:, n, :], ALU.subtract).then_inc(S.xlo, 1)
                        if lag and u == 8:
                            dve.wait_ge(S.tg, i)
                            TS(mo.gq, mo.tg, 0.25, 0.25, ALU.mult, ALU.add).then_inc(S.gq, 1)
                        if lead and u == 10:
                            own.at(i + 1)
                            dve.wait_ge(S.logits, i + 2)
                            own.link(TT(mo.lgs, bank[7][:, 0:TILES * E].rearrange("p (t e) -> p t e", e=E),
                                        gate_b4[:, :, :], ALU.add), wait_apart)
                            for t in range(TILES):
                                last = dve.max(mo.top[:, t, :], mo.lgs[:, t, :])
                            own.link(last)
                            TT(mo.dtop.rearrange("p (t o) -> p t o", o=1), mo.top[:, :, 0:1], mo.top[:, :, 1:2],
                               ALU.subtract).then_inc(S.dtop, 1)
                            for t in range(TILES):
                                last = dve.max_index(mo.topi[:, t, :], mo.top[:, t, :], mo.lgs[:, t, :])
                            own.link(last)
                            own.link(dve.tensor_copy(mo.topf, mo.topi))
                            for m in range(2):
                                own.link(TT(mo.eq[:, m, :, :], iota8[:, :, :],
                                            mo.topf[:, :, m:m + 1].to_broadcast([P, TILES, E]), ALU.is_equal))
                        if lag and u == 11:
                            dve.wait_ge(S.dmT, i)
                            dve.wait_ge(S.gq, i)
                            own_m = TT(mo.m.rearrange("p (t c) -> p t c", c=P),
                                       bank[6][:, :].rearrange("p (t c) -> p t c", c=P),
                                       mo.gq.rearrange("p (t o) -> p t o", o=1).to_broadcast([P, TILES, P]),
                                       ALU.mult)
                            own_m.then_inc(S.m, 1)
                            dve.wait_ge(S.m, i)
                            dve.wait_ge(S.r2, i)
                            add_to_x(i - 1, first, mo.m, 1.0, S.x)
                        if lead and u == 12:
                            dve.wait_ge(S.th, i + 2)
                            own.link(TS(mo.w12[:, 0, :], mo.th, 0.5, 0.5, ALU.mult, ALU.add))
                            own.link(TS(mo.w12[:, 1, :], mo.th, -0.5, 0.5, ALU.mult, ALU.add))
                            for m in range(2):
                                wm = mo.w12[:, m, :].rearrange("p (t o) -> p t o", o=1)
                                own.link(TT(mo.eq[:, m, :, :], mo.eq[:, m, :, :],
                                            wm.to_broadcast([P, TILES, E]), ALU.mult))
                            own.link(TT(mo.wd, mo.eq[:, 0, :, :], mo.eq[:, 1, :, :], ALU.add))
                            own.link(dve.tensor_copy(mo.wp[:, :, 0:E], mo.wd))
                            own.close()
                            TT(mo.wp[:, :, E:2 * E], mo.wd, mo.wp[:, :, 0:E], ALU.subtract).then_inc(S.wpair, 1)
                        if lead and u == 14:
                            dve.wait_ge(S.wpT, i + 2)
                            dve.tensor_copy(mo.wT[:, n, :], bank[7][0:2 * E, 0:CH // 2].bitcast(F16))\
                               .then_inc(S.wT, 1)
                pipeline(dve, first, NCH, step)

            def flow(S, first):
                chain = Chain(dve, S.chain, 1)
                own = Chain(dve, S.own, 13)
                dve.wait_ge(S0.nrm, 1)
                dve.reciprocal(fl.INV, fl.NRM).then_inc(S.inv, 1)
                dve.wait_ge(S.inv, 1)
                for n, sem in enumerate((S.x, S.kv, S.out)):
                    dve.memset(spare[:, 1 + n:2 + n], 0.0).then_inc(sem, CREDIT)
                scan = dve.tensor_tensor_scan

                def running(buffer, values, p, start):
                    return scan(buffer, onecol[:, 0:1].to_broadcast([P, CH]), values,
                                buffer[:, CH - 1:CH] if p else start, ALU.mult, ALU.add)

                def step(i, p, lead, mid, lag):
                    n = 1 - p

                    def turn(o):
                        g = HD * (i - 1) + o
                        if o == 0:
                            dve.wait_ge(S.kcqq, 2 * i)
                        dve.wait_ge(S.v, g + 1)
                        STT(out=fl.kv[:, o % 2, :], in0=bank[5 + o % 2][:, :], scalar=bvR[:, o:o + 1],
                            in1=fl.kc[:, n, :], op0=ALU.add, op1=ALU.mult).then_inc(S.kv, 1)
                        dve.wait_ge(S.kv, g + 1 + CREDIT)
                        scan(fl.S[:, o, :], onecol[:, 0:1].to_broadcast([P, CH]), fl.kv[:, o % 2, :],
                             fl.S[:, o, CH - 1:CH] if n else 0.0, ALU.mult, ALU.add).then_inc(S.s, 1)

                    if lag:
                        turn(0)
                        turn(1)
                    if mid:
                        own.at(i)
                        dve.wait_ge(S.sig, 2 * i + 2)
                        running(fl.Ck, fl.k, p, FLOW_EPS)
                        own.link(running(fl.Cq, fl.q, p, FLOW_EPS))
                        STT(out=fl.pr[:, 0, :], in0=fl.q, scalar=FLOW_EPS, in1=fl.Ck, op0=ALU.add,
                            op1=ALU.mult).then_inc(S.pr, 1)
                        STT(out=fl.pr[:, 1, :], in0=fl.k, scalar=FLOW_EPS, in1=fl.Cq, op0=ALU.add,
                            op1=ALU.mult).then_inc(S.pr, 1)
                    if lead:
                        chain.at(i + 1)
                        moments(chain, i + 1, first, n, S.stats)
                        chain.close()
                    if mid:
                        for m in range(2):
                            dve.wait_ge(S.lnr, 4 * i + 3 + m)
                            own.link(TT(fl.t, bank[3 + m][:, :], fl.r[:, m, :], ALU.mult))
                            own.link(STT(out=fl.rd[:, m, :], in0=fl.t, scalar=2.0, in1=fl.r[:, m, :],
                                         op0=ALU.subtract, op1=ALU.mult))
                        dve.wait_ge(S.nqk, 2 * i + 2)
                        for m, (nx, cum) in enumerate(((fl.NK, fl.Cks), (fl.NQ, fl.Cqs))):
                            own.link(TT(fl.ks, nx, fl.rd[:, 1 - m, :], ALU.mult))
                            own.link(running(cum, fl.ks, p, -FLOW_EPS))
                        for m, (x, cum) in enumerate(((fl.q, fl.Cks), (fl.k, fl.Cqs))):
                            STT(out=fl.pr[:, m, :], in0=x, scalar=FLOW_EPS, in1=cum, op0=ALU.add,
                                op1=ALU.mult).then_inc(S.pr, 1)
                    if lag:
                        turn(2)
                        turn(3)
                    if mid:
                        for m in range(2):
                            dve.wait_ge(S.den, 4 * i + 3 + m)
                            TT(fl.c[:, m, :], bank[3 + m][:, :], fl.INV[:, p, :], ALU.mult).then_inc(S.c12, 1)
                    if lag:
                        turn(4)
                        turn(5)
                    if mid:
                        dve.wait_ge(S.sa_cs, 2 * i + 2)
                        own.link(running(fl.Cc, fl.cs, p, 0.0))
                        own.link(dve.reciprocal(fl.rc, fl.Cc))
                        own.link(TT(fl.m1, fl.cs, fl.rc, ALU.mult))
                        own.link(TT(fl.qr, fl.q, fl.rd[:, 0, :], ALU.mult))
                        TT(fl.kc[:, p, :], fl.m1, fl.NK, ALU.mult).then_inc(S.kcqq, 1)
                        STT(out=fl.qq[:, p, :], in0=fl.qr, scalar=-1.0, in1=fl.sa, op0=ALU.mult, op1=ALU.mult)\
                            .then_inc(S.kcqq, 1)
                        own.close()
                    if lag:
                        turn(6)
                        turn(7)
                        dve.wait_ge(S.out, HD * i + CREDIT)
                        add_to_x(i - 1, first, bank[7][:, :], 1.0, S.x)
                pipeline(dve, first, NCH, step)

            setup()
            stages(dve, ffn0, mixing, experts, flow)

        @block.tensor
        def _(pe):
            mm, tr = pe.matmul, pe.transpose

            def three(dst, whi, wlo, xhi, xlo, start=True, stop=True):
                mm(dst, whi, xhi, start=start, stop=False, skip_group_check=True)
                mm(dst, whi, xlo, start=False, stop=False, skip_group_check=True)
                return mm(dst, wlo, xhi, start=False, stop=stop, skip_group_check=True)

            def setup():
                pe.wait_ge(S0.consts, N_CONST)
                pe.wait_ge(S0.cast, 1)
                for k in range(3):
                    for j in range(HB):
                        last = tr(bank[k][:, j * P:(j + 1) * P], sm.wf[:, k, j * P:(j + 1) * P], ident[:, :])
                    last.then_inc(S0.trf, 1)
                pe.wait_ge(S0.w_attn0, 16 * 9)
                for k in range(4):
                    last = tr(bank[3][:, k * P:(k + 1) * P], sm.wa[:, k, :], ident[:, :])
                last.then_inc(S0.trw, 1)
                pe.wait_ge(S0.g, 1)
                for r in range(NROT):
                    last = tr(bank[6][:, r * P:(r + 1) * P], sm.G[:, r, :], ident[:, :])
                last.then_inc(S0.gtp, 1)
                pe.wait_ge(S0.gt, 1)
                for n in range(TAYLOR - 1):
                    pe.wait_ge(S0.rot, n + 1)
                    for r in range(NROT):
                        last = mm(bank[6][:, r * P:(r + 1) * P], sm.GT[:, r, :], sm.rot[:, r, :], start=True,
                                  stop=True)
                    last.then_inc(S0.hp, 1)
                pe.wait_ge(S0.rot, TAYLOR)
                for r in range(NROT):
                    last = tr(bank[7][:, r * P:(r + 1) * P], sm.rot[:, r, :], ident[:, :])
                last.then_inc(S0.rtp, 1)
                with pe.Fori(0, SQUARINGS) as i:
                    pe.wait_ge(S0.pair, i + 1)
                    for r in range(NROT):
                        mm(bank[6][:, r * P:(r + 1) * P], sm.rotT[:, r, :], sm.rot[:, r, :], start=True, stop=True)
                    for r in range(NROT):
                        last = mm(bank[7][:, r * P:(r + 1) * P], sm.rot[:, r, :], sm.rotT[:, r, :], start=True,
                                  stop=True)
                    last.then_inc(S0.loop_pe, 1)
                pe.wait_ge(S0.pair, SQUARINGS + 1)
                mm(bank[6][:, 0:P], sm.rot[:, 1, :], sm.rotT[:, 0, :], start=True, stop=True).then_inc(S0.mtp, 1)
                pe.wait_ge(S0.mt, 1)
                mm(bank[7][:, 0:P], sm.MT, sm.rot[:, 2, :], start=True, stop=True).then_inc(S0.rp, 1)
                pe.wait_ge(S0.w_moe, 16 * N_MOE)
                tr(bank[4][:, 0:E], sm.eb2, ident[0:E, 0:E]).then_inc(S0.small, 1)
                mm(bank[5][:, 0:E], ones[:, :], gate_b[:, :], start=True, stop=True)
                mm(bank[5][:, E:E + 1], ones[:, :], gcb[:, :], start=True, stop=True).then_inc(S0.small2, 1)
                pe.wait_ge(S0.r, 1)
                for g in range(NU // TILES):
                    after(pe, S0.fT, g)
                    for n in range(TILES):
                        last = tr(bank[0][:, n * P:(n + 1) * P], sm.ew2[:, TILES * g + n, :], ident[:, :])
                    last.then_inc(S0.ft, 1)
                    pe.wait_ge(S0.fT, g + 1)
                    after(pe, S0.flo, g)
                    for n in range(TILES):
                        last = mm(bank[1][:, n * P:(n + 1) * P], sm.blkT[:, n, :], sm.R, start=True, stop=True)
                    last.then_inc(S0.fm, 1)
                pe.wait_ge(S0.eb2T, 2)
                mm(bank[2][0:2 * E, 0:P], sm.eb2T.rearrange("p a b -> p (a b)"), sm.R, start=True, stop=True)\
                    .then_inc(S0.fm, 1)

            def turn_chunk(z, zp, sem_z, value, sem_out):
                pe.wait_ge(sem_z, value)
                for t in range(TILES):
                    last = tr(bank[0][:, t * P:(t + 1) * P], z[:, zp, t * P:(t + 1) * P], ident[:, :])
                last.then_inc(sem_out, 1)

            def ffn0(S, first):
                def step(i, p, lead, mid, lag):
                    if mid:
                        pe.wait_ge(S.xlo, i + 1)
                        for j in range(HB):
                            b = (HB * p + j) % 2
                            after(pe, S.h, HB * i + j - 1)
                            cols = slice(j * P, (j + 1) * P)
                            for k, dst in ((0, bank[1 + b]), (1, bank[3 + b])):
                                last = three(dst[:, :], f0hi[:, k, cols], f0lo[:, k, cols], f0.xhi[:, p, :],
                                             f0.xlo[:, p, :])
                            last.then_inc(S.gu, 1)
                            if lead and j == 0:
                                turn_chunk(f0.z, 1 - p, S.z, i + 2, S.tr)
                    elif lead:
                        turn_chunk(f0.z, 1 - p, S.z, i + 2, S.tr)
                    if lag:
                        pe.wait_ge(S.hlo, HB * i)
                        for t in range(TILES):
                            for j in range(HB):
                                u = HB * (1 - p) + j
                                tok = slice(t * P, (t + 1) * P)
                                w = slice(j * P, (j + 1) * P)
                                last = three(bank[6 - p][:, tok], f0.hhi[:, u, tok], f0.hlo[:, u, tok],
                                             f0hi[:, 2, w], f0lo[:, 2, w], start=(j == 0), stop=(j == HB - 1))
                        last.then_inc(S.down, 1)
                pipeline(pe, first, NCH, step)

            def mixing(S, first):
                def step(i, p, lead, mid, lag):
                    if mid:
                        for m, x in enumerate((tm.xk, tm.xv, tm.xr)):
                            pe.wait_ge(S.xkvr, 3 * i + m + 1)
                            mm(bank[1 + 3 * p + m][:, :], waT[:, m, :], x, start=True, stop=True)\
                                .then_inc(S.kv, 1)
                    if lag:
                        pe.wait_ge(S.y, i)
                        after(pe, S.x, i - 1 + CREDIT)
                        for t in range(TILES):
                            tok = slice(t * P, (t + 1) * P)
                            last = mm(bank[7][:, tok], tm.y[:, 1 - p, tok], waT[:, 3, :], start=True, stop=True)
                        last.then_inc(S.out, 1)
                    if lead:
                        turn_chunk(tm.z, 1 - p, S.z, i + 2, S.tr)
                pipeline(pe, first, NCH, step)

            def experts(S, first):
                def step(i, p, lead, mid, lag):
                    n = 1 - p

                    def second(c, cp, u):
                        pe.wait_ge(S.hlo, NU * c + u + 1)
                        if u == 0:
                            after(pe, S.dm, c)
                            mm(bank[5][:, :], ebhi[:, :], mo.wT[:, cp, :], start=True, stop=False,
                               skip_group_check=True)
                            mm(bank[5][:, :], eblo[:, :], mo.wT[:, cp, :], start=False, stop=False,
                               skip_group_check=True)
                        three(bank[5][:, :], ew2hi[:, u, :], ew2lo[:, u, :], mo.hhi[:, u % 8, :],
                              mo.hlo[:, u % 8, :], start=False, stop=(u == NU - 1)).then_inc(S.mm2, 1)

                    for u in range(NU):
                        if mid:
                            if u == 0:
                                pe.wait_ge(S.xlo, i + 1)
                            if u % EB == 0:
                                e = u // EB
                                if e == 0:
                                    pe.wait_ge(S.wT, i + 1)
                                after(pe, S.hw, NU * i + EB * (e - 1))
                                mm(bank[3 + e % 2][:, :], sel[:, e, :], mo.wT[:, p, :], start=True, stop=True)\
                                    .then_inc(S.wb, 1)
                            after(pe, S.gelu, NU * i + u - 1)
                            three(bank[1 + u % 2][:, :], ew1hi[:, u, :], ew1lo[:, u, :], mo.xhi[:, p, :],
                                  mo.xlo[:, p, :]).then_inc(S.mm1, 1)
                        if lag and u < SKEW - 1:
                            for v in range(NU - SKEW + u, NU - SKEW + u + (2 if u == SKEW - 2 else 1)):
                                second(i - 1, n, v)
                        if mid and u >= SKEW:
                            second(i, p, u - SKEW)
                        if lag and u == 6:
                            pe.wait_ge(S.dm, i)
                            for t in range(TILES):
                                tok = slice(t * P, (t + 1) * P)
                                mm(bank[7][:, t:t + 1], mo.ab[:, n, tok], gc12[:, :], start=True, stop=False)
                                last = mm(bank[7][:, t:t + 1], mo.dm[:, n, tok], gcw[:, 1:2], start=False,
                                          stop=True)
                            last.then_inc(S.gate, 1)
                            for t in range(TILES):
                                tok = slice(t * P, (t + 1) * P)
                                last = tr(bank[6][:, tok], mo.ab[:, n, tok], ident[:, :])
                            last.then_inc(S.abT, 1)
                        if lead and u == 6:
                            turn_chunk(mo.z2, n, S.z2, i + 2, S.tr)
                        if lead and u == 9:
                            pe.wait_ge(S.xn, i + 2)
                            after(pe, S.tg, i)
                            after(pe, S.abel, i + 1)
                            for t in range(TILES):
                                last = mm(bank[7][:, t * E:(t + 1) * E], mo.xn[:, t * P:(t + 1) * P], gate_w[:, :],
                                          start=True, stop=True)
                            last.then_inc(S.logits, 1)
                        if lag and u == 10:
                            pe.wait_ge(S.r2, i)
                            for t in range(TILES):
                                tok = slice(t * P, (t + 1) * P)
                                last = tr(bank[6][:, tok], mo.dm[:, n, tok], ident[:, :])
                            last.then_inc(S.dmT, 1)
                        if lead and u == 13:
                            pe.wait_ge(S.wpair, i + 2)
                            turned = bank[7][0:2 * E, 0:CH // 2].bitcast(F16)
                            for t in range(TILES):
                                last = tr(turned[:, t * P:(t + 1) * P], mo.wp[:, t, :], ident16[:, :])
                            last.then_inc(S.wpT, 1)
                        if lead and u == NU - 1:
                            pe.wait_ge(S.wT, i + 2)
                            pe.wait_ge(S.xlo, i + 2)
                            three(bank[7][:, :], abhi[:, :], ablo[:, :], mo.xhi[:, n, :], mo.xlo[:, n, :])\
                                .then_inc(S.abel_mm, 1)
                pipeline(pe, first, NCH, step)

            def flow(S, first):
                def step(i, p, lead, mid, lag):
                    def turned_v(o):
                        after(pe, S.kv, HD * (i - 1) + max(o - 1, 0) + CREDIT)
                        mm(bank[5 + o % 2][:, :], WvR[:, o, :], fl.xn[:, 1 - p, :], start=True, stop=True)\
                            .then_inc(S.v, 1)

                    def project(o):
                        pe.wait_ge(S.pd, HD * (i - 1) + o + 1)
                        if o == 0:
                            after(pe, S.x, i - 1 + CREDIT)
                        for t in range(TILES):
                            tok = slice(t * P, (t + 1) * P)
                            if o == 0:
                                mm(bank[7][:, tok], ones[:, :], bo[:, :], start=(t == 0), stop=False,
                                   skip_group_check=True)
                            last = mm(bank[7][:, tok], fl.pd[:, o % 4, tok], WoR[:, o, :], start=False,
                                      stop=(o == HD - 1), skip_group_check=True)
                        last.then_inc(S.out, 1)

                    def sums(first, count):
                        for m in range(2):
                            pe.wait_ge(S.pr, count + m)
                            mm(bank[3 + m][:, :], blockones[:, :], fl.pr[:, m, :], start=True, stop=True)\
                                .then_inc(S.den, 1)
                    if lag:
                        turned_v(0)
                        turned_v(1)
                    if mid:
                        pe.wait_ge(S.xn, i + 1)
                        after(pe, S.sig, 2 * i)
                        for m in range(2):
                            mm(bank[1 + m][:, :], fw[:, m, :], fl.xn[:, p, :], start=True, stop=True)\
                                .then_inc(S.qk, 1)
                        sums(0, 4 * i + 1)
                    if lag:
                        for o in (2, 3):
                            turned_v(o)
                        project(0)
                    if lead:
                        turn_chunk(fl.z, 1 - p, S.z, i + 2, S.tr)
                    if mid:
                        sums(1, 4 * i + 3)
                    if lag:
                        for o in range(4, HD):
                            turned_v(o)
                            project(o - 3)
                        for o in range(HD - 3, HD):
                            project(o)
                pipeline(pe, first, NCH, step)

            setup()
            stages(pe, ffn0, mixing, experts, flow)


_INS = ["L0_attn_x", "L0_attn_time_decay", "L0_attn_time_first", "L0_attn_time_mix_k", "L0_attn_time_mix_v",
        "L0_attn_time_mix_r", "L0_attn_Wk", "L0_attn_Wv", "L0_attn_Wr", "L0_attn_Wo", "L0_ffn_w_gate",
        "L0_ffn_w_up", "L0_ffn_w_down", "L1_attn_Wq", "L1_attn_bq", "L1_attn_Wk", "L1_attn_bk", "L1_attn_Wv",
        "L1_attn_bv", "L1_attn_Wo", "L1_attn_bo", "L1_ffn_ln_gamma", "L1_ffn_ln_beta", "L1_ffn_abel_w",
        "L1_ffn_abel_b", "L1_ffn_moe_gate_w", "L1_ffn_moe_gate_b", "L1_ffn_ew1", "L1_ffn_eb1", "L1_ffn_ew2",
        "L1_ffn_eb2", "L1_ffn_gens", "L1_ffn_gc_w", "L1_ffn_gc_b"]


def kernel(**inputs):
    import numpy as _np
    import concourse.bacc as _bacc
    from concourse import mybir as _mybir
    from concourse.bass_utils import run_bass_kernel_spmd as _run

    nc = _bacc.Bacc("TRN2", target_bir_lowering=False, num_devices=1)
    arrays, args = {}, {}
    for name in _INS:
        a = _np.ascontiguousarray(inputs[name])
        arrays[f"in_{name}_dram"] = a
        args[name] = nc.dram_tensor(f"in_{name}_dram", a.shape, _mybir.dt.from_np(a.dtype), kind="ExternalInput").ap()
    shape = tuple(inputs["L0_attn_x"].shape)
    out = nc.dram_tensor("out_0_dram", shape, _mybir.dt.float32, kind="ExternalOutput").ap()
    macaron_kernel(nc, args, out)
    r = _run(nc, [arrays], core_ids=[0])
    return r.results[0]["out_0_dram"]
```

```python
from contextlib import ExitStack

import concourse.bass as bass
from concourse import mybir

ALU = mybir.AluOpType
ACT = mybir.ActivationFunctionType
F32 = mybir.dt.float32
F16 = mybir.dt.float16
I32 = mybir.dt.int32
U32 = mybir.dt.uint32
AX = mybir.AxisListType
RMAX = bass.bass_isa.ReduceOp.max

P = 128
TILES = 4
CH = P * TILES
LN_EPS = 1e-5
FLOW_EPS = 1e-6
QSCALE = 1.0 / 127.0
WS = 64.0
TAYLOR = 10
SQUARINGS = 16
HEADS = 16
HD = P // HEADS
SKEW = 5
MM1_BANK = (0, 1, 2, 0, 1, 2, 0, 1, 2, 0, 1, 2, 0, 1, 2, 1)
FAR = -1e38


def bank_free(u):
    before = [v for v in range(u) if MM1_BANK[v] == MM1_BANK[u]]
    if before:
        return before[-1] + 1
    return 1 + max(v for v, b in enumerate(MM1_BANK) if b == MM1_BANK[u]) - len(MM1_BANK)


def after(eng, sem, count):
    if isinstance(count, int) and count <= 0:
        return
    eng.wait_ge(sem, count)


class Buffers:
    pass


class Semaphores:
    pass


class Chain:

    def __init__(self, eng, sem, per_chunk=0):
        self.eng, self.sem, self.per_chunk = eng, sem, per_chunk
        self.base = self.n = 0

    def at(self, chunk):
        self.base, self.n = self.per_chunk * chunk, 0

    def link(self, instruction, wait=None):
        instruction.then_inc(self.sem, 1)
        self.n += 1
        if wait:
            wait(self.eng, self.sem, self.base + self.n)
        else:
            self.eng.wait_ge(self.sem, self.base + self.n)

    def close(self):
        assert self.n == self.per_chunk, (self.n, self.per_chunk)


def pipeline(eng, first, chunks, step):
    step(first - 1, 1, True, False, False)
    step(first, 0, True, True, False)
    with eng.Fori(0, (chunks - 2) // 2) as m:
        step(2 * m + (first + 1), 1, True, True, True)
        step(2 * m + (first + 2), 0, True, True, True)
    step(first + chunks - 1, 1, False, True, True)
    step(first + chunks, 0, False, False, True)


class Arena:

    def __init__(self, whole):
        self.whole, self.used = whole, 0

    def take(self, dims, dt=F32, parts=P):
        n = 1
        for d in dims:
            n *= d
        words = n if dt != F16 else n // 2
        view = self.whole[0:parts, self.used:self.used + words]
        self.used += words
        assert self.used <= self.whole.shape[1], self.used
        if dt != F32:
            view = view.bitcast(dt)
        if len(dims) == 2:
            view = view.rearrange("p (a b) -> p a b", a=dims[0])
        if len(dims) == 3:
            view = view.rearrange("p (a b c) -> p a b c", a=dims[0], b=dims[1])
        return view


def macaron_kernel(nc, ins, out):
    B, T, C = ins["L0_attn_x"].shape
    TOK = B * T
    NCH = TOK // CH
    NT = TOK // P
    HB = ins["L0_ffn_w_gate"].shape[0] // P
    E, _, EH = ins["L1_ffn_ew1"].shape
    EB = EH // P
    NU = E * EB
    NROT = ins["L1_ffn_gens"].shape[0]
    assert C == P and T == 2 * CH and NCH % 2 == 0 and NU % 8 == 0 and HB == 3

    ctx = ExitStack()
    with ctx:
        ctx.enter_context(nc.allow_non_contiguous_dma(reason="small vectors and permuted rows of weights"))

        def sb(name, shape, dt=F32):
            return ctx.enter_context(nc.sbuf_tensor(name, shape, dt))

        def sem(name):
            return ctx.enter_context(nc.semaphore(name))

        bank = [ctx.enter_context(nc.psum_tensor(f"bank{i}", [P, CH], F32)) for i in range(8)]
        X = sb("X", [P, NT * P])
        ident = sb("ident", [P, P])
        ident16 = sb("ident16", [P, P], F16)
        neghalf = sb("neghalf", [P, NT])
        eps = sb("eps", [P, NT])
        spare = sb("spare", [P, 4])
        pool_spare = sb("pool_spare", [P, 1])
        stats = sb("stats", [P, NT, 6])
        var = sb("var", [P, NT])
        nmean = sb("nmean", [P, NT])
        veps = sb("veps", [P, NT])
        rstd = sb("rstd", [P, NT])
        nbias = sb("nbias", [P, NT])
        r2 = sb("r2", [P, NT])
        v2 = sb("v2", [P, NT])
        rr = sb("rr", [P, NT])
        nbias2 = sb("nbias2", [P, NT])
        keep = sb("keep", [P, NT])
        shift = sb("shift", [P, NT])
        f0hi = sb("f0hi", [P, 3, HB * P], F16)
        f0lo = sb("f0lo", [P, 3, HB * P], F16)
        ew1hi = sb("ew1hi", [P, NU, P], F16)
        ew1lo = sb("ew1lo", [P, NU, P], F16)
        ew2hi = sb("ew2hi", [P, NU, P], F16)
        ew2lo = sb("ew2lo", [P, NU, P], F16)
        abhi = sb("abhi", [P, P], F16)
        ablo = sb("ablo", [P, P], F16)
        ebhi = sb("ebhi", [2 * E, P], F16)
        eblo = sb("eblo", [2 * E, P], F16)
        sel = sb("sel", [2 * E, E, P], F16)
        gamma = sb("gamma", [P, 1])
        beta = sb("beta", [P, 1])
        abel_b = sb("abel_b", [P, 1])
        eb1 = sb("eb1", [P, NU])
        gate_w = sb("gate_w", [P, E])
        gate_b = sb("gate_b", [1, E])
        gate_b4 = sb("gate_b4", [P, TILES, E])
        gcw = sb("gcw", [P, 2])
        gcb = sb("gcb", [1, 1])
        gcbh = sb("gcbh", [P, 1])
        gc12w = sb("gc12w", [P, P])
        gc2w = sb("gc2w", [P, P])
        ones = sb("ones", [1, P])
        iota8 = sb("iota8", [P, TILES, E])
        waT = sb("waT", [P, 4, P])
        tvec = sb("tvec", [P, 5])
        wneg = sb("wneg", [P, 1])
        fw = sb("fw", [P, 4, P])
        WoR = sb("WoR", [P, HD, P])
        WvR = sb("WvR", [P, HD, P])
        bvR = sb("bvR", [P, HD])
        fb = sb("fb", [P, 2])
        bo = sb("bo", [1, P])
        blockones = sb("blockones", [P, P])
        zcol = sb("zcol", [P, 1])
        onecol = sb("onecol", [P, 1])
        arena = sb("arena", [P, 32500])

        a = Arena(arena)
        sm = Buffers()
        sm.wi = a.take([3, HB * P], I32)
        sm.wf = a.take([3, HB * P])
        sm.wa = a.take([4, P])
        sm.ew1 = a.take([NU, P])
        sm.ew2 = a.take([NU, P])
        sm.ab = a.take([P])
        sm.eb2 = a.take([P], parts=E)
        sm.eb2T = a.take([2, E])
        sm.G = a.take([NROT, P])
        sm.Gabs = a.take([NROT, P])
        sm.GT = a.take([NROT, P])
        sm.rot = a.take([NROT, P])
        sm.rotT = a.take([NROT, P])
        sm.ident3 = a.take([NROT, P])
        sm.mask = a.take([NROT, P])
        sm.thr = a.take([NROT, SQUARINGS])
        sm.cneg = a.take([NROT, SQUARINGS])
        sm.active = a.take([NROT, SQUARINGS])
        sm.shrink = a.take([NROT, SQUARINGS])
        sm.rowsum = a.take([NROT])
        sm.norm = a.take([NROT])
        sm.factor = a.take([NROT])
        sm.MT = a.take([P])
        sm.R = a.take([P])
        sm.blkT = a.take([TILES, P])
        a = Arena(arena)
        f0 = Buffers()
        f0.z = a.take([2, CH])
        f0.xhi = a.take([2, CH], F16)
        f0.xlo = a.take([2, CH], F16)
        f0.sg = a.take([2, CH])
        f0.h = a.take([2, CH])
        f0.hhi = a.take([2 * HB, CH], F16)
        f0.hlo = a.take([2 * HB, CH], F16)
        f0.y = a.take([CH])
        a = Arena(arena)
        tm = Buffers()
        tm.z = a.take([2, CH])
        tm.XN = a.take([1 + 2 * CH])
        tm.D = a.take([CH])
        tm.xk = a.take([CH])
        tm.xv = a.take([CH])
        tm.xr = a.take([CH])
        tm.PM = a.take([1 + 2 * CH])
        tm.SA = a.take([1 + 2 * CH])
        tm.SB = a.take([1 + 2 * CH])
        tm.arg = a.take([4, CH])
        tm.ex = a.take([4, CH])
        tm.q = a.take([CH])
        tm.f2v = a.take([CH])
        tm.e2v = a.take([CH])
        tm.n1 = a.take([CH])
        tm.n2 = a.take([CH])
        tm.num = a.take([CH])
        tm.den = a.take([CH])
        tm.lnd = a.take([CH])
        tm.r0 = a.take([CH])
        tm.t = a.take([CH])
        tm.sr = a.take([CH])
        tm.y = a.take([2, CH])
        a = Arena(arena)
        mo = Buffers()
        mo.z2 = a.take([2, CH])
        mo.xn = a.take([CH])
        mo.xhi = a.take([2, CH], F16)
        mo.xlo = a.take([2, CH], F16)
        mo.hf = a.take([4, CH])
        mo.hw = a.take([4, CH])
        mo.hhi = a.take([8, CH], F16)
        mo.hlo = a.take([8, CH], F16)
        mo.ab = a.take([2, CH])
        mo.dm = a.take([CH])
        mo.r = a.take([CH])
        mo.m = a.take([CH])
        mo.lgs = a.take([TILES, E])
        mo.top = a.take([TILES, E])
        mo.topi = a.take([TILES, E], U32)
        mo.topf = a.take([TILES, E])
        mo.dtop = a.take([TILES])
        mo.th = a.take([TILES])
        mo.w12 = a.take([2, TILES])
        mo.eq = a.take([2, TILES, E])
        mo.wd = a.take([TILES, E])
        mo.wp = a.take([TILES, 2 * E], F16)
        mo.wT = a.take([2, CH], F16, parts=2 * E)
        mo.tg = a.take([CH])
        a = Arena(arena)
        fl = Buffers()
        fl.NRM = a.take([2, CH])
        fl.INV = a.take([2, CH])
        fl.z = a.take([2, CH])
        fl.xn = a.take([2, CH])
        fl.q = a.take([2, CH])
        fl.k = a.take([2, CH])
        fl.NQ = a.take([CH])
        fl.NK = a.take([CH])
        fl.Ck = a.take([CH])
        fl.Cq = a.take([CH])
        fl.Cks = a.take([CH])
        fl.Cqs = a.take([CH])
        fl.Cc = a.take([CH])
        fl.pr = a.take([2, CH])
        fl.lnd = a.take([3, CH])
        fl.r = a.take([3, CH])
        fl.t = a.take([3, CH])
        fl.xv = a.take([2, CH])
        fl.rd = a.take([3, CH])
        fl.ks = a.take([2, CH])
        fl.c = a.take([2, CH])
        fl.sa = a.take([CH])
        fl.cs = a.take([CH])
        fl.csnk = a.take([CH])
        fl.kc = a.take([2, CH])
        fl.qr = a.take([CH])
        fl.qq = a.take([2, CH])
        fl.kv = a.take([2, CH])
        fl.S = a.take([HD, CH])
        fl.pd = a.take([4, CH])

        S0 = Semaphores()
        S0.x_first = sem("setup_x_first")
        S0.x_rest = sem("setup_x_rest")
        S0.w_ffn0 = sem("setup_w_ffn0")
        S0.w_attn0 = sem("setup_w_attn0")
        S0.w_moe = sem("setup_w_moe")
        S0.w_gens = sem("setup_w_gens")
        S0.w_flow = sem("setup_w_flow")
        S0.consts = sem("setup_consts")
        S0.dve = sem("setup_dve")
        S0.act = sem("setup_act")
        S0.pool = sem("setup_pool")
        S0.loop_pe = sem("setup_loop_pe")
        S0.pair = sem("setup_pair")
        S0.loop_mask = sem("setup_loop_mask")
        S0.norm = sem("setup_norm")
        S0.cast = sem("setup_cast")
        S0.gabs = sem("setup_gabs")
        S0.rowsum = sem("setup_rowsum")
        S0.trf = sem("setup_trf")
        S0.f0hi = sem("setup_f0hi")
        S0.f0lo = sem("setup_f0lo")
        S0.trw = sem("setup_trw")
        S0.decay = sem("setup_decay")
        S0.e1hi = sem("setup_e1hi")
        S0.small = sem("setup_small")
        S0.small2 = sem("setup_small2")
        S0.eb2T = sem("setup_eb2T")
        S0.g = sem("setup_g")
        S0.gtp = sem("setup_gtp")
        S0.gt = sem("setup_gt")
        S0.rot = sem("setup_rot")
        S0.hp = sem("setup_hp")
        S0.rtp = sem("setup_rtp")
        S0.mtp = sem("setup_mtp")
        S0.mt = sem("setup_mt")
        S0.rp = sem("setup_rp")
        S0.r = sem("setup_r")
        S0.ft = sem("setup_ft")
        S0.fT = sem("setup_fT")
        S0.fm = sem("setup_fm")
        S0.fhi = sem("setup_fhi")
        S0.flo = sem("setup_flo")
        S0.nrm = sem("setup_nrm")
        LN = Semaphores()
        LN.var = sem("norm_var")
        LN.dve = sem("norm_dve")
        LN.pool = sem("norm_pool")
        LN.rstd = sem("norm_rstd")
        LN.bn = sem("norm_bn")
        FF = Semaphores()
        FF.z = sem("ffn_z")
        FF.tr = sem("ffn_tr")
        FF.x = sem("ffn_x")
        FF.xhi = sem("ffn_xhi")
        FF.xlo = sem("ffn_xlo")
        FF.gu = sem("ffn_gu")
        FF.sg = sem("ffn_sg")
        FF.h = sem("ffn_h")
        FF.hhi = sem("ffn_hhi")
        FF.hlo = sem("ffn_hlo")
        FF.down_mm = sem("ffn_down_mm")
        FF.y = sem("ffn_y")
        FF.down = sem("ffn_down")
        TM = Semaphores()
        TM.z = sem("mix_z")
        TM.tr = sem("mix_tr")
        TM.x = sem("mix_x")
        TM.init = sem("mix_init")
        TM.own = sem("mix_own")
        TM.xn = sem("mix_xn")
        TM.d = sem("mix_d")
        TM.xkvr = sem("mix_xkvr")
        TM.kv = sem("mix_kv")
        TM.arg_q = sem("mix_arg_q")
        TM.arg3 = sem("mix_arg3")
        TM.args = sem("mix_args")
        TM.ex = sem("mix_ex")
        TM.dex = sem("mix_dex")
        TM.sr = sem("mix_sr")
        TM.den = sem("mix_den")
        TM.scans = sem("mix_scans")
        TM.n12 = sem("mix_n12")
        TM.y = sem("mix_y")
        TM.out = sem("mix_out")
        MO = Semaphores()
        MO.z = sem("moe_z")
        MO.tr = sem("moe_tr")
        MO.x = sem("moe_x")
        MO.own = sem("moe_own")
        MO.xhi = sem("moe_xhi")
        MO.xlo = sem("moe_xlo")
        MO.xn = sem("moe_xn")
        MO.logits = sem("moe_logits")
        MO.dtop = sem("moe_dtop")
        MO.th = sem("moe_th")
        MO.wpair = sem("moe_wpair")
        MO.wpT = sem("moe_wpT")
        MO.wT = sem("moe_wT")
        MO.abel_mm = sem("moe_abel_mm")
        MO.abel = sem("moe_abel")
        MO.mm1 = sem("moe_mm1")
        MO.gelu = sem("moe_gelu")
        MO.wb = sem("moe_wb")
        MO.hw = sem("moe_hw")
        MO.hhi = sem("moe_hhi")
        MO.hlo = sem("moe_hlo")
        MO.mm2 = sem("moe_mm2")
        MO.dm = sem("moe_dm")
        MO.gate = sem("moe_gate")
        MO.tg = sem("moe_tg")
        MO.zadd = sem("moe_zadd")
        MO.m = sem("moe_m")
        MO.r = sem("moe_r")
        MO.rT = sem("moe_rT")
        FL = Semaphores()
        FL.z = sem("flow_z")
        FL.tr = sem("flow_tr")
        FL.x = sem("flow_x")
        FL.own = sem("flow_own")
        FL.inv = sem("flow_inv")
        FL.xn = sem("flow_xn")
        FL.qk = sem("flow_qk")
        FL.sig = sem("flow_sig")
        FL.nqk = sem("flow_nqk")
        FL.pr = sem("flow_pr")
        FL.den = sem("flow_den")
        FL.lnr = sem("flow_lnr")
        FL.sa = sem("flow_sa")
        FL.cs = sem("flow_cs")
        FL.cc = sem("flow_cc")
        FL.lnc = sem("flow_lnc")
        FL.rd = sem("flow_rd")
        FL.qr = sem("flow_qr")
        FL.qq = sem("flow_qq")
        FL.csnk = sem("flow_csnk")
        FL.xv = sem("flow_xv")
        FL.c12 = sem("flow_c12")
        FL.kcqq = sem("flow_kcqq")
        FL.v = sem("flow_v")
        FL.kv = sem("flow_kv")
        FL.s = sem("flow_s")
        FL.pd = sem("flow_pd")
        FL.out = sem("flow_out")
        N_CONST = 10
        N_MOE = 13
        N_FLOW = 4 + 2 + 1 + 2 * (2 * HD - 1)

        CREDIT = 1

        def wait_apart(eng, sem, count):
            eng.wait_ge(sem, count)
            eng.memset(spare[:, 0:1], 0.0)

        def stages(eng, ffn0, mixing, experts, flow):
            eng.wait_ge(S0.consts, N_CONST)
            eng.wait_ge(S0.flo, NU // TILES + 1)
            eng.wait_ge(S0.x_first, 16)
            eng.wait_ge(S0.x_rest, 16 * (NCH - 1))
            ffn0(FF, 0, 1)
            eng.wait_ge(FF.x, NCH + CREDIT)
            mixing(TM, 0, 2)
            eng.wait_ge(TM.x, NCH + CREDIT)
            ffn0(FF, NCH, 3)
            eng.wait_ge(FF.x, 2 * NCH + CREDIT)
            experts(MO, 0, 4)
            eng.wait_ge(MO.x, NCH)
            flow(FL, 0, 5)
            eng.wait_ge(FL.x, NCH + CREDIT)
            experts(MO, NCH, 6)
        stored = ctx.enter_context(nc.semaphore("stored"))

        x_tiles = ins["L0_attn_x"].rearrange("b (t p) c -> p (b t) c", p=P)
        out_tiles = out.rearrange("b (t p) c -> p (b t) c", p=P)
        X3 = X[:, :].rearrange("p (t c) -> p t c", c=P)

        block = ctx.enter_context(nc.Block())

        @block.sync
        def _(sp):
            sp.dma_start(X3[:, 0:TILES, :], x_tiles[:, 0:TILES, :]).then_inc(S0.x_first, 16)
            for k, name in enumerate(("gate", "up")):
                sp.dma_start(sm.wi[:, k, :].rearrange("p (j d) -> p j d", d=P),
                             ins[f"L0_ffn_w_{name}"].rearrange("(j p) d -> p j d", p=P)).then_inc(S0.w_ffn0, 16)
            sp.dma_start(sm.wi[:, 2, :], ins["L0_ffn_w_down"]).then_inc(S0.w_ffn0, 16)
            sp.dma_start(sm.G, ins["L1_ffn_gens"].rearrange("r p c -> p r c")).then_inc(S0.w_gens, 16)
            for k, name in enumerate(("Wk", "Wv", "Wr", "Wo")):
                sp.dma_start(sm.wa[:, k, :], ins[f"L0_attn_{name}"]).then_inc(S0.w_attn0, 16)
            for k, name in enumerate(("time_decay", "time_first", "time_mix_k", "time_mix_v", "time_mix_r")):
                sp.dma_start(tvec[:, k:k + 1], ins[f"L0_attn_{name}"].rearrange("a b c -> c (a b)"))\
                  .then_inc(S0.w_attn0, 16)
            for c in range(1, NCH):
                sp.dma_start(X3[:, c * TILES:(c + 1) * TILES, :], x_tiles[:, c * TILES:(c + 1) * TILES, :])\
                  .then_inc(S0.x_rest, 16)
            ew2_rows = ins["L1_ffn_ew2"].rearrange("e (j p) d -> p (e j) d", p=P)
            moe_loads = [
                (sm.ew1.rearrange("p (e j) n -> p e (j n)", j=EB), ins["L1_ffn_ew1"].rearrange("e c h -> c e h")),
                (sm.ew2[:, 0:NU // 2, :], ew2_rows[:, 0:NU // 2, :]),
                (sm.ew2[:, NU // 2:NU, :], ew2_rows[:, NU // 2:NU, :]),
                (sm.ab, ins["L1_ffn_abel_w"]),
                (sm.eb2, ins["L1_ffn_eb2"]),
                (gamma[:, :], ins["L1_ffn_ln_gamma"].rearrange("(c o) -> c o", o=1)),
                (beta[:, :], ins["L1_ffn_ln_beta"].rearrange("(c o) -> c o", o=1)),
                (abel_b[:, :], ins["L1_ffn_abel_b"].rearrange("(c o) -> c o", o=1)),
                (eb1[:, :], ins["L1_ffn_eb1"].rearrange("e (j p) -> p (e j)", p=P)),
                (gate_w[:, :], ins["L1_ffn_moe_gate_w"]),
                (gate_b[:, :], ins["L1_ffn_moe_gate_b"].rearrange("(o e) -> o e", o=1)),
                (gcw[:, :], ins["L1_ffn_gc_w"].rearrange("(a p) o -> p (a o)", p=P)),
                (gcb[:, :], ins["L1_ffn_gc_b"].rearrange("(o e) -> o e", o=1)),
            ]
            assert len(moe_loads) == N_MOE
            for dst, src in moe_loads:
                sp.dma_start(dst, src).then_inc(S0.w_moe, 16)
            for k, name in enumerate(("Wq", "Wk", "Wv", "Wo")):
                sp.dma_start(fw[:, k, :], ins[f"L1_attn_{name}"]).then_inc(S0.w_flow, 16)
            for k, name in enumerate(("bq", "bk")):
                sp.dma_start(fb[:, k:k + 1], ins[f"L1_attn_{name}"].rearrange("(c o) -> c o", o=1))\
                  .then_inc(S0.w_flow, 16)
            sp.dma_start(bo[:, :], ins["L1_attn_bo"].rearrange("(o c) -> o c", o=1)).then_inc(S0.w_flow, 16)
            wo_rows = ins["L1_attn_Wo"].rearrange("(h m) n -> h m n", m=HD)
            bv_rows = ins["L1_attn_bv"].rearrange("(h m) -> h m", m=HD)
            for d in range(HD):
                sp.dma_start(WoR[d:P:HD, 0:HD - d, :], wo_rows[:, d:HD, :]).then_inc(S0.w_flow, 16)
                sp.dma_start(bvR[d:P:HD, 0:HD - d], bv_rows[:, d:HD]).then_inc(S0.w_flow, 16)
                if d:
                    sp.dma_start(WoR[d:P:HD, HD - d:HD, :], wo_rows[:, 0:d, :]).then_inc(S0.w_flow, 16)
                    sp.dma_start(bvR[d:P:HD, HD - d:HD], bv_rows[:, 0:d]).then_inc(S0.w_flow, 16)
            with sp.Fori(0, NCH) as c:
                sp.wait_ge(MO.x, c + (NCH + 1))
                sp.dma_start(out_tiles[:, bass.ds(c * TILES, TILES), :],
                             X3[:, bass.ds(c * TILES, TILES), :]).then_inc(stored, 16)
            sp.wait_ge(stored, 16 * NCH)

        @block.gpsimd
        def _(pool):

            def setup():
                pool.memset(ident[:, :], 0.0).then_inc(S0.pool, 1)
                pool.memset(ident16[:, :], 0.0).then_inc(S0.pool, 1)
                pool.memset(sm.ident3, 0.0).then_inc(S0.pool, 1)
                pool.memset(sel[:, :, :], 0.0).then_inc(S0.pool, 1)
                pool.memset(blockones[:, :], 1.0).then_inc(S0.pool, 1)
                pool.memset(neghalf[:, :], -0.5).then_inc(S0.consts, 1)
                pool.memset(eps[:, :], LN_EPS).then_inc(S0.consts, 1)
                pool.memset(ones[:, :], 1.0).then_inc(S0.consts, 1)
                pool.memset(onecol[:, :], 1.0).then_inc(S0.consts, 1)
                pool.iota(iota8[:, :, :], [[0, TILES], [1, E]], base=0, channel_multiplier=0,
                          allow_small_or_imprecise_dtypes=True).then_inc(S0.consts, 1)
                pool.wait_ge(S0.pool, 5)
                pool.affine_select(out=sel[:, :, :], in_=sel[:, :, :], compare_op=ALU.not_equal, fill=1.0, base=0,
                                   pattern=[[-1, E], [0, P]], channel_multiplier=1).then_inc(S0.pool, 1)
                pool.affine_select(out=blockones[:, :], in_=blockones[:, :], compare_op=ALU.is_ge, fill=0.0,
                                   base=0, pattern=[[-HD, HEADS], [0, HD]], channel_multiplier=1)\
                    .then_inc(S0.pool, 1)
                for m in (ident[:, :], ident16[:, :]):
                    pool.affine_select(out=m, in_=m, compare_op=ALU.not_equal, fill=1.0, base=0,
                                       pattern=[[-1, P]], channel_multiplier=1).then_inc(S0.consts, 1)
                pool.affine_select(out=sm.ident3, in_=sm.ident3, compare_op=ALU.not_equal, fill=1.0, base=0,
                                   pattern=[[0, NROT], [-1, P]], channel_multiplier=1).then_inc(S0.consts, 1)
                pool.wait_ge(S0.pool, 7)
                pool.affine_select(out=sel[:, :, :], in_=sel[:, :, :], compare_op=ALU.not_equal, fill=1.0, base=-E,
                                   pattern=[[-1, E], [0, P]], channel_multiplier=1).then_inc(S0.consts, 1)
                pool.affine_select(out=blockones[:, :], in_=blockones[:, :], compare_op=ALU.is_ge, fill=0.0,
                                   base=HD - 1, pattern=[[HD, HEADS], [0, HD]], channel_multiplier=-1)\
                    .then_inc(S0.consts, 1)
                pool.wait_ge(S0.rowsum, 1)
                pool.partition_all_reduce(sm.norm, sm.rowsum, P, RMAX).then_inc(S0.norm, 1)

            norm_chain = Chain(pool, LN.pool)

            def norm(number, twice=False):
                def link(instruction):
                    norm_chain.link(instruction)

                pool.wait_ge(LN.var, number)
                for part in (slice(0, TILES), slice(TILES, NT)):
                    v, e, h = var[:, part], eps[:, part], neghalf[:, part]
                    link(pool.tensor_tensor(veps[:, part], v, e, ALU.add))
                    link(pool.tensor_tensor(rstd[:, part], veps[:, part], h, ALU.pow))
                    link(pool.tensor_tensor(nbias[:, part], nmean[:, part], rstd[:, part], ALU.mult))
                    if twice:
                        link(pool.tensor_tensor(r2[:, part], rstd[:, part], rstd[:, part], ALU.mult))
                        link(pool.tensor_tensor(r2[:, part], v, r2[:, part], ALU.mult))
                        link(pool.tensor_tensor(r2[:, part], r2[:, part], e, ALU.add))
                        link(pool.tensor_tensor(v2[:, part], r2[:, part], h, ALU.pow))
                        link(pool.tensor_tensor(rr[:, part], rstd[:, part], v2[:, part], ALU.mult))
                        link(pool.tensor_tensor(nbias2[:, part], nmean[:, part], rr[:, part], ALU.mult))
                        link(pool.tensor_scalar(keep[:, part], rstd[:, part], 0.5, 1.0, ALU.mult, ALU.add))
                        link(pool.tensor_scalar(shift[:, part], nbias[:, part], 0.5, None, ALU.mult))
                    pool.memset(pool_spare[:, :], 0.0).then_inc(LN.rstd, 1)

            def ffn0(S, first, number):
                norm(number)

                def step(i, p, lead, mid, lag):
                    if mid:
                        for j in range(HB):
                            u = HB * p + j
                            pool.wait_ge(S.hhi, HB * i + j + 1)
                            pool.tensor_tensor(f0.hlo[:, u, :], f0.h[:, u % 2, :], f0.hhi[:, u, :],
                                               ALU.subtract).then_inc(S.hlo, 1)
                pipeline(pool, first, NCH, step)

            def mixing(S, first, number):
                norm(number)
                pool.wait_ge(S.init, 1)

                def step(i, p, lead, mid, lag):
                    o = p * CH
                    if mid:
                        pool.wait_ge(S.arg_q, i + 1)
                        pool.tensor_tensor(tm.arg[:, 2, :], tm.PM[:, o:o + CH], tm.q, ALU.subtract)\
                            .then_inc(S.arg3, 1)
                    if lead:
                        n = (1 - p) * CH
                        pool.wait_ge(S.xn, i + 2)
                        pool.tensor_tensor(tm.D, tm.XN[:, 1 + n:1 + n + CH], tm.XN[:, n:n + CH],
                                           ALU.subtract).then_inc(S.d, 1)
                    if mid:
                        pool.wait_ge(S.ex, 4 * i + 4)
                        pool.wait_ge(S.scans, 2 * i + 2)
                        pool.tensor_tensor(tm.n1, tm.ex[:, 2, :], tm.SA[:, o:o + CH], ALU.mult)\
                            .then_inc(S.n12, 1)
                        pool.tensor_tensor(tm.n2, tm.ex[:, 2, :], tm.SB[:, o:o + CH], ALU.mult)\
                            .then_inc(S.n12, 1)
                pipeline(pool, first, NCH, step)

            def experts(S, first, number):
                norm(number, twice=True)

                def step(i, p, lead, mid, lag):
                    def low(u):
                        pool.wait_ge(S.hhi, NU * i + u + 1)
                        pool.tensor_tensor(mo.hlo[:, u % 8, :], mo.hw[:, u % 4, :], mo.hhi[:, u % 8, :],
                                           ALU.subtract).then_inc(S.hlo, 1)
                    for u in range(NU):
                        if mid:
                            low(u)
                pipeline(pool, first, NCH, step)

            def flow(S, first, number):
                norm(number)
                pool.iota(fl.NRM.rearrange("p a n -> p (a n)"), [[1, 2 * CH]], base=1, channel_multiplier=0,
                          allow_small_or_imprecise_dtypes=True).then_inc(S0.nrm, 1)
                pool.wait_ge(S0.nrm, 1)

                def step(i, p, lead, mid, lag):
                    def weigh(*turns):
                        for o in turns if lag else ():
                            pool.wait_ge(S.s, HD * (i - 1) + o + 1)
                            after(pool, S.out, HD * (i - 1) + max(o - 3, 0) + CREDIT)
                            pool.tensor_tensor(fl.pd[:, o % 4, :], fl.S[:, o, :], fl.qq[:, 1 - p, :],
                                               ALU.mult).then_inc(S.pd, 1)
                    if mid:
                        pool.wait_ge(S.sig, 2 * i + 2)
                        after(pool, S.csnk, i)
                        pool.tensor_tensor(fl.NK, fl.k[:, p, :], fl.NRM[:, p, :], ALU.mult).then_inc(S.nqk, 1)
                        pool.tensor_tensor(fl.NQ, fl.q[:, p, :], fl.NRM[:, p, :], ALU.mult).then_inc(S.nqk, 1)
                    if lag:
                        pool.wait_ge(S.qq, i)
                    weigh(0, 1, 2)
                    if mid:
                        pool.wait_ge(S.rd, 2 * i + 1)
                        pool.tensor_tensor(fl.qr, fl.q[:, p, :], fl.rd[:, 0, :], ALU.mult).then_inc(S.qr, 1)
                    weigh(3, 4)
                    if mid:
                        pool.wait_ge(S.cs, i + 1)
                        pool.tensor_tensor(fl.csnk, fl.cs, fl.NK, ALU.mult).then_inc(S.csnk, 1)
                    weigh(5, 6, 7)
                    if mid:
                        pool.wait_ge(S.sa, i + 1)
                        pool.wait_ge(S.qr, i + 1)
                        pool.tensor_tensor(fl.qq[:, p, :], fl.qr, fl.sa, ALU.mult).then_inc(S.qq, 1)
                pipeline(pool, first, NCH, step)

            setup()
            stages(pool, ffn0, mixing, experts, flow)

        @block.scalar
        def _(act):
            A = act.activation

            def setup():
                act.wait_ge(S0.w_gens, 16)
                A(sm.Gabs, sm.G, ACT.Abs).then_inc(S0.gabs, 1)
                for k in range(3):
                    act.wait_ge(S0.trf, k + 1)
                    A(f0hi[:, k, :], bank[k][:, 0:HB * P], ACT.Copy).then_inc(S0.f0hi, 1)
                act.wait_ge(S0.trw, 1)
                A(waT[:, :, :].rearrange("p a b -> p (a b)"), bank[3][:, :], ACT.Copy).then_inc(S0.act, 1)
                A(wneg[:, :], tvec[:, 0:1], ACT.Exp).then_inc(S0.decay, 1)
                act.wait_ge(S0.gtp, 1)
                A(sm.GT.rearrange("p a b -> p (a b)"), bank[6][:, 0:NROT * P], ACT.Copy).then_inc(S0.gt, 1)
                act.wait_ge(S0.w_moe, 16 * N_MOE)
                A(ew1hi[:, :, :], sm.ew1, ACT.Copy, scale=WS).then_inc(S0.e1hi, 1)
                A(abhi[:, :], sm.ab, ACT.Copy, scale=WS).then_inc(S0.e1hi, 1)
                act.wait_ge(S0.rtp, 1)
                A(sm.rotT.rearrange("p a b -> p (a b)"), bank[7][:, 0:NROT * P], ACT.Copy).then_inc(S0.pair, 1)
                act.wait_ge(S0.mtp, 1)
                A(sm.MT, bank[6][:, 0:P], ACT.Copy).then_inc(S0.mt, 1)
                act.wait_ge(S0.rp, 1)
                A(sm.R, bank[7][:, 0:P], ACT.Copy).then_inc(S0.r, 1)
                act.wait_ge(S0.small, 1)
                for n in range(2):
                    A(sm.eb2T[:, n, :], bank[4][:, 0:E], ACT.Copy).then_inc(S0.eb2T, 1)
                for g in range(NU // TILES):
                    act.wait_ge(S0.ft, g + 1)
                    A(sm.blkT.rearrange("p a b -> p (a b)"), bank[0][:, :], ACT.Copy).then_inc(S0.fT, 1)
                    act.wait_ge(S0.fm, g + 1)
                    A(ew2hi[:, TILES * g:TILES * g + TILES, :].rearrange("p a b -> p (a b)"), bank[1][:, :],
                      ACT.Copy, scale=WS).then_inc(S0.fhi, 1)
                act.wait_ge(S0.fm, NU // TILES + 1)
                A(ebhi[:, :], bank[2][0:2 * E, 0:P], ACT.Copy, scale=WS).then_inc(S0.fhi, 1)

            def normalise(z, zp, c, sem, first, number, scale, bias, tiles=range(TILES)):
                if tiles[0] == 0 and isinstance(c, int) and c < first + 2:
                    act.wait_ge(LN.rstd, 2 * number - (c == first))
                for t in tiles:
                    tile = (c - first) * TILES + t
                    last = A(z[:, zp, t * P:(t + 1) * P], X[:, bass.ds((c - first) * CH + t * P, P)], ACT.Identity,
                             bias=bias[:, bass.ds(tile, 1)], scale=scale[:, bass.ds(tile, 1)])
                if tiles[-1] == TILES - 1:
                    last.then_inc(sem, 1)

            def ffn0(S, first, number):
                def step(i, p, lead, mid, lag):
                    def low(j):
                        act.wait_ge(S.h, HB * i + j + 1)
                        A(f0.hhi[:, HB * p + j, :], f0.h[:, (HB * p + j) % 2, :], ACT.Copy).then_inc(S.hhi, 1)
                    for j in range(HB):
                        if mid:
                            act.wait_ge(S.gu, HB * i + j + 1)
                            A(f0.sg[:, (HB * p + j) % 2, :], bank[1 + (HB * p + j) % 2][:, :], ACT.Silu,
                              scale=QSCALE).then_inc(S.sg, 1)
                        if lead and j == 0:
                            normalise(f0.z, 1 - p, i + 1, S.z, first, number, rstd, nbias)
                        if mid and j:
                            low(j - 1)
                        if lag and j == 1:
                            act.wait_ge(S.down_mm, i)
                            A(f0.y, bank[5][:, :], ACT.Copy).then_inc(S.y, 1)
                    if lead:
                        act.wait_ge(S.tr, i + 2)
                        A(f0.xhi[:, 1 - p, :], bank[0][:, :], ACT.Copy).then_inc(S.xhi, 1)
                    if mid:
                        low(HB - 1)
                pipeline(act, first, NCH, step)

            def mixing(S, first, number):
                def step(i, p, lead, mid, lag):
                    if mid:
                        o = p * CH
                        act.wait_ge(S.args, 3 * i + 1)
                        A(tm.ex[:, 0, :], tm.arg[:, 0, :], ACT.Exp).then_inc(S.ex, 1)
                        act.wait_ge(S.args, 3 * i + 2)
                        A(tm.ex[:, 1, :], tm.arg[:, 1, :], ACT.Exp).then_inc(S.ex, 1)
                        act.wait_ge(S.args, 3 * i + 3)
                        A(tm.ex[:, 3, :], tm.arg[:, 3, :], ACT.Exp).then_inc(S.ex, 1)
                        act.wait_ge(S.arg3, i + 1)
                        A(tm.ex[:, 2, :], tm.arg[:, 2, :], ACT.Exp).then_inc(S.ex, 1)
                    if lead:
                        normalise(tm.z, 1 - p, i + 1, S.z, first, number, rstd, nbias)
                        act.wait_ge(S.tr, i + 2)
                        n = 1 + (1 - p) * CH
                        A(tm.XN[:, n:n + CH], bank[0][:, :], ACT.Copy).then_inc(S.xn, 1)
                    if mid:
                        act.wait_ge(S.kv, 3 * i + 3)
                        A(tm.sr, bank[3 + 3 * p][:, :], ACT.Sigmoid).then_inc(S.sr, 1)
                        act.wait_ge(S.den, i + 1)
                        A(tm.lnd, tm.den, ACT.Ln).then_inc(S.dex, 1)
                        act.wait_ge(S.dex, 2 * i + 1)
                        A(tm.r0, tm.lnd, ACT.Exp, scale=-1.0).then_inc(S.dex, 1)
                pipeline(act, first, NCH, step)

            def experts(S, first, number):
                def step(i, p, lead, mid, lag):
                    def high(c, u):
                        act.wait_ge(S.hw, NU * c + u + 1)
                        after(act, S.mm2, NU * c + u - 7)
                        A(mo.hhi[:, u % 8, :], mo.hw[:, u % 4, :], ACT.Copy).then_inc(S.hhi, 1)
                    for u in range(NU):
                        if mid:
                            act.wait_ge(S.mm1, NU * i + u + 1)
                            after(act, S.hw, NU * i + u - 3)
                            A(mo.hf[:, u % 4, :], bank[MM1_BANK[u]][:, :], ACT.Gelu, scale=1.0 / WS,
                              bias=eb1[:, u:u + 1]).then_inc(S.gelu, 1)
                            if u:
                                high(i, u - 1)
                        if lead and u < TILES:
                            normalise(mo.z2, 1 - p, i + 1, S.z, first, number, rr, nbias2, [u])
                        if lead and u == 6:
                            act.wait_ge(S.tr, i + 2)
                            A(mo.xn, bank[6][:, :], ACT.Identity, scale=gamma[:, :], bias=beta[:, :])\
                                .then_inc(S.xn, 1)
                        if lag and u == 9:
                            act.wait_ge(S.gate, i)
                            A(mo.tg, bank[6][:, :], ACT.Tanh, scale=0.5, bias=gcbh[:, :]).then_inc(S.tg, 1)
                        if lead and u == 10:
                            act.wait_ge(S.dtop, i + 2)
                            A(mo.th, mo.dtop, ACT.Tanh, scale=0.5).then_inc(S.th, 1)
                        if lead and u == NU - 1:
                            act.wait_ge(S.abel_mm, i + 2)
                            A(mo.ab[:, 1 - p, :], bank[6][:, :], ACT.Gelu, scale=1.0 / WS, bias=abel_b[:, :])\
                                .then_inc(S.abel, 1)
                    if mid:
                        high(i, NU - 1)
                pipeline(act, first, NCH, step)

            def flow(S, first, number):
                def step(i, p, lead, mid, lag):
                    n = 1 - p
                    if lead:
                        normalise(fl.z, n, i + 1, S.z, first, number, rstd, nbias)
                        act.wait_ge(S.tr, i + 2)
                        after(act, S.xv, i)
                        A(fl.xn[:, n, :], bank[0][:, :], ACT.Copy).then_inc(S.xn, 1)
                    if mid:
                        act.preload_act_table_set("natural_log_exp_and_others")
                        for m in range(2):
                            act.wait_ge(S.den, 4 * i + m + 1)
                            A(fl.lnd[:, m, :], bank[3 + m][:, :], ACT.Ln).then_inc(S.lnr, 1)
                        for m in range(2):
                            act.wait_ge(S.lnr, 4 * i + m + 1)
                            A(fl.r[:, m, :], fl.lnd[:, m, :], ACT.Exp, scale=-1.0).then_inc(S.lnr, 1)
                        A(fl.xv[:, p, :], fl.xn[:, p, :], ACT.Copy).then_inc(S.xv, 1)
                    if mid:
                        act.wait_ge(S.c12, 2 * i + 1)
                        A(fl.cs, fl.c[:, 1, :], ACT.Exp, scale=-1.0).then_inc(S.cs, 1)
                        act.wait_ge(S.cc, i + 1)
                        A(fl.lnd[:, 2, :], fl.Cc, ACT.Ln).then_inc(S.lnc, 1)
                        act.wait_ge(S.lnc, 2 * i + 1)
                        A(fl.r[:, 2, :], fl.lnd[:, 2, :], ACT.Exp, scale=-1.0).then_inc(S.lnc, 1)
                        act.wait_ge(S.c12, 2 * i + 2)
                        A(fl.sa, fl.c[:, 0, :], ACT.Sigmoid, scale=-1.0).then_inc(S.sa, 1)
                    if lead:
                        for m, dst in enumerate((fl.q, fl.k)):
                            act.wait_ge(S.qk, 2 * i + m + 3)
                            A(dst[:, n, :], bank[1 + m][:, :], ACT.Sigmoid, bias=fb[:, m:m + 1]).then_inc(S.sig, 1)
                pipeline(act, first, NCH, step)

            setup()
            stages(act, ffn0, mixing, experts, flow)

        @block.vector
        def _(dve):
            TS, TT, STT = dve.tensor_scalar, dve.tensor_tensor, dve.scalar_tensor_tensor
            flat = "p a b -> p (a b)"

            def setup():
                chain = Chain(dve, S0.dve)
                dve.wait_ge(S0.w_ffn0, 48)
                dve.tensor_copy(sm.wf, sm.wi).then_inc(S0.cast, 1)
                for i in range(SQUARINGS):
                    last = dve.memset(sm.thr[:, :, i:i + 1], float(2 ** i))
                chain.link(last)
                dve.wait_ge(S0.gabs, 1)
                dve.tensor_reduce(sm.rowsum, sm.Gabs, AX.X, ALU.add).then_inc(S0.rowsum, 1)
                chain.link(dve.reciprocal(sm.cneg.rearrange(flat), sm.thr.rearrange(flat)))
                chain.link(TS(sm.cneg.rearrange(flat), sm.cneg.rearrange(flat), 0.5, -1.0, ALU.mult, ALU.add))
                for k in range(3):
                    dve.wait_ge(S0.f0hi, k + 1)
                    TT(f0lo[:, k, :], bank[k][:, 0:HB * P], f0hi[:, k, :], ALU.subtract).then_inc(S0.f0lo, 1)
                dve.wait_ge(S0.norm, 1)
                for r in range(NROT):
                    last = TS(sm.active[:, r, :], sm.thr[:, r, :], sm.norm[:, r:r + 1], None, ALU.is_lt)
                chain.link(last)
                chain.link(TT(sm.shrink, sm.active, sm.cneg, ALU.mult))
                chain.link(TS(sm.shrink, sm.shrink, 1.0, None, ALU.add))
                chain.link(dve.tensor_reduce(sm.factor, sm.shrink, AX.X, ALU.min))
                for r in range(NROT):
                    last = TS(sm.G[:, r, :], sm.G[:, r, :], sm.factor[:, r:r + 1], None, ALU.mult)
                last.then_inc(S0.g, 1)
                dve.wait_ge(S0.g, 1)
                dve.wait_ge(S0.consts, N_CONST)
                STT(out=sm.rot, in0=sm.G, scalar=1.0 / TAYLOR, in1=sm.ident3, op0=ALU.mult, op1=ALU.add)\
                    .then_inc(S0.rot, 1)
                for n, k in enumerate(range(TAYLOR - 1, 0, -1)):
                    dve.wait_ge(S0.hp, n + 1)
                    STT(out=sm.rot.rearrange(flat), in0=bank[6][:, 0:NROT * P], scalar=1.0 / k,
                        in1=sm.ident3.rearrange(flat), op0=ALU.mult, op1=ALU.add).then_inc(S0.rot, 1)
                with dve.Fori(0, SQUARINGS) as i:
                    dve.wait_ge(S0.pair, i + 1)
                    for r in range(NROT):
                        last = dve.tensor_copy(sm.mask[:, r, :],
                                               sm.active[:, r, bass.ds(i, 1)].to_broadcast([P, P]))
                    last.then_inc(S0.loop_mask, 1)
                    dve.wait_ge(S0.loop_mask, i + 1)
                    wait_apart(dve, S0.loop_pe, i + 1)
                    bits = sm.mask.rearrange(flat).bitcast(I32)
                    dve.copy_predicated(sm.rot.rearrange(flat), bits, bank[6][:, 0:NROT * P])
                    dve.copy_predicated(sm.rotT.rearrange(flat), bits, bank[7][:, 0:NROT * P])\
                       .then_inc(S0.pair, 1)
                dve.wait_ge(S0.decay, 1)
                chain.link(TS(wneg[:, :], wneg[:, :], -1.0, None, ALU.mult))
                dve.wait_ge(S0.e1hi, 2)
                STT(out=ew1lo[:, :, :], in0=sm.ew1, scalar=WS, in1=ew1hi[:, :, :], op0=ALU.mult, op1=ALU.subtract)
                STT(out=ablo[:, :], in0=sm.ab, scalar=WS, in1=abhi[:, :], op0=ALU.mult, op1=ALU.subtract)
                TT(gc12w[:, :], gcw[:, 0:1].to_broadcast([P, P]), gcw[:, 1:2].to_broadcast([P, P]), ALU.add)
                dve.tensor_copy(gc2w[:, :], gcw[:, 1:2].to_broadcast([P, P]))
                dve.wait_ge(S0.small2, 1)
                for t in range(TILES):
                    dve.tensor_copy(gate_b4[:, t, :], bank[5][:, 0:E])
                TS(gcbh[:, :], bank[5][:, E:E + 1], 0.5, None, ALU.mult)
                dve.wait_ge(S0.w_flow, 16 * N_FLOW)
                wv = fw[:, 2, :].rearrange("p (h m) -> p h m", m=HD)
                for o in range(HD):
                    turned = WvR[:, o, :].rearrange("p (h d) -> p h d", d=HD)
                    last = dve.tensor_copy(turned[:, :, 0:HD - o], wv[:, :, o:HD])
                    if o:
                        last = dve.tensor_copy(turned[:, :, HD - o:HD], wv[:, :, 0:o])
                for g in range(NU // TILES):
                    dve.wait_ge(S0.fhi, g + 1)
                    STT(out=ew2lo[:, TILES * g:TILES * g + TILES, :].rearrange(flat), in0=bank[1][:, :], scalar=WS,
                        in1=ew2hi[:, TILES * g:TILES * g + TILES, :].rearrange(flat), op0=ALU.mult,
                        op1=ALU.subtract).then_inc(S0.flo, 1)
                dve.wait_ge(S0.fhi, NU // TILES + 1)
                STT(out=eblo[:, :], in0=bank[2][0:2 * E, 0:P], scalar=WS, in1=ebhi[:, :], op0=ALU.mult,
                    op1=ALU.subtract).then_inc(S0.flo, 1)

            def tile_stats(c):
                for t in range(TILES):
                    last = dve.bn_stats(stats[:, bass.ds(c * TILES + t, 1), :], X[:, bass.ds(c * CH + t * P, P)])
                last.then_inc(LN.bn, 1)

            norm_chain = Chain(dve, LN.dve)

            def variances(number):
                dve.wait_ge(LN.bn, NCH * number)
                col = lambda k: stats[:, :, k:k + 1].rearrange("p t o -> p (t o)")
                link = norm_chain.link
                TT(veps[:, :], col(1), col(4), ALU.subtract).then_inc(LN.dve, 1)
                TT(var[:, :], col(2), col(5), ALU.add).then_inc(LN.dve, 1)
                norm_chain.n += 2
                link(STT(out=nmean[:, :], in0=col(1), scalar=-1.0, in1=col(4), op0=ALU.mult, op1=ALU.subtract))
                TS(nmean[:, :], nmean[:, :], 0.5, None, ALU.mult).then_inc(LN.dve, 1)
                norm_chain.n += 1
                link(STT(out=veps[:, :], in0=veps[:, :], scalar=0.25, in1=veps[:, :], op0=ALU.mult, op1=ALU.mult))
                STT(out=var[:, :], in0=var[:, :], scalar=1.0 / P, in1=veps[:, :], op0=ALU.mult, op1=ALU.add)\
                    .then_inc(LN.var, 1)

            def add_to_x(c, first, in0, scalar, sem):
                xc = X[:, bass.ds((c - first) * CH, CH)]
                STT(out=xc, in0=in0, scalar=scalar, in1=xc, op0=ALU.mult, op1=ALU.add).then_inc(sem, 1)

            def finish_x(c, first, in0, scalar, sem, count):
                add_to_x(c, first, in0, scalar, sem)
                wait_apart(dve, sem, count)
                tile_stats(c - first)

            def ffn0(S, first, number):
                variances(number)
                if first == 0:
                    dve.memset(spare[:, 1:2], 0.0).then_inc(S.x, CREDIT)

                def step(i, p, lead, mid, lag):
                    if mid:
                        for j in range(HB):
                            u = (HB * p + j) % 2
                            dve.wait_ge(S.sg, HB * i + j + 1)
                            after(dve, S.hlo, HB * i + j - 1)
                            STT(out=f0.h[:, u, :], in0=bank[3 + u][:, :], scalar=QSCALE, in1=f0.sg[:, u, :],
                                op0=ALU.mult, op1=ALU.mult).then_inc(S.h, 1)
                    if lead:
                        dve.wait_ge(S.xhi, i + 2)
                        TT(f0.xlo[:, 1 - p, :], bank[0][:, :], f0.xhi[:, 1 - p, :], ALU.subtract)\
                            .then_inc(S.xlo, 1)
                    if lag:
                        dve.wait_ge(S.down, i)
                        finish_x(i - 1, first, bank[7][:, :], 0.5 * QSCALE, S.x, i + CREDIT)
                pipeline(dve, first, NCH, step)

            def mixing(S, first, number):
                variances(number)
                own = Chain(dve, S.own, 7)
                w, u, mix = wneg[:, 0:1], tvec[:, 1:2], lambda n: tvec[:, 2 + n:3 + n]
                dve.memset(tm.XN[:, 0:1], 0.0)
                dve.memset(tm.PM[:, 0:1], FAR)
                dve.memset(tm.SA[:, 0:1], 0.0)
                dve.memset(tm.SB[:, 0:1], 0.0).then_inc(S.init, 1)
                dve.wait_ge(S.init, 1)
                dve.memset(spare[:, 1:2], 0.0).then_inc(S.x, CREDIT)

                def step(i, p, lead, mid, lag):
                    o = p * CH
                    if mid:
                        own.at(i)
                    if mid:
                        k, v = bank[2 + 3 * p - 1][:, :], bank[2 + 3 * p][:, :]
                        before, now = slice(o, o + CH), slice(o + 1, o + 1 + CH)
                        dve.wait_ge(S.kv, 3 * i + 1)
                        own.link(dve.tensor_tensor_scan(tm.PM[:, now], w.to_broadcast([P, CH]), k,
                                                        tm.PM[:, o:o + 1] if p else FAR, ALU.add, ALU.max))
                        STT(out=tm.q, in0=k, scalar=u, in1=tm.PM[:, before], op0=ALU.add, op1=ALU.max)\
                            .then_inc(S.arg_q, 1)
                        STT(out=tm.arg[:, 0, :], in0=tm.PM[:, before], scalar=w, in1=tm.PM[:, now], op0=ALU.add,
                            op1=ALU.subtract).then_inc(S.args, 1)
                        TT(tm.arg[:, 1, :], k, tm.PM[:, now], ALU.subtract).then_inc(S.args, 1)
                        dve.wait_ge(S.arg_q, i + 1)
                        STT(out=tm.arg[:, 3, :], in0=k, scalar=u, in1=tm.q, op0=ALU.add, op1=ALU.subtract)\
                            .then_inc(S.args, 1)
                    if lag:
                        dve.wait_ge(S.out, i)
                        finish_x(i - 1, first, bank[7][:, :], -1.0, S.x, i + CREDIT)
                    if mid:
                        dve.wait_ge(S.kv, 3 * i + 2)
                        dve.wait_ge(S.ex, 4 * i + 2)
                        own.link(TT(tm.f2v, tm.ex[:, 1, :], v, ALU.mult))
                        dve.tensor_tensor_scan(tm.SB[:, now], tm.ex[:, 0, :], tm.ex[:, 1, :],
                                               tm.SB[:, o:o + 1] if p else 0.0, ALU.mult, ALU.add)\
                           .then_inc(S.scans, 1)
                        dve.tensor_tensor_scan(tm.SA[:, now], tm.ex[:, 0, :], tm.f2v,
                                               tm.SA[:, o:o + 1] if p else 0.0, ALU.mult, ALU.add)\
                           .then_inc(S.scans, 1)
                        dve.wait_ge(S.ex, 4 * i + 3)
                        own.link(TT(tm.e2v, tm.ex[:, 3, :], v, ALU.mult))
                    if lead:
                        n = (1 - p) * CH
                        dve.wait_ge(S.d, i + 2)
                        for m, dst in enumerate((tm.xk, tm.xv, tm.xr)):
                            after(dve, S.kv, 3 * i + m + 1)
                            STT(out=dst, in0=tm.D, scalar=mix(m), in1=tm.XN[:, n:n + CH], op0=ALU.mult,
                                op1=ALU.add).then_inc(S.xkvr, 1)
                    if mid:
                        dve.wait_ge(S.n12, 2 * i + 2)
                        TT(tm.den, tm.n2, tm.ex[:, 3, :], ALU.add).then_inc(S.den, 1)
                        own.link(TT(tm.num, tm.n1, tm.e2v, ALU.add))
                        dve.wait_ge(S.dex, 2 * i + 2)
                        dve.wait_ge(S.den, i + 1)
                        own.link(TT(tm.t, tm.den, tm.r0, ALU.mult))
                        own.link(STT(out=tm.t, in0=tm.t, scalar=2.0, in1=tm.r0, op0=ALU.subtract, op1=ALU.mult))
                        own.link(TT(tm.num, tm.num, tm.t, ALU.mult))
                        dve.wait_ge(S.sr, i + 1)
                        own.close()
                        TT(tm.y[:, p, :], tm.num, tm.sr, ALU.mult).then_inc(S.y, 1)
                pipeline(dve, first, NCH, step)

            def experts(S, first, number):
                variances(number)
                own = Chain(dve, S.own, 12)

                def step(i, p, lead, mid, lag):
                    n = 1 - p
                    for u in range(NU):
                        if lag and u == 4:
                            dve.wait_ge(S.mm2, NU * i)
                            STT(out=mo.dm, in0=bank[5][:, :], scalar=1.0 / WS, in1=mo.ab[:, n, :],
                                op0=ALU.mult, op1=ALU.subtract).then_inc(S.dm, 1)
                        if mid:
                            dve.wait_ge(S.gelu, NU * i + u + 1)
                            dve.wait_ge(S.wb, E * i + u // EB + 1)
                            after(dve, S.hlo, NU * i + u - 3)
                            TT(mo.hw[:, u % 4, :], mo.hf[:, u % 4, :], bank[3 + (u // EB) % 2][:, :], ALU.mult)\
                                .then_inc(S.hw, 1)
                        if lead and u == 6:
                            dve.wait_ge(S.xn, i + 2)
                            dve.tensor_copy(mo.xhi[:, n, :], mo.xn).then_inc(S.xhi, 1)
                            dve.wait_ge(S.xhi, i + 2)
                            TT(mo.xlo[:, n, :], mo.xn, mo.xhi[:, n, :], ALU.subtract).then_inc(S.xlo, 1)
                        if lead and u == 7:
                            dve.wait_ge(S.z, i + 2)
                            if isinstance(i, int) and i < first + 1:
                                dve.wait_ge(LN.rstd, 2 * number - (i + 1 == first))
                            for t in range(TILES):
                                tile = X[:, bass.ds((i + 1 - first) * CH + t * P, P)]
                                c = bass.ds((i + 1 - first) * TILES + t, 1)
                                last = TS(tile, tile, keep[:, c], shift[:, c], ALU.mult, ALU.add)
                            last.then_inc(S.zadd, 1)
                        if lag and u == 10:
                            dve.wait_ge(S.tg, i)
                            own_t = STT(out=mo.m, in0=mo.tg, scalar=1.0, in1=mo.dm, op0=ALU.add, op1=ALU.mult)
                            own_t.then_inc(S.m, 1)
                            dve.wait_ge(S.m, i)
                            STT(out=mo.r, in0=mo.m, scalar=0.5, in1=mo.ab[:, n, :], op0=ALU.mult, op1=ALU.add)\
                                .then_inc(S.r, 1)
                        if lead and u == 8:
                            own.at(i + 1)
                            dve.wait_ge(S.logits, i + 2)
                            own.link(TT(mo.lgs, bank[7][:, 0:TILES * E].rearrange("p (t e) -> p t e", e=E),
                                        gate_b4[:, :, :], ALU.add), wait_apart)
                            for t in range(TILES):
                                last = dve.max(mo.top[:, t, :], mo.lgs[:, t, :])
                            own.link(last)
                            TT(mo.dtop.rearrange("p (t o) -> p t o", o=1), mo.top[:, :, 0:1], mo.top[:, :, 1:2],
                               ALU.subtract).then_inc(S.dtop, 1)
                            for t in range(TILES):
                                last = dve.max_index(mo.topi[:, t, :], mo.top[:, t, :], mo.lgs[:, t, :])
                            own.link(last)
                            own.link(dve.tensor_copy(mo.topf, mo.topi))
                            for m in range(2):
                                own.link(TT(mo.eq[:, m, :, :], iota8[:, :, :],
                                            mo.topf[:, :, m:m + 1].to_broadcast([P, TILES, E]), ALU.is_equal))
                        if lead and u == 11:
                            dve.wait_ge(S.th, i + 2)
                            own.link(TS(mo.w12[:, 0, :], mo.th, 0.5, 0.5, ALU.mult, ALU.add))
                            own.link(TS(mo.w12[:, 1, :], mo.th, -0.5, 0.5, ALU.mult, ALU.add))
                            for m in range(2):
                                wm = mo.w12[:, m, :].rearrange("p (t o) -> p t o", o=1)
                                own.link(TT(mo.eq[:, m, :, :], mo.eq[:, m, :, :],
                                            wm.to_broadcast([P, TILES, E]), ALU.mult))
                            own.link(TT(mo.wd, mo.eq[:, 0, :, :], mo.eq[:, 1, :, :], ALU.add))
                            own.link(dve.tensor_copy(mo.wp[:, :, 0:E], mo.wd))
                            own.close()
                            TT(mo.wp[:, :, E:2 * E], mo.wd, mo.wp[:, :, 0:E], ALU.subtract).then_inc(S.wpair, 1)
                        if lag and u == 13:
                            dve.wait_ge(S.rT, i)
                            dve.wait_ge(S.zadd, i)
                            if first == 0:
                                finish_x(i - 1, first, bank[6][:, :], 0.5, S.x, i)
                            else:
                                add_to_x(i - 1, first, bank[6][:, :], 0.5, S.x)
                        if lead and u == 13:
                            dve.wait_ge(S.wpT, i + 2)
                            dve.tensor_copy(mo.wT[:, n, :], bank[7][0:2 * E, 0:CH // 2].bitcast(F16))\
                               .then_inc(S.wT, 1)
                pipeline(dve, first, NCH, step)

            def flow(S, first, number):
                variances(number)
                own = Chain(dve, S.own, 8)
                dve.wait_ge(S0.nrm, 1)
                dve.reciprocal(fl.INV, fl.NRM).then_inc(S.inv, 1)
                dve.wait_ge(S.inv, 1)
                for n, sem in enumerate((S.x, S.kv, S.out)):
                    dve.memset(spare[:, 1 + n:2 + n], 0.0).then_inc(sem, CREDIT)
                scan = dve.tensor_tensor_scan

                def running(buffer, values, p, start):
                    return scan(buffer, onecol[:, 0:1].to_broadcast([P, CH]), values,
                                buffer[:, CH - 1:CH] if p else start, ALU.mult, ALU.add)

                def step(i, p, lead, mid, lag):
                    n = 1 - p

                    def turn(*turns):
                        for o in turns if lag else ():
                            g = HD * (i - 1) + o
                            dve.wait_ge(S.v, g + 1)
                            STT(out=fl.kv[:, o % 2, :], in0=bank[5 + o % 2][:, :], scalar=bvR[:, o:o + 1],
                                in1=fl.kc[:, n, :], op0=ALU.add, op1=ALU.mult).then_inc(S.kv, 1)
                            dve.wait_ge(S.kv, g + 1 + CREDIT)
                            scan(fl.S[:, o, :], onecol[:, 0:1].to_broadcast([P, CH]), fl.kv[:, o % 2, :],
                                 fl.S[:, o, CH - 1:CH] if n else 0.0, ALU.mult, ALU.add).then_inc(S.s, 1)

                    def newton(m):
                        return STT(out=fl.rd[:, m, :], in0=fl.t[:, m, :], scalar=2.0, in1=fl.r[:, m, :],
                                   op0=ALU.subtract, op1=ALU.mult)

                    if lag:
                        dve.wait_ge(S.kcqq, i)
                    if mid:
                        own.at(i)
                        dve.wait_ge(S.sig, 2 * i + 2)
                        running(fl.Ck, fl.k[:, p, :], p, FLOW_EPS)
                        own.link(running(fl.Cq, fl.q[:, p, :], p, FLOW_EPS))
                        STT(out=fl.pr[:, 0, :], in0=fl.q[:, p, :], scalar=FLOW_EPS, in1=fl.Ck, op0=ALU.add,
                            op1=ALU.mult).then_inc(S.pr, 1)
                        STT(out=fl.pr[:, 1, :], in0=fl.k[:, p, :], scalar=FLOW_EPS, in1=fl.Cq, op0=ALU.add,
                            op1=ALU.mult).then_inc(S.pr, 1)
                    turn(0, 1, 2, 3)
                    if mid:
                        for m in range(2):
                            dve.wait_ge(S.lnr, 4 * i + 3 + m)
                            last = TT(fl.t[:, m, :], bank[3 + m][:, :], fl.r[:, m, :], ALU.mult)
                        own.link(last)
                        for m in range(2):
                            newton(m).then_inc(S.rd, 1)
                        dve.wait_ge(S.nqk, 2 * i + 2)
                        dve.wait_ge(S.rd, 2 * i + 2)
                        for m, (nx, cum) in enumerate(((fl.NK, fl.Cks), (fl.NQ, fl.Cqs))):
                            own.link(TT(fl.ks[:, m, :], nx, fl.rd[:, 1 - m, :], ALU.mult))
                            own.link(running(cum, fl.ks[:, m, :], p, -FLOW_EPS))
                        for m, (x, cum) in enumerate(((fl.q, fl.Cks), (fl.k, fl.Cqs))):
                            STT(out=fl.pr[:, m, :], in0=x[:, p, :], scalar=FLOW_EPS, in1=cum, op0=ALU.add,
                                op1=ALU.mult).then_inc(S.pr, 1)
                    turn(4, 5)
                    if mid:
                        for m in (1, 0):
                            dve.wait_ge(S.den, 4 * i + 3 + m)
                            TT(fl.c[:, m, :], bank[3 + m][:, :], fl.INV[:, p, :], ALU.mult).then_inc(S.c12, 1)
                    turn(6)
                    if mid:
                        dve.wait_ge(S.cs, i + 1)
                        running(fl.Cc, fl.cs, p, 0.0).then_inc(S.cc, 1)
                    turn(7)
                    if mid:
                        dve.wait_ge(S.lnc, 2 * i + 2)
                        dve.wait_ge(S.cc, i + 1)
                        own.link(TT(fl.t[:, 2, :], fl.Cc, fl.r[:, 2, :], ALU.mult))
                        own.link(newton(2))
                        dve.wait_ge(S.csnk, i + 1)
                        TT(fl.kc[:, p, :], fl.csnk, fl.rd[:, 2, :], ALU.mult).then_inc(S.kcqq, 1)
                        own.close()
                    if lag:
                        dve.wait_ge(S.out, HD * i + CREDIT)
                        finish_x(i - 1, first, bank[7][:, :], 1.0, S.x, i + CREDIT)
                pipeline(dve, first, NCH, step)

            setup()
            dve.wait_ge(S0.x_first, 16)
            dve.wait_ge(S0.x_rest, 16 * (NCH - 1))
            with dve.Fori(0, NCH) as c:
                tile_stats(c)
            stages(dve, ffn0, mixing, experts, flow)

        @block.tensor
        def _(pe):
            mm, tr = pe.matmul, pe.transpose

            def three(dst, whi, wlo, xhi, xlo, start=True, stop=True):
                mm(dst, whi, xhi, start=start, stop=False, skip_group_check=True)
                mm(dst, whi, xlo, start=False, stop=False, skip_group_check=True)
                return mm(dst, wlo, xhi, start=False, stop=stop, skip_group_check=True)

            def setup():
                pe.wait_ge(S0.consts, N_CONST)
                pe.wait_ge(S0.cast, 1)
                for k in range(3):
                    for j in range(HB):
                        last = tr(bank[k][:, j * P:(j + 1) * P], sm.wf[:, k, j * P:(j + 1) * P], ident[:, :])
                    last.then_inc(S0.trf, 1)
                pe.wait_ge(S0.w_attn0, 16 * 9)
                for k in range(4):
                    last = tr(bank[3][:, k * P:(k + 1) * P], sm.wa[:, k, :], ident[:, :])
                last.then_inc(S0.trw, 1)
                pe.wait_ge(S0.g, 1)
                for r in range(NROT):
                    last = tr(bank[6][:, r * P:(r + 1) * P], sm.G[:, r, :], ident[:, :])
                last.then_inc(S0.gtp, 1)
                pe.wait_ge(S0.gt, 1)
                for n in range(TAYLOR - 1):
                    pe.wait_ge(S0.rot, n + 1)
                    for r in range(NROT):
                        last = mm(bank[6][:, r * P:(r + 1) * P], sm.GT[:, r, :], sm.rot[:, r, :], start=True,
                                  stop=True)
                    last.then_inc(S0.hp, 1)
                pe.wait_ge(S0.rot, TAYLOR)
                for r in range(NROT):
                    last = tr(bank[7][:, r * P:(r + 1) * P], sm.rot[:, r, :], ident[:, :])
                last.then_inc(S0.rtp, 1)
                with pe.Fori(0, SQUARINGS) as i:
                    pe.wait_ge(S0.pair, i + 1)
                    for r in range(NROT):
                        mm(bank[6][:, r * P:(r + 1) * P], sm.rotT[:, r, :], sm.rot[:, r, :], start=True, stop=True)
                    for r in range(NROT):
                        last = mm(bank[7][:, r * P:(r + 1) * P], sm.rot[:, r, :], sm.rotT[:, r, :], start=True,
                                  stop=True)
                    last.then_inc(S0.loop_pe, 1)
                pe.wait_ge(S0.pair, SQUARINGS + 1)
                mm(bank[6][:, 0:P], sm.rot[:, 1, :], sm.rotT[:, 0, :], start=True, stop=True).then_inc(S0.mtp, 1)
                pe.wait_ge(S0.mt, 1)
                mm(bank[7][:, 0:P], sm.MT, sm.rot[:, 2, :], start=True, stop=True).then_inc(S0.rp, 1)
                pe.wait_ge(S0.w_moe, 16 * N_MOE)
                tr(bank[4][:, 0:E], sm.eb2, ident[0:E, 0:E]).then_inc(S0.small, 1)
                mm(bank[5][:, 0:E], ones[:, :], gate_b[:, :], start=True, stop=True)
                mm(bank[5][:, E:E + 1], ones[:, :], gcb[:, :], start=True, stop=True).then_inc(S0.small2, 1)
                pe.wait_ge(S0.r, 1)
                for g in range(NU // TILES):
                    after(pe, S0.fT, g)
                    for n in range(TILES):
                        last = tr(bank[0][:, n * P:(n + 1) * P], sm.ew2[:, TILES * g + n, :], ident[:, :])
                    last.then_inc(S0.ft, 1)
                    pe.wait_ge(S0.fT, g + 1)
                    after(pe, S0.flo, g)
                    for n in range(TILES):
                        last = mm(bank[1][:, n * P:(n + 1) * P], sm.blkT[:, n, :], sm.R, start=True, stop=True)
                    last.then_inc(S0.fm, 1)
                pe.wait_ge(S0.eb2T, 2)
                mm(bank[2][0:2 * E, 0:P], sm.eb2T.rearrange("p a b -> p (a b)"), sm.R, start=True, stop=True)\
                    .then_inc(S0.fm, 1)

            def turn_chunk(z, zp, sem_z, value, sem_out, to=0):
                pe.wait_ge(sem_z, value)
                for t in range(TILES):
                    last = tr(bank[to][:, t * P:(t + 1) * P], z[:, zp, t * P:(t + 1) * P], ident[:, :])
                last.then_inc(sem_out, 1)

            def ffn0(S, first, number):
                def step(i, p, lead, mid, lag):
                    for j in range(HB):
                        if mid:
                            if j == 0:
                                pe.wait_ge(S.xlo, i + 1)
                            b = (HB * p + j) % 2
                            after(pe, S.h, HB * i + j - 1)
                            cols = slice(j * P, (j + 1) * P)
                            for k, dst in ((0, bank[1 + b]), (1, bank[3 + b])):
                                last = three(dst[:, :], f0hi[:, k, cols], f0lo[:, k, cols], f0.xhi[:, p, :],
                                             f0.xlo[:, p, :])
                            last.then_inc(S.gu, 1)
                        if lag and j == 0:
                            pe.wait_ge(S.hlo, HB * i)
                            for m in range(HB):
                                u = HB * (1 - p) + m
                                w = slice(m * P, (m + 1) * P)
                                last = three(bank[5][:, :], f0hi[:, 2, w], f0lo[:, 2, w], f0.hhi[:, u, :],
                                             f0.hlo[:, u, :], start=(m == 0), stop=(m == HB - 1))
                            last.then_inc(S.down_mm, 1)
                    if lead:
                        turn_chunk(f0.z, 1 - p, S.z, i + 2, S.tr)
                    if lag:
                        pe.wait_ge(S.y, i)
                        after(pe, S.x, i - 1 + CREDIT)
                        for t in range(TILES):
                            tok = slice(t * P, (t + 1) * P)
                            last = tr(bank[7][:, tok], f0.y[:, tok], ident[:, :])
                        last.then_inc(S.down, 1)
                pipeline(pe, first, NCH, step)

            def mixing(S, first, number):
                def step(i, p, lead, mid, lag):
                    if mid:
                        for m, x in enumerate((tm.xk, tm.xv, tm.xr)):
                            pe.wait_ge(S.xkvr, 3 * i + m + 1)
                            mm(bank[1 + 3 * p + m][:, :], waT[:, m, :], x, start=True, stop=True)\
                                .then_inc(S.kv, 1)
                    if lag:
                        pe.wait_ge(S.y, i)
                        after(pe, S.x, i - 1 + CREDIT)
                        for t in range(TILES):
                            tok = slice(t * P, (t + 1) * P)
                            last = mm(bank[7][:, tok], tm.y[:, 1 - p, tok], waT[:, 3, :], start=True, stop=True)
                        last.then_inc(S.out, 1)
                    if lead:
                        turn_chunk(tm.z, 1 - p, S.z, i + 2, S.tr)
                pipeline(pe, first, NCH, step)

            def experts(S, first, number):
                def step(i, p, lead, mid, lag):
                    n = 1 - p

                    def second(c, cp, u):
                        pe.wait_ge(S.hlo, NU * c + u + 1)
                        if u == 0:
                            after(pe, S.dm, c)
                            mm(bank[5][:, :], ebhi[:, :], mo.wT[:, cp, :], start=True, stop=False,
                               skip_group_check=True)
                            mm(bank[5][:, :], eblo[:, :], mo.wT[:, cp, :], start=False, stop=False,
                               skip_group_check=True)
                        three(bank[5][:, :], ew2hi[:, u, :], ew2lo[:, u, :], mo.hhi[:, u % 8, :],
                              mo.hlo[:, u % 8, :], start=False, stop=(u == NU - 1)).then_inc(S.mm2, 1)

                    for u in range(NU):
                        if mid:
                            if u == 0:
                                pe.wait_ge(S.xlo, i + 1)
                            if u % EB == 0:
                                e = u // EB
                                if e == 0:
                                    pe.wait_ge(S.wT, i + 1)
                                after(pe, S.hw, NU * i + EB * (e - 1))
                                mm(bank[3 + e % 2][:, :], sel[:, e, :], mo.wT[:, p, :], start=True, stop=True)\
                                    .then_inc(S.wb, 1)
                            after(pe, S.gelu, NU * i + bank_free(u))
                            three(bank[MM1_BANK[u]][:, :], ew1hi[:, u, :], ew1lo[:, u, :], mo.xhi[:, p, :],
                                  mo.xlo[:, p, :]).then_inc(S.mm1, 1)
                        if lag and u < SKEW - 1:
                            for v in range(NU - SKEW + u, NU - SKEW + u + (2 if u == SKEW - 2 else 1)):
                                second(i - 1, n, v)
                        if mid and u >= SKEW:
                            second(i, p, u - SKEW)
                        if lead and u == 5:
                            after(pe, S.abel, i + 1)
                            turn_chunk(mo.z2, n, S.z, i + 2, S.tr, 6)
                        if lag and u == 8:
                            pe.wait_ge(S.dm, i)
                            if lead:
                                pe.wait_ge(S.xn, i + 2)
                            mm(bank[6][:, :], gc12w[:, :], mo.ab[:, n, :], start=True, stop=False)
                            mm(bank[6][:, :], gc2w[:, :], mo.dm, start=False, stop=True).then_inc(S.gate, 1)
                        if lead and u == 7:
                            pe.wait_ge(S.xn, i + 2)
                            for t in range(TILES):
                                last = mm(bank[7][:, t * E:(t + 1) * E], mo.xn[:, t * P:(t + 1) * P], gate_w[:, :],
                                          start=True, stop=True)
                            last.then_inc(S.logits, 1)
                        if lag and u == 12:
                            pe.wait_ge(S.r, i)
                            for t in range(TILES):
                                tok = slice(t * P, (t + 1) * P)
                                last = tr(bank[6][:, tok], mo.r[:, tok], ident[:, :])
                            last.then_inc(S.rT, 1)
                        if lead and u == 13:
                            pe.wait_ge(S.wpair, i + 2)
                            turned = bank[7][0:2 * E, 0:CH // 2].bitcast(F16)
                            for t in range(TILES):
                                last = tr(turned[:, t * P:(t + 1) * P], mo.wp[:, t, :], ident16[:, :])
                            last.then_inc(S.wpT, 1)
                        if lead and u == NU - 1:
                            if lag:
                                pe.wait_ge(S.x, i)
                            pe.wait_ge(S.xlo, i + 2)
                            three(bank[6][:, :], abhi[:, :], ablo[:, :], mo.xhi[:, n, :], mo.xlo[:, n, :])\
                                .then_inc(S.abel_mm, 1)
                pipeline(pe, first, NCH, step)

            def flow(S, first, number):
                def step(i, p, lead, mid, lag):
                    def turned_v(*turns):
                        for o in turns if lag else ():
                            after(pe, S.kv, HD * (i - 1) + max(o - 1, 0) + CREDIT)
                            mm(bank[5 + o % 2][:, :], WvR[:, o, :], fl.xv[:, 1 - p, :], start=True, stop=True)\
                                .then_inc(S.v, 1)

                    def project(*turns):
                        for o in turns if lag else ():
                            pe.wait_ge(S.pd, HD * (i - 1) + o + 1)
                            if o == 0:
                                after(pe, S.x, i - 1 + CREDIT)
                            for t in range(TILES):
                                tok = slice(t * P, (t + 1) * P)
                                if o == 0:
                                    mm(bank[7][:, tok], ones[:, :], bo[:, :], start=(t == 0), stop=False,
                                       skip_group_check=True)
                                last = mm(bank[7][:, tok], fl.pd[:, o % 4, tok], WoR[:, o, :], start=False,
                                          stop=(o == HD - 1), skip_group_check=True)
                            last.then_inc(S.out, 1)

                    def sums(count):
                        for m in range(2):
                            pe.wait_ge(S.pr, count + m)
                            mm(bank[3 + m][:, :], blockones[:, :], fl.pr[:, m, :], start=True, stop=True)\
                                .then_inc(S.den, 1)

                    if lag:
                        pe.wait_ge(S.xv, i)
                    turned_v(0, 1)
                    if lead:
                        turn_chunk(fl.z, 1 - p, S.z, i + 2, S.tr)
                    if mid:
                        sums(4 * i + 1)
                    turned_v(2, 3)
                    project(0)
                    if lead:
                        pe.wait_ge(S.xn, i + 2)
                        for m in range(2):
                            mm(bank[1 + m][:, :], fw[:, m, :], fl.xn[:, 1 - p, :], start=True, stop=True)\
                                .then_inc(S.qk, 1)
                    turned_v(4)
                    project(1)
                    turned_v(5)
                    project(2)
                    if mid:
                        sums(4 * i + 3)
                    turned_v(6)
                    project(3)
                    turned_v(7)
                    project(4, 5, 6, 7)
                pipeline(pe, first, NCH, step)

            setup()
            stages(pe, ffn0, mixing, experts, flow)


_INS = ["L0_attn_x", "L0_attn_time_decay", "L0_attn_time_first", "L0_attn_time_mix_k", "L0_attn_time_mix_v",
        "L0_attn_time_mix_r", "L0_attn_Wk", "L0_attn_Wv", "L0_attn_Wr", "L0_attn_Wo", "L0_ffn_w_gate",
        "L0_ffn_w_up", "L0_ffn_w_down", "L1_attn_Wq", "L1_attn_bq", "L1_attn_Wk", "L1_attn_bk", "L1_attn_Wv",
        "L1_attn_bv", "L1_attn_Wo", "L1_attn_bo", "L1_ffn_ln_gamma", "L1_ffn_ln_beta", "L1_ffn_abel_w",
        "L1_ffn_abel_b", "L1_ffn_moe_gate_w", "L1_ffn_moe_gate_b", "L1_ffn_ew1", "L1_ffn_eb1", "L1_ffn_ew2",
        "L1_ffn_eb2", "L1_ffn_gens", "L1_ffn_gc_w", "L1_ffn_gc_b"]


def kernel(**inputs):
    import numpy as _np
    import concourse.bacc as _bacc
    from concourse import mybir as _mybir
    from concourse.bass_utils import run_bass_kernel_spmd as _run

    nc = _bacc.Bacc("TRN2", target_bir_lowering=False, num_devices=1)
    arrays, args = {}, {}
    for name in _INS:
        a = _np.ascontiguousarray(inputs[name])
        arrays[f"in_{name}_dram"] = a
        args[name] = nc.dram_tensor(f"in_{name}_dram", a.shape, _mybir.dt.from_np(a.dtype), kind="ExternalInput").ap()
    shape = tuple(inputs["L0_attn_x"].shape)
    out = nc.dram_tensor("out_0_dram", shape, _mybir.dt.float32, kind="ExternalOutput").ap()
    macaron_kernel(nc, args, out)
    r = _run(nc, [arrays], core_ids=[0])
    return r.results[0]["out_0_dram"]
```

```python
from contextlib import ExitStack

import concourse.bass as bass
from concourse import mybir

ALU = mybir.AluOpType
ACT = mybir.ActivationFunctionType
F32 = mybir.dt.float32
F16 = mybir.dt.float16
I32 = mybir.dt.int32
U32 = mybir.dt.uint32
AX = mybir.AxisListType
RMAX = bass.bass_isa.ReduceOp.max

P = 128
TILES = 4
CH = P * TILES
LN_EPS = 1e-5
FLOW_EPS = 1e-6
QSCALE = 1.0 / 127.0
WS = 64.0
TAYLOR = 10
SQUARINGS = 16
HEADS = 16
HD = P // HEADS
SHARED = (4, 5)
OWN = HD - len(SHARED)
SKEW = 5
MM1_BANK = (0, 1, 2, 0, 1, 2, 0, 1, 2, 0, 1, 2, 0, 1, 2, 1)
FAR = -1e38


def bank_free(u):
    before = [v for v in range(u) if MM1_BANK[v] == MM1_BANK[u]]
    if before:
        return before[-1] + 1
    return 1 + max(v for v, b in enumerate(MM1_BANK) if b == MM1_BANK[u]) - len(MM1_BANK)


def after(eng, sem, count):
    if isinstance(count, int) and count <= 0:
        return
    eng.wait_ge(sem, count)


class Buffers:
    pass


class Semaphores:
    pass


class Chain:

    def __init__(self, eng, sem, per_chunk=0):
        self.eng, self.sem, self.per_chunk = eng, sem, per_chunk
        self.base = self.n = 0

    def at(self, chunk):
        self.base, self.n = self.per_chunk * chunk, 0

    def link(self, instruction, wait=None):
        instruction.then_inc(self.sem, 1)
        self.n += 1
        if wait:
            wait(self.eng, self.sem, self.base + self.n)
        else:
            self.eng.wait_ge(self.sem, self.base + self.n)

    def close(self):
        assert self.n == self.per_chunk, (self.n, self.per_chunk)


def pipeline(eng, first, chunks, step):
    step(first - 1, 1, True, False, False)
    step(first, 0, True, True, False)
    with eng.Fori(0, (chunks - 2) // 2) as m:
        step(2 * m + (first + 1), 1, True, True, True)
        step(2 * m + (first + 2), 0, True, True, True)
    step(first + chunks - 1, 1, False, True, True)
    step(first + chunks, 0, False, False, True)


class Arena:

    def __init__(self, whole):
        self.whole, self.used = whole, 0

    def take(self, dims, dt=F32, parts=P):
        n = 1
        for d in dims:
            n *= d
        words = n if dt != F16 else n // 2
        view = self.whole[0:parts, self.used:self.used + words]
        self.used += words
        assert self.used <= self.whole.shape[1], self.used
        if dt != F32:
            view = view.bitcast(dt)
        if len(dims) == 2:
            view = view.rearrange("p (a b) -> p a b", a=dims[0])
        if len(dims) == 3:
            view = view.rearrange("p (a b c) -> p a b c", a=dims[0], b=dims[1])
        return view


def macaron_kernel(nc, ins, out):
    B, T, C = ins["L0_attn_x"].shape
    TOK = B * T
    NCH = TOK // CH
    NT = TOK // P
    HB = ins["L0_ffn_w_gate"].shape[0] // P
    E, _, EH = ins["L1_ffn_ew1"].shape
    EB = EH // P
    NU = E * EB
    NROT = ins["L1_ffn_gens"].shape[0]
    assert C == P and T == 2 * CH and NCH % 2 == 0 and NU == 16 and HB == 3 and TAYLOR > NCH and SQUARINGS % 2 == 0

    ctx = ExitStack()
    with ctx:
        ctx.enter_context(nc.allow_non_contiguous_dma(reason="small vectors and permuted rows of weights"))

        def sb(name, shape, dt=F32):
            return ctx.enter_context(nc.sbuf_tensor(name, shape, dt))

        def sem(name):
            return ctx.enter_context(nc.semaphore(name))

        bank = [ctx.enter_context(nc.psum_tensor(f"bank{i}", [P, CH], F32)) for i in range(8)]
        X = sb("X", [P, NT * P])
        ident = sb("ident", [P, P])
        ident16 = sb("ident16", [P, P], F16)
        neghalf = sb("neghalf", [P, NT])
        eps = sb("eps", [P, NT])
        spare = sb("spare", [P, 4 + 2 * NROT])
        pool_spare = sb("pool_spare", [P, 1])
        stats = sb("stats", [P, NT, 6])
        var = sb("var", [P, NT])
        nmean = sb("nmean", [P, NT])
        veps = sb("veps", [P, NT])
        halfd = sb("halfd", [P, NT])
        rstd = sb("rstd", [P, NT])
        nbias = sb("nbias", [P, NT])
        r2 = sb("r2", [P, NT])
        v2 = sb("v2", [P, NT])
        rr = sb("rr", [P, NT])
        nbias2 = sb("nbias2", [P, NT])
        keep = sb("keep", [P, NT])
        shift = sb("shift", [P, NT])
        f0hi = sb("f0hi", [P, 3, HB * P], F16)
        f0lo = sb("f0lo", [P, 3, HB * P], F16)
        ew1hi = sb("ew1hi", [P, NU, P], F16)
        ew1lo = sb("ew1lo", [P, NU, P], F16)
        ew2hi = sb("ew2hi", [P, NU, P], F16)
        ew2lo = sb("ew2lo", [P, NU, P], F16)
        abhi = sb("abhi", [P, P], F16)
        ablo = sb("ablo", [P, P], F16)
        ebhi = sb("ebhi", [2 * E, P], F16)
        eblo = sb("eblo", [2 * E, P], F16)
        sel = sb("sel", [2 * E, E, P], F16)
        gamma = sb("gamma", [P, 1])
        beta = sb("beta", [P, 1])
        abel_b = sb("abel_b", [P, 1])
        eb1 = sb("eb1", [P, NU])
        gate_w = sb("gate_w", [P, E])
        gate_b = sb("gate_b", [1, E])
        gate_b4 = sb("gate_b4", [P, TILES, E])
        gcw = sb("gcw", [P, 2])
        gcb = sb("gcb", [1, 1])
        gcbh = sb("gcbh", [P, 1])
        gc12 = sb("gc12", [P, 1])
        ones16 = sb("ones16", [P, P], F16)
        ones = sb("ones", [1, P])
        iota8 = sb("iota8", [P, TILES, E])
        waT = sb("waT", [P, 4, P])
        tvec = sb("tvec", [P, 5])
        wneg = sb("wneg", [P, 1])
        fw = sb("fw", [P, 4, P])
        WoR = sb("WoR", [P, HD, P])
        WvR = sb("WvR", [P, HD, P])
        bvR = sb("bvR", [P, HD])
        fb = sb("fb", [P, 2])
        bo = sb("bo", [1, P])
        blockones = sb("blockones", [P, P])
        onecol = sb("onecol", [P, 1])
        Z = sb("Z", [P, 2, CH])
        arena = sb("arena", [P, 32500])

        a = Arena(arena)
        sm = Buffers()
        sm.wi = a.take([3, HB * P], I32)
        sm.wf = a.take([3, HB * P])
        sm.wa = a.take([4, P])
        sm.ew1 = a.take([NU, P])
        sm.ew2 = a.take([NU, P])
        sm.ab = a.take([P])
        sm.eb2 = a.take([P], parts=E)
        sm.eb2T = a.take([2, E])
        sm.G = a.take([NROT, P])
        sm.Gabs = a.take([NROT, P])
        sm.GT = a.take([NROT, P])
        sm.rr = a.take([NROT, 2 * P])
        sm.ident3 = a.take([NROT, P])
        sm.mask = a.take([2, NROT, P])
        sm.thr = a.take([NROT, SQUARINGS])
        sm.cneg = a.take([NROT, SQUARINGS])
        sm.active = a.take([NROT, SQUARINGS])
        sm.shrink = a.take([NROT, SQUARINGS])
        sm.rowsum = a.take([NROT])
        sm.norm = a.take([NROT])
        sm.factor = a.take([NROT])
        sm.MT = a.take([P])
        sm.R = a.take([P])
        sm.blkT = a.take([2, CH])
        a = Arena(arena)
        f0 = Buffers()
        f0.xhi = a.take([2, CH], F16)
        f0.xlo = a.take([2, CH], F16)
        f0.sg = a.take([2, CH])
        f0.h = a.take([2, CH])
        f0.hhi = a.take([2 * HB, CH], F16)
        f0.hlo = a.take([2 * HB, CH], F16)
        f0.y = a.take([CH])
        a = Arena(arena)
        tm = Buffers()
        tm.XN = a.take([1 + 2 * CH])
        tm.D = a.take([CH])
        tm.xk = a.take([CH])
        tm.xv = a.take([CH])
        tm.xr = a.take([CH])
        tm.PM = a.take([1 + 2 * CH])
        tm.SA = a.take([1 + 2 * CH])
        tm.SB = a.take([1 + 2 * CH])
        tm.arg = a.take([4, CH])
        tm.ex = a.take([4, CH])
        tm.q = a.take([CH])
        tm.f2v = a.take([CH])
        tm.e2v = a.take([CH])
        tm.n1 = a.take([CH])
        tm.n2 = a.take([CH])
        tm.num = a.take([CH])
        tm.ns = a.take([CH])
        tm.den = a.take([CH])
        tm.lnd = a.take([CH])
        tm.r0 = a.take([CH])
        tm.t = a.take([CH])
        tm.sr = a.take([CH])
        tm.y = a.take([2, CH])
        a = Arena(arena)
        mo = Buffers()
        mo.xn = a.take([CH])
        mo.xhi = a.take([2, CH], F16)
        mo.xlo = a.take([2, CH], F16)
        mo.hf = a.take([4, CH])
        mo.hw = a.take([4, CH])
        mo.hhi = a.take([8, CH], F16)
        mo.hlo = a.take([8, CH], F16)
        mo.ab = a.take([2, CH])
        mo.dm = a.take([CH])
        mo.gs = a.take([2, CH])
        mo.gs16 = a.take([2, CH], F16)
        mo.r = a.take([CH])
        mo.m = a.take([CH])
        mo.lgs = a.take([TILES, E])
        mo.top = a.take([TILES, E])
        mo.topi = a.take([TILES, E], U32)
        mo.topf = a.take([TILES, E])
        mo.dtop = a.take([TILES])
        mo.th = a.take([TILES])
        mo.w12 = a.take([2, TILES])
        mo.eq = a.take([2, TILES, E])
        mo.wd = a.take([TILES, E])
        mo.wp = a.take([TILES, 2 * E], F16)
        mo.wT = a.take([2, CH], F16, parts=2 * E)
        mo.tg = a.take([CH])
        a = Arena(arena)
        fl = Buffers()
        fl.NRM = a.take([2, CH])
        fl.INV = a.take([2, CH])
        fl.xn = a.take([2, CH])
        fl.q = a.take([2, CH])
        fl.k = a.take([2, CH])
        fl.NQ = a.take([CH])
        fl.NK = a.take([CH])
        fl.Ck = a.take([CH])
        fl.Cq = a.take([CH])
        fl.Cks = a.take([CH])
        fl.Cqs = a.take([CH])
        fl.Cc = a.take([CH])
        fl.pr = a.take([2, CH])
        fl.lnd = a.take([3, CH])
        fl.r = a.take([3, CH])
        fl.t = a.take([3, CH])
        fl.xv = a.take([2, CH])
        fl.rd = a.take([3, CH])
        fl.ks = a.take([2, CH])
        fl.c = a.take([2, CH])
        fl.sa = a.take([CH])
        fl.cs = a.take([CH])
        fl.csnk = a.take([CH])
        fl.kc = a.take([2, CH])
        fl.qr = a.take([CH])
        fl.qq = a.take([2, CH])
        fl.kv = a.take([4, CH])
        fl.S = a.take([HD, CH])
        fl.pd = a.take([4, CH])

        S0 = Semaphores()
        S0.x_first = sem("setup_x_first")
        S0.x_rest = sem("setup_x_rest")
        S0.w_ffn0 = sem("setup_w_ffn0")
        S0.w_attn0 = sem("setup_w_attn0")
        S0.w_moe = sem("setup_w_moe")
        S0.w_gens = sem("setup_w_gens")
        S0.w_flow = sem("setup_w_flow")
        S0.consts = sem("setup_consts")
        S0.dve = sem("setup_dve")
        S0.act = sem("setup_act")
        S0.pool = sem("setup_pool")
        S0.loop_pe = sem("setup_loop_pe")
        S0.pair = sem("setup_pair")
        S0.active = sem("setup_active")
        S0.loop_mask = sem("setup_loop_mask")
        S0.norm = sem("setup_norm")
        S0.cast = sem("setup_cast")
        S0.gabs = sem("setup_gabs")
        S0.rowsum = sem("setup_rowsum")
        S0.trf = sem("setup_trf")
        S0.f0hi = sem("setup_f0hi")
        S0.f0lo = sem("setup_f0lo")
        S0.trw = sem("setup_trw")
        S0.decay = sem("setup_decay")
        S0.e1hi = sem("setup_e1hi")
        S0.small = sem("setup_small")
        S0.small2 = sem("setup_small2")
        S0.eb2T = sem("setup_eb2T")
        S0.g = sem("setup_g")
        S0.gtp = sem("setup_gtp")
        S0.gt = sem("setup_gt")
        S0.rot = sem("setup_rot")
        S0.hp = sem("setup_hp")
        S0.rtp = sem("setup_rtp")
        S0.mtp = sem("setup_mtp")
        S0.mt = sem("setup_mt")
        S0.rp = sem("setup_rp")
        S0.r = sem("setup_r")
        S0.ft = sem("setup_ft")
        S0.fT = sem("setup_fT")
        S0.fm = sem("setup_fm")
        S0.fhi = sem("setup_fhi")
        S0.flo = sem("setup_flo")
        S0.nrm = sem("setup_nrm")
        LN = Semaphores()
        LN.var = sem("norm_var")
        LN.dve = sem("norm_dve")
        LN.pool = sem("norm_pool")
        LN.rstd = sem("norm_rstd")
        LN.bn = sem("norm_bn")
        FF = Semaphores()
        FF.z = sem("ffn_z")
        FF.tr = sem("ffn_tr")
        FF.x = sem("ffn_x")
        FF.xhi = sem("ffn_xhi")
        FF.xlo = sem("ffn_xlo")
        FF.gu = sem("ffn_gu")
        FF.sg = sem("ffn_sg")
        FF.h = sem("ffn_h")
        FF.hhi = sem("ffn_hhi")
        FF.hlo = sem("ffn_hlo")
        FF.down_mm = sem("ffn_down_mm")
        FF.y = sem("ffn_y")
        FF.down = sem("ffn_down")
        TM = Semaphores()
        TM.z = sem("mix_z")
        TM.tr = sem("mix_tr")
        TM.x = sem("mix_x")
        TM.init = sem("mix_init")
        TM.own = sem("mix_own")
        TM.xn = sem("mix_xn")
        TM.d = sem("mix_d")
        TM.xkvr = sem("mix_xkvr")
        TM.kv = sem("mix_kv")
        TM.arg_q = sem("mix_arg_q")
        TM.arg3 = sem("mix_arg3")
        TM.args = sem("mix_args")
        TM.ex = sem("mix_ex")
        TM.dex = sem("mix_dex")
        TM.sr = sem("mix_sr")
        TM.den = sem("mix_den")
        TM.scans = sem("mix_scans")
        TM.n12 = sem("mix_n12")
        TM.y = sem("mix_y")
        TM.e2v = sem("mix_e2v")
        TM.num = sem("mix_num")
        TM.out = sem("mix_out")
        MO = Semaphores()
        MO.z = sem("moe_z")
        MO.tr = sem("moe_tr")
        MO.x = sem("moe_x")
        MO.own = sem("moe_own")
        MO.xhi = sem("moe_xhi")
        MO.xlo = sem("moe_xlo")
        MO.xn = sem("moe_xn")
        MO.logits = sem("moe_logits")
        MO.dtop = sem("moe_dtop")
        MO.th = sem("moe_th")
        MO.wpair = sem("moe_wpair")
        MO.wpT = sem("moe_wpT")
        MO.wT = sem("moe_wT")
        MO.abel_mm = sem("moe_abel_mm")
        MO.abel = sem("moe_abel")
        MO.mm1 = sem("moe_mm1")
        MO.gelu = sem("moe_gelu")
        MO.wb = sem("moe_wb")
        MO.hw = sem("moe_hw")
        MO.hhi = sem("moe_hhi")
        MO.hlo = sem("moe_hlo")
        MO.mm2 = sem("moe_mm2")
        MO.dm = sem("moe_dm")
        MO.gate = sem("moe_gate")
        MO.tg = sem("moe_tg")
        MO.zadd = sem("moe_zadd")
        MO.m = sem("moe_m")
        MO.gs = sem("moe_gs")
        MO.r = sem("moe_r")
        MO.rT = sem("moe_rT")
        FL = Semaphores()
        FL.z = sem("flow_z")
        FL.tr = sem("flow_tr")
        FL.x = sem("flow_x")
        FL.own = sem("flow_own")
        FL.inv = sem("flow_inv")
        FL.xn = sem("flow_xn")
        FL.qk = sem("flow_qk")
        FL.sig = sem("flow_sig")
        FL.nqk = sem("flow_nqk")
        FL.pr = sem("flow_pr")
        FL.den = sem("flow_den")
        FL.lnr = sem("flow_lnr")
        FL.sa = sem("flow_sa")
        FL.cs = sem("flow_cs")
        FL.cc = sem("flow_cc")
        FL.lnc = sem("flow_lnc")
        FL.rd = sem("flow_rd")
        FL.run = sem("flow_run")
        FL.vs = sem("flow_vs")
        FL.kvp = sem("flow_kvp")
        FL.qr = sem("flow_qr")
        FL.qq = sem("flow_qq")
        FL.csnk = sem("flow_csnk")
        FL.xv = sem("flow_xv")
        FL.c12 = sem("flow_c12")
        FL.kcqq = sem("flow_kcqq")
        FL.v = sem("flow_v")
        FL.kv = sem("flow_kv")
        FL.s = sem("flow_s")
        FL.pd = sem("flow_pd")
        FL.out = sem("flow_out")
        N_CONST = 11
        N_MOE = 13
        N_FLOW = 4 + 2 + 1 + 2 * (2 * HD - 1)

        CREDIT = 1

        def wait_apart(eng, sem, count, word=0):
            eng.wait_ge(sem, count)
            eng.memset(spare[:, word:word + 1], 0.0)

        def stages(eng, ffn0, mixing, experts, flow, ahead):
            eng.wait_ge(S0.consts, N_CONST)
            eng.wait_ge(S0.x_first, 16)
            eng.wait_ge(S0.x_rest, 16 * (NCH - 1))
            ahead(FF, 0, 1)
            eng.wait_ge(S0.flo, NU // TILES + 1)
            ffn0(FF, 0, 1)
            ahead(TM, 0, 2)
            eng.wait_ge(FF.x, NCH + CREDIT)
            mixing(TM, 0, 2)
            ahead(FF, NCH, 3)
            eng.wait_ge(TM.x, NCH + CREDIT)
            ffn0(FF, NCH, 3)
            ahead(MO, 0, 4)
            eng.wait_ge(FF.x, 2 * NCH + CREDIT)
            experts(MO, 0, 4)
            ahead(FL, 0, 5)
            eng.wait_ge(MO.x, NCH)
            flow(FL, 0, 5)
            ahead(MO, NCH, 6)
            eng.wait_ge(FL.x, NCH + CREDIT)
            experts(MO, NCH, 6)
        stored = ctx.enter_context(nc.semaphore("stored"))

        x_tiles = ins["L0_attn_x"].rearrange("b (t p) c -> p (b t) c", p=P)
        out_tiles = out.rearrange("b (t p) c -> p (b t) c", p=P)
        X3 = X[:, :].rearrange("p (t c) -> p t c", c=P)

        block = ctx.enter_context(nc.Block())

        @block.sync
        def _(sp):
            sp.dma_start(X3[:, 0:TILES, :], x_tiles[:, 0:TILES, :]).then_inc(S0.x_first, 16)
            for k, name in enumerate(("gate", "up")):
                sp.dma_start(sm.wi[:, k, :].rearrange("p (j d) -> p j d", d=P),
                             ins[f"L0_ffn_w_{name}"].rearrange("(j p) d -> p j d", p=P)).then_inc(S0.w_ffn0, 16)
            sp.dma_start(sm.wi[:, 2, :], ins["L0_ffn_w_down"]).then_inc(S0.w_ffn0, 16)
            sp.dma_start(sm.G, ins["L1_ffn_gens"].rearrange("r p c -> p r c")).then_inc(S0.w_gens, 16)
            for k, name in enumerate(("Wk", "Wv", "Wr", "Wo")):
                sp.dma_start(sm.wa[:, k, :], ins[f"L0_attn_{name}"]).then_inc(S0.w_attn0, 16)
            for k, name in enumerate(("time_decay", "time_first", "time_mix_k", "time_mix_v", "time_mix_r")):
                sp.dma_start(tvec[:, k:k + 1], ins[f"L0_attn_{name}"].rearrange("a b c -> c (a b)"))\
                  .then_inc(S0.w_attn0, 16)
            for c in range(1, NCH):
                sp.dma_start(X3[:, c * TILES:(c + 1) * TILES, :], x_tiles[:, c * TILES:(c + 1) * TILES, :])\
                  .then_inc(S0.x_rest, 16)
            ew2_rows = ins["L1_ffn_ew2"].rearrange("e (j p) d -> p (e j) d", p=P)
            moe_loads = [
                (sm.ew1.rearrange("p (e j) n -> p e (j n)", j=EB), ins["L1_ffn_ew1"].rearrange("e c h -> c e h")),
                (sm.ew2[:, 0:NU // 2, :], ew2_rows[:, 0:NU // 2, :]),
                (sm.ew2[:, NU // 2:NU, :], ew2_rows[:, NU // 2:NU, :]),
                (sm.ab, ins["L1_ffn_abel_w"]),
                (sm.eb2, ins["L1_ffn_eb2"]),
                (gamma[:, :], ins["L1_ffn_ln_gamma"].rearrange("(c o) -> c o", o=1)),
                (beta[:, :], ins["L1_ffn_ln_beta"].rearrange("(c o) -> c o", o=1)),
                (abel_b[:, :], ins["L1_ffn_abel_b"].rearrange("(c o) -> c o", o=1)),
                (eb1[:, :], ins["L1_ffn_eb1"].rearrange("e (j p) -> p (e j)", p=P)),
                (gate_w[:, :], ins["L1_ffn_moe_gate_w"]),
                (gate_b[:, :], ins["L1_ffn_moe_gate_b"].rearrange("(o e) -> o e", o=1)),
                (gcw[:, :], ins["L1_ffn_gc_w"].rearrange("(a p) o -> p (a o)", p=P)),
                (gcb[:, :], ins["L1_ffn_gc_b"].rearrange("(o e) -> o e", o=1)),
            ]
            assert len(moe_loads) == N_MOE
            for dst, src in moe_loads:
                sp.dma_start(dst, src).then_inc(S0.w_moe, 16)
            for k, name in enumerate(("Wq", "Wk", "Wv", "Wo")):
                sp.dma_start(fw[:, k, :], ins[f"L1_attn_{name}"]).then_inc(S0.w_flow, 16)
            for k, name in enumerate(("bq", "bk")):
                sp.dma_start(fb[:, k:k + 1], ins[f"L1_attn_{name}"].rearrange("(c o) -> c o", o=1))\
                  .then_inc(S0.w_flow, 16)
            sp.dma_start(bo[:, :], ins["L1_attn_bo"].rearrange("(o c) -> o c", o=1)).then_inc(S0.w_flow, 16)
            wo_rows = ins["L1_attn_Wo"].rearrange("(h m) n -> h m n", m=HD)
            bv_rows = ins["L1_attn_bv"].rearrange("(h m) -> h m", m=HD)
            for d in range(HD):
                sp.dma_start(WoR[d:P:HD, 0:HD - d, :], wo_rows[:, d:HD, :]).then_inc(S0.w_flow, 16)
                sp.dma_start(bvR[d:P:HD, 0:HD - d], bv_rows[:, d:HD]).then_inc(S0.w_flow, 16)
                if d:
                    sp.dma_start(WoR[d:P:HD, HD - d:HD, :], wo_rows[:, 0:d, :]).then_inc(S0.w_flow, 16)
                    sp.dma_start(bvR[d:P:HD, HD - d:HD], bv_rows[:, 0:d]).then_inc(S0.w_flow, 16)
            with sp.Fori(0, NCH) as c:
                sp.wait_ge(MO.x, c + (NCH + 1))
                sp.dma_start(out_tiles[:, bass.ds(c * TILES, TILES), :],
                             X3[:, bass.ds(c * TILES, TILES), :]).then_inc(stored, 16)
            sp.wait_ge(stored, 16 * NCH)

        @block.gpsimd
        def _(pool):

            def setup():
                pool.memset(ident[:, :], 0.0).then_inc(S0.pool, 1)
                pool.memset(ident16[:, :], 0.0).then_inc(S0.pool, 1)
                pool.memset(sm.ident3, 0.0).then_inc(S0.pool, 1)
                pool.memset(sel[:, :, :], 0.0).then_inc(S0.pool, 1)
                pool.memset(blockones[:, :], 1.0).then_inc(S0.pool, 1)
                pool.memset(neghalf[:, :], -0.5).then_inc(S0.consts, 1)
                pool.memset(eps[:, :], LN_EPS).then_inc(S0.consts, 1)
                pool.memset(ones[:, :], 1.0).then_inc(S0.consts, 1)
                pool.memset(ones16[:, :], 1.0).then_inc(S0.consts, 1)
                pool.memset(onecol[:, :], 1.0).then_inc(S0.consts, 1)
                pool.iota(iota8[:, :, :], [[0, TILES], [1, E]], base=0, channel_multiplier=0,
                          allow_small_or_imprecise_dtypes=True).then_inc(S0.consts, 1)
                pool.wait_ge(S0.pool, 5)
                pool.affine_select(out=sel[:, :, :], in_=sel[:, :, :], compare_op=ALU.not_equal, fill=1.0, base=0,
                                   pattern=[[-1, E], [0, P]], channel_multiplier=1).then_inc(S0.pool, 1)
                pool.affine_select(out=blockones[:, :], in_=blockones[:, :], compare_op=ALU.is_ge, fill=0.0,
                                   base=0, pattern=[[-HD, HEADS], [0, HD]], channel_multiplier=1)\
                    .then_inc(S0.pool, 1)
                for m in (ident[:, :], ident16[:, :]):
                    pool.affine_select(out=m, in_=m, compare_op=ALU.not_equal, fill=1.0, base=0,
                                       pattern=[[-1, P]], channel_multiplier=1).then_inc(S0.consts, 1)
                pool.affine_select(out=sm.ident3, in_=sm.ident3, compare_op=ALU.not_equal, fill=1.0, base=0,
                                   pattern=[[0, NROT], [-1, P]], channel_multiplier=1).then_inc(S0.consts, 1)
                pool.wait_ge(S0.pool, 7)
                pool.affine_select(out=sel[:, :, :], in_=sel[:, :, :], compare_op=ALU.not_equal, fill=1.0, base=-E,
                                   pattern=[[-1, E], [0, P]], channel_multiplier=1).then_inc(S0.consts, 1)
                pool.affine_select(out=blockones[:, :], in_=blockones[:, :], compare_op=ALU.is_ge, fill=0.0,
                                   base=HD - 1, pattern=[[HD, HEADS], [0, HD]], channel_multiplier=-1)\
                    .then_inc(S0.consts, 1)
                pool.wait_ge(S0.rowsum, 1)
                pool.partition_all_reduce(sm.norm, sm.rowsum, P, RMAX).then_inc(S0.norm, 1)

            norm_chain = Chain(pool, LN.pool)

            def ahead(S, first, number):
                def link(instruction):
                    norm_chain.link(instruction)

                for n, part in enumerate((slice(0, TILES), slice(TILES, NT - TILES), slice(NT - TILES, NT))):
                    pool.wait_ge(LN.var, 2 * number - (n < 2))
                    v, e, h = var[:, part], eps[:, part], neghalf[:, part]
                    link(pool.tensor_tensor(veps[:, part], v, e, ALU.add))
                    link(pool.tensor_tensor(rstd[:, part], veps[:, part], h, ALU.pow))
                    link(pool.tensor_tensor(nbias[:, part], nmean[:, part], rstd[:, part], ALU.mult))
                    if S is MO:
                        link(pool.tensor_tensor(r2[:, part], rstd[:, part], rstd[:, part], ALU.mult))
                        link(pool.tensor_tensor(r2[:, part], v, r2[:, part], ALU.mult))
                        link(pool.tensor_tensor(r2[:, part], r2[:, part], e, ALU.add))
                        link(pool.tensor_tensor(v2[:, part], r2[:, part], h, ALU.pow))
                        link(pool.tensor_tensor(rr[:, part], rstd[:, part], v2[:, part], ALU.mult))
                        link(pool.tensor_tensor(nbias2[:, part], nmean[:, part], rr[:, part], ALU.mult))
                        link(pool.tensor_scalar(keep[:, part], rstd[:, part], 0.5, 1.0, ALU.mult, ALU.add))
                        link(pool.tensor_scalar(shift[:, part], nbias[:, part], 0.5, None, ALU.mult))
                    pool.memset(pool_spare[:, :], 0.0).then_inc(LN.rstd, 1)

            def ffn0(S, first, number):

                def step(i, p, lead, mid, lag):
                    if mid:
                        for j in range(HB):
                            u = HB * p + j
                            pool.wait_ge(S.hhi, HB * i + j + 1)
                            pool.tensor_tensor(f0.hlo[:, u, :], f0.h[:, u % 2, :], f0.hhi[:, u, :],
                                               ALU.subtract).then_inc(S.hlo, 1)
                pipeline(pool, first, NCH, step)

            def mixing(S, first, number):
                pool.wait_ge(S.init, 1)

                def step(i, p, lead, mid, lag):
                    o = p * CH
                    if mid:
                        pool.wait_ge(S.arg_q, i + 1)
                        pool.tensor_tensor(tm.arg[:, 2, :], tm.PM[:, o:o + CH], tm.q, ALU.subtract)\
                            .then_inc(S.arg3, 1)
                    if lead:
                        n = (1 - p) * CH
                        pool.wait_ge(S.xn, i + 2)
                        pool.tensor_tensor(tm.D, tm.XN[:, 1 + n:1 + n + CH], tm.XN[:, n:n + CH],
                                           ALU.subtract).then_inc(S.d, 1)
                    if mid:
                        pool.wait_ge(S.ex, 4 * i + 3)
                        pool.wait_ge(S.scans, 2 * i + 1)
                        pool.tensor_tensor(tm.n2, tm.ex[:, 2, :], tm.SB[:, o:o + CH], ALU.mult)\
                            .then_inc(S.n12, 1)
                        pool.wait_ge(S.scans, 2 * i + 2)
                        pool.tensor_tensor(tm.n1, tm.ex[:, 2, :], tm.SA[:, o:o + CH], ALU.mult)\
                            .then_inc(S.n12, 1)
                        pool.wait_ge(S.n12, 2 * i + 2)
                        pool.wait_ge(S.e2v, i + 1)
                        pool.tensor_tensor(tm.num, tm.n1, tm.e2v, ALU.add).then_inc(S.num, 1)
                        pool.wait_ge(S.num, 2 * i + 1)
                        pool.tensor_tensor(tm.ns, tm.num, tm.sr, ALU.mult).then_inc(S.num, 1)
                pipeline(pool, first, NCH, step)

            def experts(S, first, number):

                def step(i, p, lead, mid, lag):
                    def low(u):
                        pool.wait_ge(S.hhi, NU * i + u + 1)
                        pool.tensor_tensor(mo.hlo[:, u % 8, :], mo.hw[:, u % 4, :], mo.hhi[:, u % 8, :],
                                           ALU.subtract).then_inc(S.hlo, 1)
                    for u in range(NU):
                        if mid:
                            low(u)
                pipeline(pool, first, NCH, step)

            def flow(S, first, number):
                pool.iota(fl.NRM.rearrange("p a n -> p (a n)"), [[1, 2 * CH]], base=1, channel_multiplier=0,
                          allow_small_or_imprecise_dtypes=True).then_inc(S0.nrm, 1)
                pool.wait_ge(S0.nrm, 1)

                def step(i, p, lead, mid, lag):
                    def weigh(*turns):
                        for o in turns if lag else ():
                            pool.wait_ge(S.s, HD * (i - 1) + o + 1)
                            after(pool, S.out, HD * (i - 1) + max(o - 3, 0) + CREDIT)
                            pool.tensor_tensor(fl.pd[:, o % 4, :], fl.S[:, o, :], fl.qq[:, 1 - p, :],
                                               ALU.mult).then_inc(S.pd, 1)
                    if mid:
                        pool.wait_ge(S.sig, 2 * i + 2)
                        after(pool, S.csnk, i)
                        pool.tensor_tensor(fl.NK, fl.k[:, p, :], fl.NRM[:, p, :], ALU.mult).then_inc(S.nqk, 1)
                        pool.tensor_tensor(fl.NQ, fl.q[:, p, :], fl.NRM[:, p, :], ALU.mult).then_inc(S.nqk, 1)
                    if lag:
                        pool.wait_ge(S.qq, i)
                    weigh(0, 1, 2)
                    if mid:
                        pool.wait_ge(S.rd, 2 * i + 1)
                        pool.tensor_tensor(fl.qr, fl.q[:, p, :], fl.rd[:, 0, :], ALU.mult).then_inc(S.qr, 1)
                    weigh(3)
                    for o in SHARED if lag else ():
                        pool.wait_ge(S.vs, len(SHARED) * (i - 1) + o - SHARED[0] + 1)
                        pool.tensor_tensor(fl.kv[:, o % 4, :], fl.kv[:, o % 4, :], fl.kc[:, 1 - p, :],
                                           ALU.mult).then_inc(S.kvp, 1)
                    weigh(4, 5)
                    if mid:
                        pool.wait_ge(S.cs, i + 1)
                        pool.tensor_tensor(fl.csnk, fl.cs, fl.NK, ALU.mult).then_inc(S.csnk, 1)
                    weigh(6, 7)
                    if mid:
                        pool.wait_ge(S.sa, i + 1)
                        pool.wait_ge(S.qr, i + 1)
                        pool.tensor_tensor(fl.qq[:, p, :], fl.qr, fl.sa, ALU.mult).then_inc(S.qq, 1)
                pipeline(pool, first, NCH, step)

            setup()
            stages(pool, ffn0, mixing, experts, flow, ahead)

        @block.scalar
        def _(act):
            A = act.activation

            def setup():
                act.wait_ge(S0.w_gens, 16)
                A(sm.Gabs, sm.G, ACT.Abs).then_inc(S0.gabs, 1)
                for k in range(3):
                    act.wait_ge(S0.trf, k + 1)
                    A(f0hi[:, k, :], bank[k][:, 0:HB * P], ACT.Copy).then_inc(S0.f0hi, 1)
                act.wait_ge(S0.trw, 1)
                A(waT[:, :, :].rearrange("p a b -> p (a b)"), bank[3][:, :], ACT.Copy).then_inc(S0.act, 1)
                A(wneg[:, :], tvec[:, 0:1], ACT.Exp).then_inc(S0.decay, 1)
                act.wait_ge(S0.gtp, 1)
                A(sm.GT.rearrange("p a b -> p (a b)"), bank[6][:, 0:NROT * P], ACT.Copy).then_inc(S0.gt, 1)
                act.wait_ge(S0.active, 1)
                for r in range(NROT):
                    act.wait_ge(S0.rtp, r + 1)
                    A(sm.rr[:, r, P:2 * P], bank[5 + r][:, P:2 * P], ACT.Copy).then_inc(S0.pair, 1)
                with act.Fori(0, SQUARINGS // 2) as m:
                    for k in range(2):
                        act.wait_ge(S0.pair, 2 * NROT * m + (NROT * k + 1))
                        A(sm.mask[:, k, :, :], sm.active[:, :, bass.ds(2 * m + k, 1)].to_broadcast([P, NROT, P]),
                          ACT.Copy).then_inc(S0.loop_mask, 1)
                act.wait_ge(S0.w_moe, 16 * N_MOE)
                A(ew1hi[:, :, :], sm.ew1, ACT.Copy, scale=WS).then_inc(S0.e1hi, 1)
                A(abhi[:, :], sm.ab, ACT.Copy, scale=WS).then_inc(S0.e1hi, 1)
                act.wait_ge(S0.mtp, 1)
                A(sm.MT, bank[6][:, 0:P], ACT.Copy).then_inc(S0.mt, 1)
                act.wait_ge(S0.rp, 1)
                A(sm.R, bank[7][:, 0:P], ACT.Copy).then_inc(S0.r, 1)
                act.wait_ge(S0.small, 1)
                for n in range(2):
                    A(sm.eb2T[:, n, :], bank[4][:, 0:E], ACT.Copy).then_inc(S0.eb2T, 1)
                def turned_block(g):
                    act.wait_ge(S0.ft, g + 1)
                    after(act, S0.fm, g - 1)
                    A(sm.blkT[:, g % 2, :], bank[2 * (g % 2)][:, :], ACT.Copy).then_inc(S0.fT, 1)

                turned_block(0)
                for g in range(NU // TILES):
                    if g + 1 < NU // TILES:
                        turned_block(g + 1)
                    act.wait_ge(S0.fm, g + 1)
                    A(ew2hi[:, TILES * g:TILES * g + TILES, :].rearrange("p a b -> p (a b)"),
                      bank[1 + 2 * (g % 2)][:, :], ACT.Copy, scale=WS).then_inc(S0.fhi, 1)
                act.wait_ge(S0.fm, NU // TILES + 1)
                A(ebhi[:, :], bank[4][0:2 * E, 0:P], ACT.Copy, scale=WS).then_inc(S0.fhi, 1)

            def normalise(c, zp, sem, first, number, tiles=range(TILES)):
                scale, bias = (rr, nbias2) if number in (4, 6) else (rstd, nbias)
                if tiles[0] == 0 and isinstance(c, int) and c < first + 2:
                    act.wait_ge(LN.rstd, 3 * number - (2 if c == first else 0))
                for t in tiles:
                    tile = (c - first) * TILES + t
                    last = A(Z[:, zp, t * P:(t + 1) * P], X[:, bass.ds((c - first) * CH + t * P, P)], ACT.Identity,
                             bias=bias[:, bass.ds(tile, 1)], scale=scale[:, bass.ds(tile, 1)])
                if tiles[-1] == TILES - 1:
                    last.then_inc(sem, 1)

            def ahead(S, first, number):
                normalise(first, 0, S.z, first, number)

            def ffn0(S, first, number):
                def step(i, p, lead, mid, lag):
                    def low(j):
                        act.wait_ge(S.h, HB * i + j + 1)
                        A(f0.hhi[:, HB * p + j, :], f0.h[:, (HB * p + j) % 2, :], ACT.Copy).then_inc(S.hhi, 1)
                    for j in range(HB):
                        if lead and mid and j == HB - 1:
                            act.wait_ge(S.tr, i + 2)
                            A(f0.xhi[:, 1 - p, :], bank[0][:, :], ACT.Copy).then_inc(S.xhi, 1)
                        if mid:
                            act.wait_ge(S.gu, HB * i + j + 1)
                            A(f0.sg[:, (HB * p + j) % 2, :], bank[1 + (HB * p + j) % 2][:, :], ACT.Silu,
                              scale=QSCALE).then_inc(S.sg, 1)
                        if lead and mid and j == 0:
                            normalise(i + 1, 1 - p, S.z, first, number)
                        if mid and j:
                            low(j - 1)
                        if lag and j == 1:
                            act.wait_ge(S.down_mm, i)
                            A(f0.y, bank[5][:, :], ACT.Copy).then_inc(S.y, 1)
                        if lead and not mid and j == HB - 1:
                            act.wait_ge(S.tr, i + 2)
                            A(f0.xhi[:, 1 - p, :], bank[0][:, :], ACT.Copy).then_inc(S.xhi, 1)
                    if mid:
                        low(HB - 1)
                pipeline(act, first, NCH, step)

            def mixing(S, first, number):
                def step(i, p, lead, mid, lag):
                    if mid:
                        if lead:
                            normalise(i + 1, 1 - p, S.z, first, number)
                        act.wait_ge(S.kv, 3 * i + 3)
                        after(act, S.y, i)
                        A(tm.sr, bank[3 + 3 * p][:, :], ACT.Sigmoid).then_inc(S.sr, 1)
                        act.preload_act_table_set("natural_log_exp_and_others")
                        act.wait_ge(S.args, 3 * i + 1)
                        A(tm.ex[:, 0, :], tm.arg[:, 0, :], ACT.Exp).then_inc(S.ex, 1)
                        act.wait_ge(S.args, 3 * i + 2)
                        A(tm.ex[:, 1, :], tm.arg[:, 1, :], ACT.Exp).then_inc(S.ex, 1)
                        act.wait_ge(S.arg3, i + 1)
                        A(tm.ex[:, 2, :], tm.arg[:, 2, :], ACT.Exp).then_inc(S.ex, 1)
                        act.wait_ge(S.args, 3 * i + 3)
                        A(tm.ex[:, 3, :], tm.arg[:, 3, :], ACT.Exp).then_inc(S.ex, 1)
                    if lead:
                        act.wait_ge(S.tr, i + 2)
                        n = 1 + (1 - p) * CH
                        A(tm.XN[:, n:n + CH], bank[0][:, :], ACT.Copy).then_inc(S.xn, 1)
                    if mid:
                        act.wait_ge(S.den, i + 1)
                        A(tm.lnd, tm.den, ACT.Ln).then_inc(S.dex, 1)
                        act.wait_ge(S.dex, 2 * i + 1)
                        A(tm.r0, tm.lnd, ACT.Exp, scale=-1.0).then_inc(S.dex, 1)
                pipeline(act, first, NCH, step)

            def experts(S, first, number):
                def step(i, p, lead, mid, lag):
                    def high(c, u):
                        act.wait_ge(S.hw, NU * c + u + 1)
                        after(act, S.mm2, NU * c + u - 7)
                        A(mo.hhi[:, u % 8, :], mo.hw[:, u % 4, :], ACT.Copy).then_inc(S.hhi, 1)
                    for u in range(NU):
                        if mid:
                            act.wait_ge(S.mm1, NU * i + u + 1)
                            after(act, S.hw, NU * i + u - 3)
                            A(mo.hf[:, u % 4, :], bank[MM1_BANK[u]][:, :], ACT.Gelu, scale=1.0 / WS,
                              bias=eb1[:, u:u + 1]).then_inc(S.gelu, 1)
                            if u:
                                high(i, u - 1)
                        if lead and mid and u < TILES:
                            normalise(i + 1, 1 - p, S.z, first, number, [u])
                        if lead and u == 6:
                            act.wait_ge(S.tr, i + 2)
                            A(mo.xn, bank[6][:, :], ACT.Identity, scale=gamma[:, :], bias=beta[:, :])\
                                .then_inc(S.xn, 1)
                        if lag and u == 9:
                            act.wait_ge(S.gate, i)
                            A(mo.tg, bank[6][:, :], ACT.Tanh, scale=0.5, bias=gcbh[:, :]).then_inc(S.tg, 1)
                        if lead and u == 10:
                            act.wait_ge(S.dtop, i + 2)
                            A(mo.th, mo.dtop, ACT.Tanh, scale=0.5).then_inc(S.th, 1)
                        if lead and u == NU - 1:
                            act.wait_ge(S.abel_mm, i + 2)
                            A(mo.ab[:, 1 - p, :], bank[6][:, :], ACT.Gelu, scale=1.0 / WS, bias=abel_b[:, :])\
                                .then_inc(S.abel, 1)
                    if mid:
                        high(i, NU - 1)
                pipeline(act, first, NCH, step)

            def flow(S, first, number):
                def step(i, p, lead, mid, lag):
                    n = 1 - p
                    if lead and mid:
                        normalise(i + 1, n, S.z, first, number)
                    if mid:
                        act.preload_act_table_set("natural_log_exp_and_others")
                        for m in range(2):
                            act.wait_ge(S.den, 4 * i + m + 1)
                            A(fl.lnd[:, m, :], bank[3 + m][:, :], ACT.Ln).then_inc(S.lnr, 1)
                        for m in range(2):
                            act.wait_ge(S.lnr, 4 * i + m + 1)
                            A(fl.r[:, m, :], fl.lnd[:, m, :], ACT.Exp, scale=-1.0).then_inc(S.lnr, 1)
                    if lead:
                        act.wait_ge(S.tr, i + 2)
                        after(act, S.xv, i)
                        A(fl.xn[:, n, :], bank[0][:, :], ACT.Copy).then_inc(S.xn, 1)
                    for o in SHARED if lag else ():
                        act.wait_ge(S.v, HD * (i - 1) + o + 1)
                        act.wait_ge(S.s, HD * (i - 1) + o - 3)
                        A(fl.kv[:, o % 4, :], bank[5 + o % 2][:, :], ACT.Identity, bias=bvR[:, o:o + 1])\
                            .then_inc(S.vs, 1)
                    if mid:
                        A(fl.xv[:, p, :], fl.xn[:, p, :], ACT.Copy).then_inc(S.xv, 1)
                    if mid:
                        act.wait_ge(S.c12, 2 * i + 1)
                        A(fl.cs, fl.c[:, 1, :], ACT.Exp, scale=-1.0).then_inc(S.cs, 1)
                        act.wait_ge(S.cc, i + 1)
                        A(fl.lnd[:, 2, :], fl.Cc, ACT.Ln).then_inc(S.lnc, 1)
                        act.wait_ge(S.lnc, 2 * i + 1)
                        A(fl.r[:, 2, :], fl.lnd[:, 2, :], ACT.Exp, scale=-1.0).then_inc(S.lnc, 1)
                    if lead:
                        for m, dst in enumerate((fl.q, fl.k)):
                            act.wait_ge(S.qk, 2 * i + m + 3)
                            A(dst[:, n, :], bank[1 + m][:, :], ACT.Sigmoid, bias=fb[:, m:m + 1]).then_inc(S.sig, 1)
                    if mid:
                        act.wait_ge(S.c12, 2 * i + 2)
                        A(fl.sa, fl.c[:, 0, :], ACT.Sigmoid, scale=-1.0).then_inc(S.sa, 1)
                pipeline(act, first, NCH, step)

            setup()
            stages(act, ffn0, mixing, experts, flow, ahead)

        @block.vector
        def _(dve):
            TS, TT, STT = dve.tensor_scalar, dve.tensor_tensor, dve.scalar_tensor_tensor
            flat = "p a b -> p (a b)"
            halves = "p (a b) -> p a b"

            def setup():
                chain = Chain(dve, S0.dve)
                dve.wait_ge(S0.w_ffn0, 48)
                dve.tensor_copy(sm.wf, sm.wi).then_inc(S0.cast, 1)
                for i in range(SQUARINGS):
                    last = dve.memset(sm.thr[:, :, i:i + 1], float(2 ** i))
                chain.link(last)
                dve.wait_ge(S0.gabs, 1)
                dve.tensor_reduce(sm.rowsum, sm.Gabs, AX.X, ALU.add).then_inc(S0.rowsum, 1)
                chain.link(dve.reciprocal(sm.cneg.rearrange(flat), sm.thr.rearrange(flat)))
                chain.link(TS(sm.cneg.rearrange(flat), sm.cneg.rearrange(flat), 0.5, -1.0, ALU.mult, ALU.add))
                for k in range(3):
                    dve.wait_ge(S0.f0hi, k + 1)
                    TT(f0lo[:, k, :], bank[k][:, 0:HB * P], f0hi[:, k, :], ALU.subtract).then_inc(S0.f0lo, 1)
                dve.wait_ge(S0.norm, 1)
                for r in range(NROT):
                    last = TS(sm.active[:, r, :], sm.thr[:, r, :], sm.norm[:, r:r + 1], None, ALU.is_lt)
                last.then_inc(S0.active, 1)
                dve.wait_ge(S0.active, 1)
                chain.link(TT(sm.shrink, sm.active, sm.cneg, ALU.mult))
                chain.link(TS(sm.shrink, sm.shrink, 1.0, None, ALU.add))
                chain.link(dve.tensor_reduce(sm.factor, sm.shrink, AX.X, ALU.min))
                for r in range(NROT):
                    last = TS(sm.G[:, r, :], sm.G[:, r, :], sm.factor[:, r:r + 1], None, ALU.mult)
                last.then_inc(S0.g, 1)
                dve.wait_ge(S0.g, 1)
                dve.wait_ge(S0.consts, N_CONST)
                for r in range(NROT):
                    STT(out=sm.rr[:, r, 0:P], in0=sm.G[:, r, :], scalar=1.0 / TAYLOR, in1=sm.ident3[:, r, :],
                        op0=ALU.mult, op1=ALU.add).then_inc(S0.rot, 1)
                dve.wait_ge(S0.x_first, 16)
                dve.wait_ge(S0.x_rest, 16 * (NCH - 1))
                for n, k in enumerate(range(TAYLOR - 1, 0, -1)):
                    for r in range(NROT):
                        dve.wait_ge(S0.hp, NROT * n + r + 1)
                        STT(out=sm.rr[:, r, 0:P], in0=bank[5 + r][:, 0:P], scalar=1.0 / k, in1=sm.ident3[:, r, :],
                            op0=ALU.mult, op1=ALU.add).then_inc(S0.rot, 1)
                    if n < NCH:
                        tile_stats(n)
                with dve.Fori(0, SQUARINGS // 2) as m:
                    for k in range(2):
                        dve.wait_ge(S0.loop_mask, 2 * m + (k + 1))
                        for r in range(NROT):
                            wait_apart(dve, S0.loop_pe, 2 * NROT * m + (NROT * k + r + 1), 4 + NROT * k + r)
                            bits = sm.mask[:, k, r:r + 1, :].to_broadcast([P, 2, P]).bitcast(I32)
                            dve.copy_predicated(sm.rr[:, r, :].rearrange(halves, a=2), bits,
                                                bank[5 + r][:, 0:2 * P].rearrange(halves, a=2)).then_inc(S0.pair, 1)
                variances(1, False)
                variances(1, True)
                dve.wait_ge(S0.decay, 1)
                chain.link(TS(wneg[:, :], wneg[:, :], -1.0, None, ALU.mult))
                dve.wait_ge(S0.e1hi, 2)
                STT(out=ew1lo[:, :, :], in0=sm.ew1, scalar=WS, in1=ew1hi[:, :, :], op0=ALU.mult, op1=ALU.subtract)
                STT(out=ablo[:, :], in0=sm.ab, scalar=WS, in1=abhi[:, :], op0=ALU.mult, op1=ALU.subtract)
                TT(gc12[:, :], gcw[:, 0:1], gcw[:, 1:2], ALU.add)
                dve.wait_ge(S0.small2, 1)
                for t in range(TILES):
                    dve.tensor_copy(gate_b4[:, t, :], bank[5][:, 0:E])
                TS(gcbh[:, :], bank[5][:, E:E + 1], 0.5, None, ALU.mult)
                dve.wait_ge(S0.w_flow, 16 * N_FLOW)
                wv = fw[:, 2, :].rearrange("p (h m) -> p h m", m=HD)
                for o in range(HD):
                    turned = WvR[:, o, :].rearrange("p (h d) -> p h d", d=HD)
                    last = dve.tensor_copy(turned[:, :, 0:HD - o], wv[:, :, o:HD])
                    if o:
                        last = dve.tensor_copy(turned[:, :, HD - o:HD], wv[:, :, 0:o])
                for g in range(NU // TILES):
                    dve.wait_ge(S0.fhi, g + 1)
                    STT(out=ew2lo[:, TILES * g:TILES * g + TILES, :].rearrange(flat), in0=bank[1 + 2 * (g % 2)][:, :],
                        scalar=WS, in1=ew2hi[:, TILES * g:TILES * g + TILES, :].rearrange(flat), op0=ALU.mult,
                        op1=ALU.subtract).then_inc(S0.flo, 1)
                dve.wait_ge(S0.fhi, NU // TILES + 1)
                STT(out=eblo[:, :], in0=bank[4][0:2 * E, 0:P], scalar=WS, in1=ebhi[:, :], op0=ALU.mult,
                    op1=ALU.subtract).then_inc(S0.flo, 1)

            def tile_stats(c):
                for t in range(TILES):
                    last = dve.bn_stats(stats[:, bass.ds(c * TILES + t, 1), :], X[:, bass.ds(c * CH + t * P, P)])
                last.then_inc(LN.bn, 1)

            norm_chain = Chain(dve, LN.dve)

            def variances(number, last):
                part = slice(NT - TILES, NT) if last else slice(0, NT - TILES)
                dve.wait_ge(LN.bn, NCH * number - (not last))
                col = lambda k: stats[:, part, k:k + 1].rearrange("p t o -> p (t o)")
                nm, m, v = nmean[:, part], halfd[:, part], var[:, part]
                link = norm_chain.link
                TT(m, col(1), col(4), ALU.subtract).then_inc(LN.dve, 1)
                TT(v, col(2), col(5), ALU.add).then_inc(LN.dve, 1)
                norm_chain.n += 2
                link(STT(out=nm, in0=col(1), scalar=-1.0, in1=col(4), op0=ALU.mult, op1=ALU.subtract))
                TS(nm, nm, 0.5, None, ALU.mult).then_inc(LN.dve, 1)
                norm_chain.n += 1
                link(STT(out=m, in0=m, scalar=0.25, in1=m, op0=ALU.mult, op1=ALU.mult))
                STT(out=v, in0=v, scalar=1.0 / P, in1=m, op0=ALU.mult, op1=ALU.add).then_inc(LN.var, 1)

            def ahead(S, first, number):
                if number > 1:
                    variances(number, True)

            def add_to_x(c, first, in0, scalar, sem):
                xc = X[:, bass.ds((c - first) * CH, CH)]
                STT(out=xc, in0=in0, scalar=scalar, in1=xc, op0=ALU.mult, op1=ALU.add).then_inc(sem, 1)

            def finish_x(c, first, in0, scalar, sem, count):
                add_to_x(c, first, in0, scalar, sem)
                wait_apart(dve, sem, count)
                tile_stats(c - first)

            def ffn0(S, first, number):
                if first == 0:
                    dve.memset(spare[:, 1:2], 0.0).then_inc(S.x, CREDIT)

                def step(i, p, lead, mid, lag):
                    if lag and not mid:
                        variances(number + 1, False)
                    if mid:
                        for j in range(HB):
                            if lead and j == HB - 1:
                                dve.wait_ge(S.xhi, i + 2)
                                TT(f0.xlo[:, 1 - p, :], bank[0][:, :], f0.xhi[:, 1 - p, :], ALU.subtract)\
                                    .then_inc(S.xlo, 1)
                            u = (HB * p + j) % 2
                            dve.wait_ge(S.sg, HB * i + j + 1)
                            after(dve, S.hlo, HB * i + j - 1)
                            STT(out=f0.h[:, u, :], in0=bank[3 + u][:, :], scalar=QSCALE, in1=f0.sg[:, u, :],
                                op0=ALU.mult, op1=ALU.mult).then_inc(S.h, 1)
                    if lead and not mid:
                        dve.wait_ge(S.xhi, i + 2)
                        TT(f0.xlo[:, 1 - p, :], bank[0][:, :], f0.xhi[:, 1 - p, :], ALU.subtract)\
                            .then_inc(S.xlo, 1)
                    if lag:
                        dve.wait_ge(S.down, i)
                        finish_x(i - 1, first, bank[7][:, :], 0.5 * QSCALE, S.x, i + CREDIT)
                pipeline(dve, first, NCH, step)

            def mixing(S, first, number):
                own = Chain(dve, S.own, 4)
                w, u, mix = wneg[:, 0:1], tvec[:, 1:2], lambda n: tvec[:, 2 + n:3 + n]
                dve.memset(tm.XN[:, 0:1], 0.0)
                dve.memset(tm.PM[:, 0:1], FAR)
                dve.memset(tm.SA[:, 0:1], 0.0)
                dve.memset(tm.SB[:, 0:1], 0.0).then_inc(S.init, 1)
                dve.wait_ge(S.init, 1)
                dve.memset(spare[:, 1:2], 0.0).then_inc(S.x, CREDIT)

                def step(i, p, lead, mid, lag):
                    if lag and not mid:
                        variances(number + 1, False)
                    o = p * CH
                    if mid:
                        own.at(i)
                    if mid:
                        k, v = bank[2 + 3 * p - 1][:, :], bank[2 + 3 * p][:, :]
                        before, now = slice(o, o + CH), slice(o + 1, o + 1 + CH)
                        dve.wait_ge(S.kv, 3 * i + 1)
                        own.link(dve.tensor_tensor_scan(tm.PM[:, now], w.to_broadcast([P, CH]), k,
                                                        tm.PM[:, o:o + 1] if p else FAR, ALU.add, ALU.max))
                        STT(out=tm.q, in0=k, scalar=u, in1=tm.PM[:, before], op0=ALU.add, op1=ALU.max)\
                            .then_inc(S.arg_q, 1)
                        STT(out=tm.arg[:, 0, :], in0=tm.PM[:, before], scalar=w, in1=tm.PM[:, now], op0=ALU.add,
                            op1=ALU.subtract).then_inc(S.args, 1)
                        TT(tm.arg[:, 1, :], k, tm.PM[:, now], ALU.subtract).then_inc(S.args, 1)
                        dve.wait_ge(S.arg_q, i + 1)
                        STT(out=tm.arg[:, 3, :], in0=k, scalar=u, in1=tm.q, op0=ALU.add, op1=ALU.subtract)\
                            .then_inc(S.args, 1)
                    if lag:
                        dve.wait_ge(S.out, i)
                        add_to_x(i - 1, first, bank[7][:, :], -1.0, S.x)
                    if mid:
                        dve.wait_ge(S.kv, 3 * i + 2)
                        dve.wait_ge(S.ex, 4 * i + 2)
                        own.link(TT(tm.f2v, tm.ex[:, 1, :], v, ALU.mult))
                        dve.tensor_tensor_scan(tm.SB[:, now], tm.ex[:, 0, :], tm.ex[:, 1, :],
                                               tm.SB[:, o:o + 1] if p else 0.0, ALU.mult, ALU.add)\
                           .then_inc(S.scans, 1)
                        dve.tensor_tensor_scan(tm.SA[:, now], tm.ex[:, 0, :], tm.f2v,
                                               tm.SA[:, o:o + 1] if p else 0.0, ALU.mult, ALU.add)\
                           .then_inc(S.scans, 1)
                        dve.wait_ge(S.ex, 4 * i + 4)
                        TT(tm.e2v, tm.ex[:, 3, :], v, ALU.mult).then_inc(S.e2v, 1)
                    def mixed(*inputs):
                        n = (1 - p) * CH
                        for m in inputs if lead else ():
                            if m == 0:
                                dve.wait_ge(S.d, i + 2)
                            after(dve, S.kv, 3 * i + m + 1)
                            STT(out=(tm.xk, tm.xv, tm.xr)[m], in0=tm.D, scalar=mix(m), in1=tm.XN[:, n:n + CH],
                                op0=ALU.mult, op1=ALU.add).then_inc(S.xkvr, 1)

                    mixed(0)
                    if mid:
                        dve.wait_ge(S.n12, 2 * i + 1)
                        TT(tm.den, tm.n2, tm.ex[:, 3, :], ALU.add).then_inc(S.den, 1)
                    mixed(1, 2)
                    if lag:
                        wait_apart(dve, S.x, i + CREDIT)
                        tile_stats(i - 1 - first)
                    if mid:
                        dve.wait_ge(S.dex, 2 * i + 2)
                        dve.wait_ge(S.den, i + 1)
                        own.link(TT(tm.t, tm.den, tm.r0, ALU.mult))
                        own.link(STT(out=tm.t, in0=tm.t, scalar=2.0, in1=tm.r0, op0=ALU.subtract, op1=ALU.mult))
                        own.close()
                        dve.wait_ge(S.num, 2 * i + 2)
                        TT(tm.y[:, p, :], tm.ns, tm.t, ALU.mult).then_inc(S.y, 1)
                pipeline(dve, first, NCH, step)

            def experts(S, first, number):
                own = Chain(dve, S.own, 12)

                def step(i, p, lead, mid, lag):
                    if lag and not mid and number < 6:
                        variances(number + 1, False)
                    n = 1 - p
                    for u in range(NU):
                        if lag and u == 3:
                            dve.wait_ge(S.mm2, NU * i)
                            STT(out=mo.dm, in0=bank[5][:, :], scalar=1.0 / WS, in1=mo.ab[:, n, :],
                                op0=ALU.mult, op1=ALU.subtract).then_inc(S.dm, 1)
                        if mid:
                            dve.wait_ge(S.gelu, NU * i + u + 1)
                            dve.wait_ge(S.wb, E * i + u // EB + 1)
                            after(dve, S.hlo, NU * i + u - 3)
                            TT(mo.hw[:, u % 4, :], mo.hf[:, u % 4, :], bank[3 + (u // EB) % 2][:, :], ALU.mult)\
                                .then_inc(S.hw, 1)
                        if lag and u == 2:
                            TS(mo.gs[:, 0, :], mo.ab[:, n, :], gc12[:, :], None, ALU.mult).then_inc(S.gs, 1)
                        if lag and u == 4:
                            dve.wait_ge(S.dm, i)
                            dve.wait_ge(S.gs, 4 * i - 3)
                            STT(out=mo.gs[:, 1, :], in0=mo.dm, scalar=gcw[:, 1:2], in1=mo.gs[:, 0, :], op0=ALU.mult,
                                op1=ALU.add).then_inc(S.gs, 1)
                        if lag and u == 5:
                            dve.wait_ge(S.gs, 4 * i - 2)
                            dve.tensor_copy(mo.gs16[:, 0, :], mo.gs[:, 1, :]).then_inc(S.gs, 1)
                        if lag and u == 6:
                            dve.wait_ge(S.gs, 4 * i - 1)
                            TT(mo.gs16[:, 1, :], mo.gs[:, 1, :], mo.gs16[:, 0, :], ALU.subtract).then_inc(S.gs, 1)
                        if lead and u == 6:
                            dve.wait_ge(S.xn, i + 2)
                            dve.tensor_copy(mo.xhi[:, n, :], mo.xn).then_inc(S.xhi, 1)
                            dve.wait_ge(S.xhi, i + 2)
                            TT(mo.xlo[:, n, :], mo.xn, mo.xhi[:, n, :], ALU.subtract).then_inc(S.xlo, 1)
                        if lead and u == 7:
                            dve.wait_ge(S.z, i + 2)
                            if isinstance(i, int) and i < first + 1:
                                dve.wait_ge(LN.rstd, 3 * number - (2 if i + 1 == first else 0))
                            for t in range(TILES):
                                tile = X[:, bass.ds((i + 1 - first) * CH + t * P, P)]
                                c = bass.ds((i + 1 - first) * TILES + t, 1)
                                last = TS(tile, tile, keep[:, c], shift[:, c], ALU.mult, ALU.add)
                            last.then_inc(S.zadd, 1)
                        if lag and u == 10:
                            dve.wait_ge(S.tg, i)
                            own_t = STT(out=mo.m, in0=mo.tg, scalar=1.0, in1=mo.dm, op0=ALU.add, op1=ALU.mult)
                            own_t.then_inc(S.m, 1)
                            dve.wait_ge(S.m, i)
                            STT(out=mo.r, in0=mo.m, scalar=0.5, in1=mo.ab[:, n, :], op0=ALU.mult, op1=ALU.add)\
                                .then_inc(S.r, 1)
                        if lead and u == 8:
                            own.at(i + 1)
                            dve.wait_ge(S.logits, i + 2)
                            own.link(TT(mo.lgs, bank[7][:, 0:TILES * E].rearrange("p (t e) -> p t e", e=E),
                                        gate_b4[:, :, :], ALU.add), wait_apart)
                            for t in range(TILES):
                                last = dve.max(mo.top[:, t, :], mo.lgs[:, t, :])
                            own.link(last)
                            TT(mo.dtop.rearrange("p (t o) -> p t o", o=1), mo.top[:, :, 0:1], mo.top[:, :, 1:2],
                               ALU.subtract).then_inc(S.dtop, 1)
                            for t in range(TILES):
                                last = dve.max_index(mo.topi[:, t, :], mo.top[:, t, :], mo.lgs[:, t, :])
                            own.link(last)
                            own.link(dve.tensor_copy(mo.topf, mo.topi))
                            for m in range(2):
                                own.link(TT(mo.eq[:, m, :, :], iota8[:, :, :],
                                            mo.topf[:, :, m:m + 1].to_broadcast([P, TILES, E]), ALU.is_equal))
                        if lead and u == 11:
                            dve.wait_ge(S.th, i + 2)
                            own.link(TS(mo.w12[:, 0, :], mo.th, 0.5, 0.5, ALU.mult, ALU.add))
                            own.link(TS(mo.w12[:, 1, :], mo.th, -0.5, 0.5, ALU.mult, ALU.add))
                            for m in range(2):
                                wm = mo.w12[:, m, :].rearrange("p (t o) -> p t o", o=1)
                                own.link(TT(mo.eq[:, m, :, :], mo.eq[:, m, :, :],
                                            wm.to_broadcast([P, TILES, E]), ALU.mult))
                            own.link(TT(mo.wd, mo.eq[:, 0, :, :], mo.eq[:, 1, :, :], ALU.add))
                            own.link(dve.tensor_copy(mo.wp[:, :, 0:E], mo.wd))
                            own.close()
                            TT(mo.wp[:, :, E:2 * E], mo.wd, mo.wp[:, :, 0:E], ALU.subtract).then_inc(S.wpair, 1)
                        if lag and u == 13:
                            dve.wait_ge(S.rT, i)
                            dve.wait_ge(S.zadd, i)
                            if first == 0:
                                finish_x(i - 1, first, bank[6][:, :], 0.5, S.x, i)
                            else:
                                add_to_x(i - 1, first, bank[6][:, :], 0.5, S.x)
                        if lead and u == 13:
                            dve.wait_ge(S.wpT, i + 2)
                            dve.tensor_copy(mo.wT[:, n, :], bank[7][0:2 * E, 0:CH // 2].bitcast(F16))\
                               .then_inc(S.wT, 1)
                pipeline(dve, first, NCH, step)

            def flow(S, first, number):
                own = Chain(dve, S.own, 7)
                dve.wait_ge(S0.nrm, 1)
                dve.reciprocal(fl.INV, fl.NRM).then_inc(S.inv, 1)
                dve.wait_ge(S.inv, 1)
                for n, sem in enumerate((S.x, S.kv, S.out)):
                    dve.memset(spare[:, 1 + n:2 + n], 0.0).then_inc(sem, CREDIT)
                scan = dve.tensor_tensor_scan

                def running(buffer, values, p, start):
                    return scan(buffer, onecol[:, 0:1].to_broadcast([P, CH]), values,
                                buffer[:, CH - 1:CH] if p else start, ALU.mult, ALU.add)

                def step(i, p, lead, mid, lag):
                    if lag and not mid:
                        variances(number + 1, False)
                    n = 1 - p

                    def turn(*turns):
                        if not lag:
                            return
                        for o in turns:
                            if o in SHARED:
                                continue
                            dve.wait_ge(S.v, HD * (i - 1) + o + 1)
                            STT(out=fl.kv[:, o % 4, :], in0=bank[5 + o % 2][:, :], scalar=bvR[:, o:o + 1],
                                in1=fl.kc[:, n, :], op0=ALU.add, op1=ALU.mult).then_inc(S.kv, 1)
                        for o in turns:
                            if o in SHARED:
                                dve.wait_ge(S.kvp, len(SHARED) * (i - 1) + o - SHARED[0] + 1)
                            else:
                                before = o if o < SHARED[0] else o - len(SHARED)
                                dve.wait_ge(S.kv, OWN * (i - 1) + before + 1 + CREDIT)
                            scan(fl.S[:, o, :], onecol[:, 0:1].to_broadcast([P, CH]), fl.kv[:, o % 4, :],
                                 fl.S[:, o, CH - 1:CH] if n else 0.0, ALU.mult, ALU.add).then_inc(S.s, 1)

                    def newton(m):
                        return STT(out=fl.rd[:, m, :], in0=fl.t[:, m, :], scalar=2.0, in1=fl.r[:, m, :],
                                   op0=ALU.subtract, op1=ALU.mult)

                    if lag:
                        dve.wait_ge(S.kcqq, i)
                    turn(0, 1)
                    if mid:
                        own.at(i)
                    turn(2, 3)
                    if mid:
                        for m in range(2):
                            dve.wait_ge(S.lnr, 4 * i + 3 + m)
                            last = TT(fl.t[:, m, :], bank[3 + m][:, :], fl.r[:, m, :], ALU.mult)
                        own.link(last)
                        for m in range(2):
                            newton(m).then_inc(S.rd, 1)
                        dve.wait_ge(S.nqk, 2 * i + 2)
                        dve.wait_ge(S.rd, 2 * i + 2)
                        for m, (nx, cum) in enumerate(((fl.NK, fl.Cks), (fl.NQ, fl.Cqs))):
                            own.link(TT(fl.ks[:, m, :], nx, fl.rd[:, 1 - m, :], ALU.mult))
                            own.link(running(cum, fl.ks[:, m, :], p, -FLOW_EPS))
                        for m, (x, cum) in enumerate(((fl.q, fl.Cks), (fl.k, fl.Cqs))):
                            STT(out=fl.pr[:, m, :], in0=x[:, p, :], scalar=FLOW_EPS, in1=cum, op0=ALU.add,
                                op1=ALU.mult).then_inc(S.pr, 1)
                    turn(4, 5)
                    if mid:
                        for m in (1, 0):
                            dve.wait_ge(S.den, 4 * i + 3 + m)
                            TT(fl.c[:, m, :], bank[3 + m][:, :], fl.INV[:, p, :], ALU.mult).then_inc(S.c12, 1)
                    turn(6)
                    if mid:
                        dve.wait_ge(S.cs, i + 1)
                        running(fl.Cc, fl.cs, p, 0.0).then_inc(S.cc, 1)
                    turn(7)
                    if mid:
                        dve.wait_ge(S.lnc, 2 * i + 2)
                        dve.wait_ge(S.cc, i + 1)
                        own.link(TT(fl.t[:, 2, :], fl.Cc, fl.r[:, 2, :], ALU.mult))
                        own.link(newton(2))
                        dve.wait_ge(S.csnk, i + 1)
                        TT(fl.kc[:, p, :], fl.csnk, fl.rd[:, 2, :], ALU.mult).then_inc(S.kcqq, 1)
                        own.close()
                    if lead:
                        dve.wait_ge(S.sig, 2 * i + 4)
                        running(fl.Ck, fl.k[:, n, :], n, FLOW_EPS)
                        running(fl.Cq, fl.q[:, n, :], n, FLOW_EPS).then_inc(S.run, 1)
                        dve.wait_ge(S.run, i + 2)
                        for m, (x, cum) in enumerate(((fl.q, fl.Ck), (fl.k, fl.Cq))):
                            STT(out=fl.pr[:, m, :], in0=x[:, n, :], scalar=FLOW_EPS, in1=cum, op0=ALU.add,
                                op1=ALU.mult).then_inc(S.pr, 1)
                    if lag:
                        dve.wait_ge(S.out, HD * i + CREDIT)
                        finish_x(i - 1, first, bank[7][:, :], 1.0, S.x, i + CREDIT)
                pipeline(dve, first, NCH, step)

            setup()
            stages(dve, ffn0, mixing, experts, flow, ahead)

        @block.tensor
        def _(pe):
            mm, tr = pe.matmul, pe.transpose

            def three(dst, whi, wlo, xhi, xlo, start=True, stop=True):
                mm(dst, whi, xhi, start=start, stop=False, skip_group_check=True)
                mm(dst, whi, xlo, start=False, stop=False, skip_group_check=True)
                return mm(dst, wlo, xhi, start=False, stop=stop, skip_group_check=True)

            def setup():
                rot, rotT = lambda r: sm.rr[:, r, 0:P], lambda r: sm.rr[:, r, P:2 * P]
                pe.wait_ge(S0.consts, N_CONST)
                pe.wait_ge(S0.cast, 1)
                for k in range(3):
                    for j in range(HB):
                        last = tr(bank[k][:, j * P:(j + 1) * P], sm.wf[:, k, j * P:(j + 1) * P], ident[:, :])
                    last.then_inc(S0.trf, 1)
                pe.wait_ge(S0.w_attn0, 16 * 9)
                for k in range(4):
                    last = tr(bank[3][:, k * P:(k + 1) * P], sm.wa[:, k, :], ident[:, :])
                last.then_inc(S0.trw, 1)
                pe.wait_ge(S0.g, 1)
                for r in range(NROT):
                    last = tr(bank[6][:, r * P:(r + 1) * P], sm.G[:, r, :], ident[:, :])
                last.then_inc(S0.gtp, 1)
                pe.wait_ge(S0.gt, 1)
                for n in range(TAYLOR - 1):
                    for r in range(NROT):
                        pe.wait_ge(S0.rot, NROT * n + r + 1)
                        mm(bank[5 + r][:, 0:P], sm.GT[:, r, :], rot(r), start=True, stop=True).then_inc(S0.hp, 1)
                for r in range(NROT):
                    pe.wait_ge(S0.rot, NROT * (TAYLOR - 1) + r + 1)
                    tr(bank[5 + r][:, P:2 * P], rot(r), ident[:, :]).then_inc(S0.rtp, 1)
                with pe.Fori(0, SQUARINGS) as i:
                    for r in range(NROT):
                        pe.wait_ge(S0.pair, NROT * i + (r + 1))
                        mm(bank[5 + r][:, 0:P], rotT(r), rot(r), start=True, stop=True)
                        mm(bank[5 + r][:, P:2 * P], rot(r), rotT(r), start=True, stop=True).then_inc(S0.loop_pe, 1)
                pe.wait_ge(S0.pair, NROT * (SQUARINGS + 1))
                mm(bank[6][:, 0:P], rot(1), rotT(0), start=True, stop=True).then_inc(S0.mtp, 1)
                pe.wait_ge(S0.mt, 1)
                mm(bank[7][:, 0:P], sm.MT, rot(2), start=True, stop=True).then_inc(S0.rp, 1)
                pe.wait_ge(S0.w_moe, 16 * N_MOE)
                tr(bank[4][:, 0:E], sm.eb2, ident[0:E, 0:E]).then_inc(S0.small, 1)
                mm(bank[5][:, 0:E], ones[:, :], gate_b[:, :], start=True, stop=True)
                mm(bank[5][:, E:E + 1], ones[:, :], gcb[:, :], start=True, stop=True).then_inc(S0.small2, 1)
                def turn_block(g):
                    after(pe, S0.fT, g - 1)
                    for n in range(TILES):
                        last = tr(bank[2 * (g % 2)][:, n * P:(n + 1) * P], sm.ew2[:, TILES * g + n, :], ident[:, :])
                    last.then_inc(S0.ft, 1)

                turn_block(0)
                pe.wait_ge(S0.r, 1)
                for g in range(NU // TILES):
                    if g + 1 < NU // TILES:
                        turn_block(g + 1)
                    pe.wait_ge(S0.fT, g + 1)
                    after(pe, S0.flo, g - 1)
                    for n in range(TILES):
                        last = mm(bank[1 + 2 * (g % 2)][:, n * P:(n + 1) * P], sm.blkT[:, g % 2, n * P:(n + 1) * P],
                                  sm.R, start=True, stop=True)
                    last.then_inc(S0.fm, 1)
                pe.wait_ge(S0.eb2T, 2)
                mm(bank[4][0:2 * E, 0:P], sm.eb2T.rearrange("p a b -> p (a b)"), sm.R, start=True, stop=True)\
                    .then_inc(S0.fm, 1)

            def turn_chunk(z, zp, sem_z, value, sem_out, to=0):
                pe.wait_ge(sem_z, value)
                for t in range(TILES):
                    last = tr(bank[to][:, t * P:(t + 1) * P], z[:, zp, t * P:(t + 1) * P], ident[:, :])
                last.then_inc(sem_out, 1)

            def ffn0(S, first, number):
                def step(i, p, lead, mid, lag):
                    for j in range(HB):
                        if mid:
                            if j == 0:
                                pe.wait_ge(S.xlo, i + 1)
                            b = (HB * p + j) % 2
                            after(pe, S.h, HB * i + j - 1)
                            cols = slice(j * P, (j + 1) * P)
                            for k, dst in ((0, bank[1 + b]), (1, bank[3 + b])):
                                last = three(dst[:, :], f0hi[:, k, cols], f0lo[:, k, cols], f0.xhi[:, p, :],
                                             f0.xlo[:, p, :])
                            last.then_inc(S.gu, 1)
                        if lag and j == 1:
                            pe.wait_ge(S.hlo, HB * i)
                            for m in range(HB):
                                u = HB * (1 - p) + m
                                w = slice(m * P, (m + 1) * P)
                                last = three(bank[5][:, :], f0hi[:, 2, w], f0lo[:, 2, w], f0.hhi[:, u, :],
                                             f0.hlo[:, u, :], start=(m == 0), stop=(m == HB - 1))
                            last.then_inc(S.down_mm, 1)
                        if lead and j == 1:
                            turn_chunk(Z, 1 - p, S.z, i + 2, S.tr)
                    if lag:
                        pe.wait_ge(S.y, i)
                        after(pe, S.x, i - 1 + CREDIT)
                        for t in range(TILES):
                            tok = slice(t * P, (t + 1) * P)
                            last = tr(bank[7][:, tok], f0.y[:, tok], ident[:, :])
                        last.then_inc(S.down, 1)
                pipeline(pe, first, NCH, step)

            def mixing(S, first, number):
                def step(i, p, lead, mid, lag):
                    if mid:
                        for m, x in enumerate((tm.xk, tm.xv, tm.xr)):
                            pe.wait_ge(S.xkvr, 3 * i + m + 1)
                            mm(bank[1 + 3 * p + m][:, :], waT[:, m, :], x, start=True, stop=True)\
                                .then_inc(S.kv, 1)
                    if lag:
                        pe.wait_ge(S.y, i)
                        after(pe, S.x, i - 1 + CREDIT)
                        for t in range(TILES):
                            tok = slice(t * P, (t + 1) * P)
                            last = mm(bank[7][:, tok], tm.y[:, 1 - p, tok], waT[:, 3, :], start=True, stop=True)
                        last.then_inc(S.out, 1)
                    if lead:
                        turn_chunk(Z, 1 - p, S.z, i + 2, S.tr)
                pipeline(pe, first, NCH, step)

            def experts(S, first, number):
                TAIL = {0: (11,), 1: (12,), 2: (13, 14), 3: (15,)}

                def step(i, p, lead, mid, lag):
                    n = 1 - p

                    def second(c, cp, u):
                        pe.wait_ge(S.hlo, NU * c + u + 1)
                        if u == 0:
                            after(pe, S.dm, c)
                            mm(bank[5][:, :], ebhi[:, :], mo.wT[:, cp, :], start=True, stop=False,
                               skip_group_check=True)
                            mm(bank[5][:, :], eblo[:, :], mo.wT[:, cp, :], start=False, stop=False,
                               skip_group_check=True)
                        three(bank[5][:, :], ew2hi[:, u, :], ew2lo[:, u, :], mo.hhi[:, u % 8, :],
                              mo.hlo[:, u % 8, :], start=False, stop=(u == NU - 1)).then_inc(S.mm2, 1)

                    for u in range(NU):
                        if mid:
                            if u == 0:
                                pe.wait_ge(S.xlo, i + 1)
                            if u % EB == 0:
                                e = u // EB
                                if e == 0:
                                    pe.wait_ge(S.wT, i + 1)
                                after(pe, S.hw, NU * i + EB * (e - 1))
                                mm(bank[3 + e % 2][:, :], sel[:, e, :], mo.wT[:, p, :], start=True, stop=True)\
                                    .then_inc(S.wb, 1)
                            after(pe, S.gelu, NU * i + bank_free(u))
                            three(bank[MM1_BANK[u]][:, :], ew1hi[:, u, :], ew1lo[:, u, :], mo.xhi[:, p, :],
                                  mo.xlo[:, p, :]).then_inc(S.mm1, 1)
                        for v in TAIL.get(u, ()) if lag else ():
                            second(i - 1, n, v)
                        if mid and u >= SKEW:
                            second(i, p, u - SKEW)
                        if lead and u == 5:
                            after(pe, S.abel, i + 1)
                            turn_chunk(Z, n, S.z, i + 2, S.tr, 6)
                        if lag and u == 8:
                            pe.wait_ge(S.gs, 4 * i)
                            if lead:
                                pe.wait_ge(S.xn, i + 2)
                            mm(bank[6][:, :], ones16[:, :], mo.gs16[:, 0, :], start=True, stop=False)
                            mm(bank[6][:, :], ones16[:, :], mo.gs16[:, 1, :], start=False, stop=True)\
                                .then_inc(S.gate, 1)
                        if lead and u == 8:
                            pe.wait_ge(S.xn, i + 2)
                            for t in range(TILES):
                                last = mm(bank[7][:, t * E:(t + 1) * E], mo.xn[:, t * P:(t + 1) * P], gate_w[:, :],
                                          start=True, stop=True)
                            last.then_inc(S.logits, 1)
                        if lag and u == 12:
                            pe.wait_ge(S.r, i)
                            for t in range(TILES):
                                tok = slice(t * P, (t + 1) * P)
                                last = tr(bank[6][:, tok], mo.r[:, tok], ident[:, :])
                            last.then_inc(S.rT, 1)
                        if lead and u == 13:
                            pe.wait_ge(S.wpair, i + 2)
                            turned = bank[7][0:2 * E, 0:CH // 2].bitcast(F16)
                            for t in range(TILES):
                                last = tr(turned[:, t * P:(t + 1) * P], mo.wp[:, t, :], ident16[:, :])
                            last.then_inc(S.wpT, 1)
                        if lead and u == NU - 1:
                            if lag:
                                pe.wait_ge(S.x, i)
                            pe.wait_ge(S.xlo, i + 2)
                            three(bank[6][:, :], abhi[:, :], ablo[:, :], mo.xhi[:, n, :], mo.xlo[:, n, :])\
                                .then_inc(S.abel_mm, 1)
                pipeline(pe, first, NCH, step)

            def flow(S, first, number):
                def step(i, p, lead, mid, lag):
                    def turned_v(*turns):
                        for o in turns if lag else ():
                            if o - 2 in SHARED:
                                pe.wait_ge(S.vs, len(SHARED) * (i - 1) + o - 2 - SHARED[0] + 1)
                            else:
                                after(pe, S.kv, OWN * (i - 1) + max(o - 1, 0) + CREDIT)
                            mm(bank[5 + o % 2][:, :], WvR[:, o, :], fl.xv[:, 1 - p, :], start=True, stop=True)\
                                .then_inc(S.v, 1)

                    def project(*turns):
                        for o in turns if lag else ():
                            pe.wait_ge(S.pd, HD * (i - 1) + o + 1)
                            if o == 0:
                                after(pe, S.x, i - 1 + CREDIT)
                            for t in range(TILES):
                                tok = slice(t * P, (t + 1) * P)
                                if o == 0:
                                    mm(bank[7][:, tok], ones[:, :], bo[:, :], start=(t == 0), stop=False,
                                       skip_group_check=True)
                                last = mm(bank[7][:, tok], fl.pd[:, o % 4, tok], WoR[:, o, :], start=False,
                                          stop=(o == HD - 1), skip_group_check=True)
                            last.then_inc(S.out, 1)

                    def sums(count):
                        for m in range(2):
                            pe.wait_ge(S.pr, count + m)
                            mm(bank[3 + m][:, :], blockones[:, :], fl.pr[:, m, :], start=True, stop=True)\
                                .then_inc(S.den, 1)

                    if lag:
                        pe.wait_ge(S.xv, i)
                    turned_v(0, 1)
                    if mid:
                        sums(4 * i + 1)
                    if lead:
                        turn_chunk(Z, 1 - p, S.z, i + 2, S.tr)
                    turned_v(2, 3)
                    project(0)
                    if lead:
                        pe.wait_ge(S.xn, i + 2)
                        for m in range(2):
                            mm(bank[1 + m][:, :], fw[:, m, :], fl.xn[:, 1 - p, :], start=True, stop=True)\
                                .then_inc(S.qk, 1)
                    turned_v(4, 5)
                    project(1, 2)
                    if mid:
                        sums(4 * i + 3)
                    turned_v(6)
                    project(3)
                    turned_v(7)
                    project(4, 5, 6, 7)
                pipeline(pe, first, NCH, step)

            setup()
            stages(pe, ffn0, mixing, experts, flow, lambda S, first, number: None)


_INS = ["L0_attn_x", "L0_attn_time_decay", "L0_attn_time_first", "L0_attn_time_mix_k", "L0_attn_time_mix_v",
        "L0_attn_time_mix_r", "L0_attn_Wk", "L0_attn_Wv", "L0_attn_Wr", "L0_attn_Wo", "L0_ffn_w_gate",
        "L0_ffn_w_up", "L0_ffn_w_down", "L1_attn_Wq", "L1_attn_bq", "L1_attn_Wk", "L1_attn_bk", "L1_attn_Wv",
        "L1_attn_bv", "L1_attn_Wo", "L1_attn_bo", "L1_ffn_ln_gamma", "L1_ffn_ln_beta", "L1_ffn_abel_w",
        "L1_ffn_abel_b", "L1_ffn_moe_gate_w", "L1_ffn_moe_gate_b", "L1_ffn_ew1", "L1_ffn_eb1", "L1_ffn_ew2",
        "L1_ffn_eb2", "L1_ffn_gens", "L1_ffn_gc_w", "L1_ffn_gc_b"]


def kernel(**inputs):
    import numpy as _np
    import concourse.bacc as _bacc
    from concourse import mybir as _mybir
    from concourse.bass_utils import run_bass_kernel_spmd as _run

    nc = _bacc.Bacc("TRN2", target_bir_lowering=False, num_devices=1)
    arrays, args = {}, {}
    for name in _INS:
        a = _np.ascontiguousarray(inputs[name])
        arrays[f"in_{name}_dram"] = a
        args[name] = nc.dram_tensor(f"in_{name}_dram", a.shape, _mybir.dt.from_np(a.dtype), kind="ExternalInput").ap()
    shape = tuple(inputs["L0_attn_x"].shape)
    out = nc.dram_tensor("out_0_dram", shape, _mybir.dt.float32, kind="ExternalOutput").ap()
    macaron_kernel(nc, args, out)
    r = _run(nc, [arrays], core_ids=[0])
    return r.results[0]["out_0_dram"]
```
